# Optimizing a Trainium2 kernel written in Bass

```python
import numpy as np
import jax
import jax.numpy as jnp

def _softmax(x, axis=-1):
    return jax.nn.softmax(x, axis=axis)

def _gelu(x):
    return jax.nn.gelu(x, approximate=True)

def _silu(x):
    return jax.nn.silu(x)

def _sigmoid(x):
    return jax.nn.sigmoid(x)

def _layernorm(x, axis=-1, eps=1e-05):
    m = jnp.mean(x, axis=axis, keepdims=True)
    v = jnp.var(x, axis=axis, keepdims=True)
    return (x - m) / jnp.sqrt(v + eps)

def _scatter_add(tgt, idx, src, axis=0):
    return tgt.at[idx].add(src)

def _segment_sum(src, seg, n):
    return jax.ops.segment_sum(src, seg, n)
kernel_name = 'mk_adj_preln_d2_adj_r2_3fe0ba'

def setup_inputs(seed: int=0):
    np.random.seed(seed)
    _w = jnp.asarray

    def _rec_inputs():
        import jax
        import jax.numpy as jnp
        _gk = jax.random.key(seed)
        x = -0.000929 + 1 * jax.random.normal(jax.random.fold_in(_gk, 1), (4096, 128), jnp.float32)
        _a = jax.random.bernoulli(jax.random.fold_in(_gk, 2), 0.000488281, (4096, 4096))
        _a = jnp.logical_or(_a, jnp.swapaxes(_a, -1, -2))
        _a = jnp.logical_or(_a, jnp.eye(4096, dtype=bool))
        adj = _a.astype(jnp.int32)
        return (x, adj)
    x, adj = _rec_inputs()

    def _L0_gnn_setup():
        import jax, jax.numpy as jnp
        import numpy as np
        NEG_INF = -1000000000.0
        key = jax.random.key(seed)
        k1, k2, k3, k4 = jax.random.split(key, 4)
        N, Fin, Fout = (4096, 128, 128)
        h = jax.random.normal(k1, (N, Fin), dtype=jnp.float32)
        adj = jax.random.randint(k2, (N, N), 0, 2, dtype=jnp.int32)
        W = jax.random.normal(k3, (Fin, Fout), dtype=jnp.float32) * (1.0 / np.sqrt(Fin))
        a = jax.random.normal(k4, (2 * Fout,), dtype=jnp.float32) * (1.0 / np.sqrt(2 * Fout))
        return {'h': h, 'adj': adj, 'W': W, 'a': a}
    _L0_gnn_all = _L0_gnn_setup()
    _L0_gnn_in = {k: v for k, v in _L0_gnn_all.items() if k in ('W', 'a')}
    del _L0_gnn_all

    def _L1_gnn_setup():
        import jax, jax.numpy as jnp
        import numpy as np
        N = 4096
        D_IN = 128
        D_HID = 128
        D_OUT = 128
        key = jax.random.key(seed)
        k_x, k_a, k0, k1, k2, k3 = jax.random.split(key, 6)
        x = jax.random.normal(k_x, (N, D_IN), dtype=jnp.float32)
        adj_matrix = jax.random.randint(k_a, (N, N), 0, 2, dtype=jnp.int32)
        s0 = 1.0 / np.sqrt(D_IN)
        s1 = 1.0 / np.sqrt(D_HID)
        w_self_0 = jax.random.uniform(k0, (D_HID, D_IN), jnp.float32, -s0, s0)
        w_neigh_0 = jax.random.uniform(k1, (D_HID, D_IN), jnp.float32, -s0, s0)
        w_self_1 = jax.random.uniform(k2, (D_OUT, D_HID), jnp.float32, -s1, s1)
        w_neigh_1 = jax.random.uniform(k3, (D_OUT, D_HID), jnp.float32, -s1, s1)
        return {'x': x, 'adj_matrix': adj_matrix, 'w_self_0': w_self_0, 'w_neigh_0': w_neigh_0, 'w_self_1': w_self_1, 'w_neigh_1': w_neigh_1}
    _L1_gnn_all = _L1_gnn_setup()
    _L1_gnn_in = {k: v for k, v in _L1_gnn_all.items() if k in ('w_self_0', 'w_neigh_0', 'w_self_1', 'w_neigh_1')}
    del _L1_gnn_all
    return {'x': x, 'adj': adj, 'L0_gnn_W': _L0_gnn_in['W'], 'L0_gnn_a': _L0_gnn_in['a'], 'L1_gnn_w_self_0': _L1_gnn_in['w_self_0'], 'L1_gnn_w_neigh_0': _L1_gnn_in['w_neigh_0'], 'L1_gnn_w_self_1': _L1_gnn_in['w_self_1'], 'L1_gnn_w_neigh_1': _L1_gnn_in['w_neigh_1']}

def reference(x, adj, L0_gnn_W, L0_gnn_a, L1_gnn_w_self_0, L1_gnn_w_neigh_0, L1_gnn_w_self_1, L1_gnn_w_neigh_1):
    import jax
    import jax.numpy as jnp

    def _L0_gnn_ref(h, adj, W, a):
        import jax, jax.numpy as jnp
        import numpy as np
        NEG_INF = -1000000000.0
        Fout = W.shape[1]
        Wh = h @ W
        a1, a2 = (a[:Fout], a[Fout:])
        s_key = Wh @ a1
        s_qry = Wh @ a2
        e = jax.nn.leaky_relu(s_qry[:, None] + s_key[None, :], negative_slope=0.2)
        scores = jnp.where(adj > 0, e, jnp.float32(NEG_INF))
        attention = jax.nn.softmax(scores, axis=1)
        h_prime = attention @ Wh
        return jax.nn.elu(h_prime)

    def _L1_gnn_ref(x, adj_matrix, w_self_0, w_neigh_0, w_self_1, w_neigh_1):
        import jax, jax.numpy as jnp
        import numpy as np
        N = 4096
        D_IN = 128
        D_HID = 128
        D_OUT = 128
        A = adj_matrix.astype(x.dtype)

        def layer(h, w_self, w_neigh):
            neigh = A @ h
            return jax.nn.relu(h @ w_self.T + neigh @ w_neigh.T)
        h = layer(x, w_self_0, w_neigh_0)
        return layer(h, w_self_1, w_neigh_1)
    h = jnp.maximum(_layernorm(x, axis=-1), 0.0)
    x = x + _L0_gnn_ref(h, adj, L0_gnn_W, L0_gnn_a)
    h = jnp.maximum(_layernorm(x, axis=-1), 0.0)
    x = x + _L1_gnn_ref(h, adj, L1_gnn_w_self_0, L1_gnn_w_neigh_0, L1_gnn_w_self_1, L1_gnn_w_neigh_1)
    return x

_drawn_inputs = setup_inputs


def setup_inputs(seed=0):
    import zlib

    import numpy as np

    out = dict(_drawn_inputs(seed))
    spreads = {}
    factors = {}
    for name, (base, spread) in spreads.items():
        noise = np.random.default_rng([zlib.crc32(name.encode()), seed]).standard_normal(out[name].shape)
        drawn = base * np.exp(spread * noise) if base else spread * noise
        out[name] = jnp.asarray(drawn.astype(out[name].dtype))
    for name, factor in factors.items():
        out[name] = (out[name] * factor).astype(out[name].dtype)
    return out
```

```python
import concourse.bass as bass
from concourse import mybir
from contextlib import ExitStack


def gat_sage_kernel(nc, x, adj, W, a, ws0, wn0, ws1, wn1, out):
    f32 = mybir.dt.float32
    f16 = mybir.dt.float16
    f8 = mybir.dt.float8e4
    u8 = mybir.dt.uint8
    i8 = mybir.dt.int8
    u32 = mybir.dt.uint32
    i32 = mybir.dt.int32
    ALU = mybir.AluOpType
    ACT = mybir.ActivationFunctionType
    AX = mybir.AxisListType
    ds = bass.ds

    N, F = x.shape
    P = 128
    NT = N // P
    IB = 2 * P
    NB = N // IB
    QJ = 4
    NQ = NT // QJ
    FILLS = NT // 2
    DJ = 2
    CH = 4
    CW = N // CH
    V = F + 1
    LN_EPS = 1e-5
    SLOPE = 0.2
    HNORM = 11.4
    TINY = 1e-30
    SPREAD = 10.0
    BIG = 1e30
    TOP = 2.0 ** 14
    LOW = 2.0 ** 11
    ONE8 = 56.0
    EPI = 17

    ctx = ExitStack()
    with ctx:
        def sb(name, shape, dt):
            return ctx.enter_context(nc.sbuf_tensor(name, shape, dt))

        def pb(name, shape, dt):
            return ctx.enter_context(nc.psum_tensor(name, shape, dt))

        def sem(name):
            return ctx.enter_context(nc.semaphore(name))

        x1_dram = nc.dram_tensor("x1_scratch", (N, F), f32).ap()
        self0_dram = nc.dram_tensor("self0_scratch", (N, F), f32).ap()
        sq_dram = nc.dram_tensor("sq_scratch", (N,), f32).ap()
        wh_dram = nc.dram_tensor("wh_scratch", (P, NT * (F + 3)), f32).ap()
        skpos_dram = nc.dram_tensor("skpos_scratch", (N,), f32).ap()
        x_t = x.rearrange("(t p) f -> p t f", p=P)
        x1_t = x1_dram.rearrange("(t p) f -> p t f", p=P)
        self0_t = self0_dram.rearrange("(t p) f -> p t f", p=P)
        out_t = out.rearrange("(t p) f -> p t f", p=P)
        adj_c = adj.rearrange("(b s p) (c j) -> b c p s j", s=2, p=P, c=CH)
        skpos_c = skpos_dram.rearrange("(c j) -> c j", c=CH)
        sq_b = sq_dram.rearrange("(b i) -> b i", b=NB)

        adjT = sb("adjT", [P, NB, NT, IB], f8)
        late = adjT[:, NB // 2:, :, :].rearrange("p b t i -> p (b t i)").bitcast(f32)
        xin = late[:, 0:NT * F].rearrange("p (t f) -> p t f", f=F)
        WHC = F + 3
        o = NT * F
        wh = late[:, o:o + NT * WHC].rearrange("p (t f) -> p t f", f=WHC)
        o += NT * WHC
        wX = late[:, o:o + 2 * QJ * V].rearrange("p (k t f) -> p k t f", k=2, f=V)
        o += 2 * QJ * V
        wY = late[:, o:o + 2 * QJ * V].rearrange("p (k t f) -> p k t f", k=2, f=V)

        late_wh = late[:, NT * F:NT * F + NT * WHC]
        setup_end = [o + 2 * QJ * V]

        def setup_only(width):
            setup_end[0] += width
            return late[:, setup_end[0] - width:setup_end[0]]

        operands = sb("operands", [P, NT, 4 * V], f16)
        ops_flat = operands[:].rearrange("p t f -> p (t f)")
        G1 = ops_flat[:, 0:NT * 2 * F].rearrange("p (t f) -> p t f", f=2 * F)
        self1 = ops_flat[:, NT * 2 * F:2 * NT * 2 * F].bitcast(f32).rearrange("p (t f) -> p t f", f=F)
        G0 = sb("G0", [P, NT, 2 * F], f16)
        stage = sb("stage", [P, CH, 2, CW], f8)
        keep = sb("keep", [P, 2, QJ, IB], i8)
        maskB = sb("maskB", [P, 2, QJ, IB], f8)
        maskC = sb("maskC", [P, 2, QJ, IB], f8)
        SQ = sb("SQ", [P, 2, IB], f32)
        ident = sb("ident", [P, P], f32)
        ident8 = sb("ident8", [P, P], f8)
        ones = setup_only(P)
        wnat = setup_only(5 * F).rearrange("p (k f) -> p k f", k=5)
        WT = setup_only(F)
        acols = setup_only(2)
        rhs0 = setup_only(WHC)
        wsn0 = sb("wsn0", [P, 2 * F], f32)
        wsn1 = sb("wsn1", [P, 2 * F], f32)
        junk = sb("junk", [P, F], f32)
        stats = sb("stats", [P, 4], f32)
        norms = sb("norms", [P, 4], f32)
        scales = sb("scales", [P, 16], f32)
        BND, INVB, S, B0, S0, I0, K0, H, B1, S1, I1, K1, spread = (scales[:, i:i + 1] for i in range(13))
        bn6 = sb("bn6", [P, 8, 6], f32)
        mv = sb("mv", [P, 8, 2], f32)
        veps = sb("veps", [P, 8], f32)
        rstdx = sb("rstdx", [P, NT], f32)
        rstd = sb("rstd", [P, 2], f32)
        minus_half = sb("minus_half", [P, 8], f32)
        half = sb("half", [P, 4], f32)
        wait_slot = sb("wait_slot", [P, 1], f32)
        wide = sb("wide", [P, 1], i32)
        hT = sb("hT", [P, 4 * P], f32)
        ext = sb("ext", [P, 2], f32)
        red = sb("red", [P, 2], f32)
        negc = sb("negc", [P, 2], f32)
        z = setup_only(NT)
        zu = setup_only(NT)
        zv = setup_only(NT)
        U = sb("U", [P, NT], f32)
        Vv = sb("Vv", [P, NT], f32)
        Xs = sb("Xs", [P, NT], f32)
        Ys = sb("Ys", [P, NT], f32)
        nsk = sb("nsk", [P, NT], f32)
        sqrow = setup_only(P)[0:NT, :]
        sumWh = sb("sumWh", [P, V], f32)
        RB = sb("RB", [P, 2, 2 * V], f32)
        RC = sb("RC", [P, 2, 2 * V], f32)
        eM, eC, ey = RB[:, :, 0:V], RC[:, :, 0:V], RB[:, :, V:V + F]
        eflag = sb("eflag", [P, 2], f32)
        erec = sb("erec", [P, 2], f32)
        escale = sb("escale", [P, 2], f32)
        emin = sb("emin", [P, 2, F], f32)
        xt = sb("xt", [P, 2, F], f32)
        x1 = sb("x1", [P, 2, F], f32)
        selfst = sb("selfst", [P, 2, F], f32)
        RT = 4
        halves = stage[:].rearrange("p c s j -> p (c s j)").bitcast(f32)
        wadj, wsk = halves[:, 0:CW].bitcast(i32), halves[:, CW:2 * CW]
        o = NT * WHC
        opf = ops_flat.bitcast(f32)
        wwh_flat = opf[:, 0:o]
        wwh = wwh_flat.rearrange("p (t f) -> p t f", f=WHC)
        exps = opf[:, o:o + 4 * P].rearrange("p (k h i) -> p k h i", k=2, h=2)
        o += 4 * P
        probs = opf[:, o:o + 2 * P].rearrange("p (k i) -> p k i", k=2)
        o += 2 * P
        abT = opf[:, o:o + 2 * P].rearrange("p (k i) -> p k i", k=2)
        o += 2 * P
        wrow = opf[0:NT, o:o + P]
        o += P
        wcols = opf[:, o:o + 2 * NT].rearrange("p (k t) -> p k t", k=2)
        o += 2 * NT
        wmax, wm, wab = opf[:, o:o + CH], opf[:, o + CH:o + CH + 4], opf[:, o + CH + 4:o + CH + 6]
        rings = stage[:].rearrange("p c s j -> p (c s j)").bitcast(f32).rearrange("p (k f) -> p k f", f=F)
        lring, oring, hpre = rings[:, 0:RT, :], rings[:, RT:2 * RT, :], rings[:, 2 * RT:2 * RT + 2, :]

        acc = pb("acc", [P, 4, 512], f32)
        tp = pb("tp", [P, 2, 512], f32)
        misc2 = pb("misc2", [P, 512], f32)
        misc = pb("misc", [P, 512], f32)

        weights_landed = sem("weights_landed")
        x_landed = [sem(f"x_landed{c}") for c in range(4)]
        adj_landed = [sem(f"adj_landed{c}") for c in range(CH)]
        sq_landed = [sem(f"sq_landed{k}") for k in range(2)]
        xt_landed = sem("xt_landed")
        x1_stored = sem("x1_stored")
        self_stored = sem("self_stored")
        sq_stored = sem("sq_stored")
        ring_landed = [sem(f"ring_landed{k}") for k in range(RT)]
        out_stored = [sem(f"out_stored{k}") for k in range(RT)]
        pool_const = sem("pool_const")
        const_ready = sem("const_ready")
        weightsT = sem("weightsT")
        wt_copied = sem("wt_copied")
        wa_done = sem("wa_done")
        rhs0_ready = sem("rhs0_ready")
        stats_ready = sem("stats_ready")
        norms_ready = sem("norms_ready")
        scales_ready = sem("scales_ready")
        dstep = sem("dstep")
        wsn_ready = sem("wsn_ready")
        veps_ready = sem("veps_ready")
        rstd_ready = sem("rstd_ready")
        ln_done = sem("ln_done")
        xT_done = sem("xT_done")
        hT_ready = sem("hT_ready")
        wh_done = sem("wh_done")
        wh_copied = sem("wh_copied")
        bound_col = sem("bound_col")
        ext_ready = sem("ext_ready")
        red_ready = sem("red_ready")
        negc_ready = sem("negc_ready")
        exps_ready = sem("exps_ready")
        xs_ready = sem("xs_ready")
        sqT_done = sem("sqT_done")
        sqrow_ready = sem("sqrow_ready")
        sumwh_done = sem("sumwh_done")
        sumwh_ready = sem("sumwh_ready")
        wX0_ready = sem("wX0_ready")
        wX_ready = sem("wX_ready")
        wY_ready = sem("wY_ready")
        hiX_ready = sem("hiX_ready")
        hiY_ready = sem("hiY_ready")
        loX_ready = sem("loX_ready")
        loY_ready = sem("loY_ready")
        wh_stored = sem("wh_stored")
        tp_filled = sem("tp_filled")
        wide_ready = sem("wide_ready")
        wh_reloaded = sem("wh_reloaded")
        wcols_ready = sem("wcols_ready")
        wrow_done = sem("wrow_done")
        wrow_ready = sem("wrow_ready")
        wrow_stored = sem("wrow_stored")
        wadj_landed = sem("wadj_landed")
        wcand_ready = sem("wcand_ready")
        wmax_ready = sem("wmax_ready")
        wstep = sem("wstep")
        ab_done = sem("ab_done")
        abT_ready = sem("abT_ready")
        wexps_ready = sem("wexps_ready")
        wlarger = sem("wlarger")
        probs_ready = sem("probs_ready")
        probs_used = sem("probs_used")
        wrows_ready = sem("wrows_ready")
        adjT_ready = sem("adjT_ready")
        signs_ready = sem("signs_ready")
        compared = sem("compared")
        maskB_ready = sem("maskB_ready")
        maskC_ready = sem("maskC_ready")
        masks_used = sem("masks_used")
        accB_copied = sem("accB_copied")
        accC_copied = sem("accC_copied")
        epi = sem("epi")
        combined = sem("combined")
        emin_ready = sem("emin_ready")
        eexp_ready = sem("eexp_ready")
        x1_ready = sem("x1_ready")
        xn_ready = sem("xn_ready")
        eT_done = sem("eT_done")
        ehT_ready = sem("ehT_ready")
        sg_done = sem("sg_done")
        ghi_ready = sem("ghi_ready")
        self_ready = sem("self_ready")
        g_ready = sem("g_ready")
        l1_done = sem("l1_done")
        l1_read = sem("l1_read")
        l1_half = sem("l1_half")
        l1_sum = sem("l1_sum")
        hpre_ready = sem("hpre_ready")
        hpT_done = sem("hpT_done")
        h1T_ready = sem("h1T_ready")
        sg1_done = sem("sg1_done")
        g1hi_ready = sem("g1hi_ready")
        self1_ready = sem("self1_ready")
        g1_ready = sem("g1_ready")
        l2_done = sem("l2_done")
        l2_read = sem("l2_read")
        l2_half = sem("l2_half")
        l2_sum = sem("l2_sum")
        out_ready = sem("out_ready")

        block = ctx.enter_context(nc.Block())

        @block.sync
        def _(sp):
            for c in range(4):
                sp.dma_start(xin[:, 8 * c:8 * c + 8, :], x_t[:, 8 * c:8 * c + 8, :]).then_inc(x_landed[c], 16)
            sp.wait_ge(sqrow_ready, 1)
            sp.dma_start(sq_dram.rearrange("(t p) -> t p", p=P), sqrow[:]).then_inc(sq_stored, 16)
            sp.wait_ge(sq_stored, 16)
            sp.dma_start(SQ[:, 0, :], sq_b[0:1, :].broadcast_to([P, IB])).then_inc(sq_landed[0], 16)
            sp.dma_start(SQ[:, 1, :], sq_b[1:2, :].broadcast_to([P, IB])).then_inc(sq_landed[1], 16)
            sp.dma_start(xt[:], x_t[:, 0:2, :]).then_inc(xt_landed, 16)
            sp.wait_ge(bound_col, 1)
            sp.dma_start(wh_dram, late_wh).then_inc(wh_stored, 16)

            def store_block(e, n):
                sp.wait_ge(x1_ready, n + 1)
                sp.dma_start(x1_t[:, ds(2 * e, 2), :], x1[:]).then_inc(x1_stored, 16)
                sp.wait_ge(self_ready, n + 1)
                sp.dma_start(self0_t[:, ds(2 * e, 2), :], selfst[:]).then_inc(self_stored, 16)

            def serve_block(b, par, last=False):
                sp.wait_ge(maskB_ready, NQ * b)
                if not last:
                    sp.dma_start(SQ[:, 1 - par, :], sq_b[ds(b + 1, 1), :].broadcast_to([P, IB])).then_inc(
                        sq_landed[1 - par], 16)
                sp.wait_ge(x1_ready, b)
                sp.dma_start(xt[:], x_t[:, ds(2 * b, 2), :]).then_inc(xt_landed, 16)
                store_block(b - 1, b - 1)

            serve_block(1, 1)
            with sp.Fori(0, (NB - 4) // 2, 1) as it:
                serve_block(2 * it + 2, 0)
                serve_block(2 * it + 3, 1)
            serve_block(NB - 2, 0)
            serve_block(NB - 1, 1, last=True)
            store_block(NB - 1, NB - 1)
            sp.wait_ge(x1_stored, 16 * NB)
            sp.wait_ge(self_stored, 16 * NB)
            sp.wait_ge(wide_ready, 1)
            with sp.If(nc.sync.value_load(wide[0:1, 0:1], min_val=0, max_val=1)):
                sp.wait_ge(masks_used, NQ * NB)
                sp.wait_ge(wh_stored, 16)
                sp.dma_start(wwh_flat, wh_dram).then_inc(wh_reloaded, 16)
                sp.wait_ge(wrow_ready, 1)
                sp.dma_start(skpos_dram.rearrange("(t p) -> t p", p=P), wrow).then_inc(wrow_stored, 16)
                sp.wait_ge(wrow_stored, 16)
                with sp.Fori(0, NB, 1) as e:
                    for s in range(2):
                        for c in range(CH):
                            if c >= 1:
                                sp.wait_ge(wmax_ready, CH * (2 * e + s) + c)
                            elif s >= 1:
                                sp.wait_ge(wmax_ready, CH * (2 * e + s))
                            else:
                                sp.wait_ge(x1_ready, NB + e)
                            sp.dma_start(wadj, adj_c[ds(e, 1), c, :, s, :].squeeze(0)).then_inc(wadj_landed, 16)
                            sp.dma_start(wsk, skpos_c[c:c + 1, :].broadcast_to([P, CW])).then_inc(wadj_landed, 16)
                    sp.dma_start(xt[:], x_t[:, ds(2 * e, 2), :]).then_inc(xt_landed, 16)
                    store_block(e, NB + e)
                sp.wait_ge(x1_stored, 32 * NB)
                sp.wait_ge(self_stored, 32 * NB)
            for k in range(RT):
                sp.dma_start(lring[:, k, :], self0_t[:, k, :]).then_inc(ring_landed[k], 16)
            with sp.Fori(1, NT // RT, 1) as r:
                for k in range(RT):
                    sp.wait_ge(l1_half, RT * r - RT + k + 1)
                    sp.dma_start(lring[:, k, :], self0_t[:, ds(RT * r + k, 1), :]).then_inc(ring_landed[k], 16)
            for k in range(RT):
                sp.wait_ge(l1_half, NT - RT + k + 1)
                sp.dma_start(lring[:, k, :], x1_t[:, k, :]).then_inc(ring_landed[k], 16)
            with sp.Fori(1, NT // RT, 1) as r:
                for k in range(RT):
                    sp.wait_ge(out_ready, RT * r - RT + k + 1)
                    sp.dma_start(lring[:, k, :], x1_t[:, ds(RT * r + k, 1), :]).then_inc(ring_landed[k], 16)
                    sp.dma_start(out_t[:, ds(RT * r - RT + k, 1), :], oring[:, k, :]).then_inc(out_stored[k], 16)
            for k in range(RT):
                sp.wait_ge(out_ready, NT - RT + k + 1)
                sp.dma_start(out_t[:, NT - RT + k, :], oring[:, k, :]).then_inc(out_stored[k], 16)
            for k in range(RT):
                sp.wait_ge(out_stored[k], 16 * NT // RT)

        @block.gpsimd
        def _(pool):
            nc.gpsimd.memset(ident[:], 0.0).then_inc(pool_const, 1)
            nc.gpsimd.memset(ones, 1.0).then_inc(pool_const, 1)
            nc.gpsimd.memset(minus_half[:], -0.5).then_inc(pool_const, 1)
            nc.gpsimd.memset(half[:], 0.5).then_inc(pool_const, 1)
            pool.wait_ge(pool_const, 4)
            nc.gpsimd.affine_select(out=ident[:], in_=ident[:], compare_op=ALU.not_equal, fill=1.0, base=0,
                                    pattern=[[-1, P]], channel_multiplier=1).then_inc(pool_const, 1)

            def load_adj(b, c):
                pool.dma_start(stage[:, c, :, :], adj_c[b, c, :, :, :]).then_inc(adj_landed[c], 16)

            pool.wait_ge(x_landed[1], 16)
            for c in range(CH):
                load_adj(0, c)
            RMAX = bass.bass_isa.ReduceOp.max

            def x_row_scales(c):
                pool.wait_ge(veps_ready, c + 1)
                nc.gpsimd.tensor_tensor(rstdx[:, 8 * c:8 * c + 8], rstdx[:, 8 * c:8 * c + 8], minus_half[:],
                                        ALU.pow).then_inc(rstd_ready, 1)

            def row_scales(n):
                pool.wait_ge(veps_ready, n + 5)
                nc.gpsimd.tensor_tensor(rstd[:], veps[:, 0:2], minus_half[:, 0:2], ALU.pow).then_inc(rstd_ready, 1)

            x_row_scales(0)
            pool.wait_ge(stats_ready, 4)
            nc.gpsimd.partition_all_reduce(norms[:], stats[:], P, RMAX).then_inc(norms_ready, 1)
            pool.wait_ge(norms_ready, 1)
            nc.gpsimd.tensor_tensor(norms[:], norms[:], half[:], ALU.pow).then_inc(norms_ready, 1)
            for c in range(1, 4):
                x_row_scales(c)
            for c in range(2):
                pool.wait_ge(tp_filled, 4 * (c + 1))
                load_adj(1, c)
            pool.wait_ge(ext_ready, 2)
            nc.gpsimd.partition_all_reduce(red[:], ext[:], P, RMAX).then_inc(red_ready, 1)
            for c in range(2, CH):
                pool.wait_ge(tp_filled, 4 * (c + 1))
                load_adj(1, c)
            pool.wait_ge(xs_ready, 2)
            pool.wait_ge(bound_col, 1)
            for c in range(NQ):
                t0 = QJ * c
                if c >= 1:
                    if c >= 2:
                        pool.wait_ge(loX_ready, c - 1)
                    nc.gpsimd.tensor_tensor(wX[:, c % 2, :, :], wh[:, t0:t0 + QJ, 0:V],
                                            Xs[:, t0:t0 + QJ].unsqueeze(2).broadcast_to([P, QJ, V]),
                                            ALU.mult).then_inc(wX_ready, 1)
                if c >= 2:
                    pool.wait_ge(loY_ready, c - 1)
                nc.gpsimd.tensor_tensor(wY[:, c % 2, :, :], wh[:, t0:t0 + QJ, 0:V],
                                        Ys[:, t0:t0 + QJ].unsqueeze(2).broadcast_to([P, QJ, V]),
                                        ALU.mult).then_inc(wY_ready, 1)

            def refill(b, c):
                pool.wait_ge(tp_filled, FILLS * (b - 1) + 4 * (c + 1))
                load_adj(b, c)

            for c in range(CH):
                refill(2, c)
            for b in range(3, NB):
                refill(b, 0)
                refill(b, 1)
                row_scales(b - 3)
                refill(b, 2)
                refill(b, 3)
            for n in range(NB - 3, NB):
                row_scales(n)

            pool.wait_ge(wide_ready, 1)
            with pool.If(nc.gpsimd.value_load(wide[0:1, 0:1], min_val=0, max_val=1)):
                with pool.Fori(0, NB, 1) as e:
                    row_scales(NB + e)

        @block.scalar
        def _(act):
            for k, w in enumerate((W, ws0, wn0, ws1, wn1)):
                act.dma_start(wnat[:, k, :], w).then_inc(weights_landed, 16)
            with nc.allow_non_contiguous_dma(reason="256 numbers"):
                act.dma_start(acols, a.rearrange("(k f) -> f k", k=2)).then_inc(weights_landed, 16)
            act.wait_ge(weightsT, 1)
            nc.scalar.activation(WT[:], tp[:, 0, 0:F], ACT.Copy).then_inc(wt_copied, 1)
            act.wait_ge(weights_landed, 96)
            nc.scalar.activation(rhs0[:, 0:F], wnat[:, 0, :], ACT.Copy).then_inc(rhs0_ready, 1)
            act.wait_ge(wa_done, 1)
            act.wait_ge(rhs0_ready, 2)
            nc.scalar.activation(rhs0[:, F + 1:F + 3], misc[:, 0:2], ACT.Copy).then_inc(rhs0_ready, 1)
            nc.scalar.activation(wsn0[:, 0:F], tp[:, 0, F:2 * F], ACT.Copy).then_inc(wsn_ready, 1)
            nc.scalar.activation(wsn1[:, 0:F], tp[:, 0, 3 * F:4 * F], ACT.Copy).then_inc(wsn_ready, 1)
            act.wait_ge(scales_ready, 1)
            nc.scalar.activation(wsn0[:, F:2 * F], tp[:, 0, 2 * F:3 * F], ACT.Copy, scale=S0).then_inc(wsn_ready, 1)
            nc.scalar.activation(wsn1[:, F:2 * F], acc[:, 3, 0:F], ACT.Copy, scale=S1).then_inc(wsn_ready, 1)

            def keep_adjT(b, m):
                act.wait_ge(tp_filled, FILLS * b + m + 1)
                if isinstance(b, int):
                    to = adjT[:, b, 2 * m:2 * m + 2, :]
                else:
                    to = adjT[:, ds(b, 1), 2 * m:2 * m + 2, :].squeeze(1)
                nc.scalar.activation(to.bitcast(u8), tp[:, m % 2, :].rearrange("p (t i) -> p t i", t=2),
                                     ACT.Copy, scale=ONE8).then_inc(adjT_ready, 1)

            for g in range(NT // 4):
                act.wait_ge(xT_done, g + 1)
                if g >= 1:
                    act.wait_ge(wh_done, g)
                nc.scalar.activation(hT[:], misc[:], ACT.Relu).then_inc(hT_ready, 1)
                keep_adjT(0, 2 * g)
                keep_adjT(0, 2 * g + 1)
                act.wait_ge(wh_done, g + 1)
                act.wait_ge(rstd_ready, g // 2 + 1)
                for k in range(4):
                    t = 4 * g + k
                    nc.scalar.activation(wh[:, t, :], acc[:, 2 * (g % 2) + k // 2, (k % 2) * 256:(k % 2) * 256 + WHC],
                                         ACT.Copy, scale=rstdx[:, t:t + 1]).then_inc(wh_copied, 1)
            act.wait_ge(sqT_done, 1)
            nc.scalar.activation(sqrow[:], misc[0:NT, 0:P], ACT.Copy).then_inc(sqrow_ready, 1)
            act.wait_ge(negc_ready, 2)
            act.wait_ge(wh_copied, NT)
            nc.scalar.activation(Xs[:], wh[:, :, F + 1], ACT.Exp, bias=negc[:, 0:1]).then_inc(exps_ready, 1)
            nc.scalar.activation(Ys[:], wh[:, :, F + 1], ACT.Exp, bias=negc[:, 1:2], scale=SLOPE).then_inc(
                exps_ready, 1)
            act.wait_ge(negc_ready, 4)
            nc.scalar.activation(U[:], zu[:], ACT.Exp).then_inc(exps_ready, 1)
            nc.scalar.activation(Vv[:], zv[:], ACT.Exp).then_inc(exps_ready, 1)
            def signs(b, par, half, q):
                count = NQ * b + q
                if q == 0:
                    act.wait_ge(sq_landed[par], 16 * half + 16)
                if not isinstance(count, int) or count >= 2:
                    act.wait_ge(maskB_ready, count - 1)
                for u in range(DJ, QJ):
                    i = nc.scalar.activation(keep[:, q % 2, u, :], SQ[:, par, :], ACT.Sign, scale=-1.0,
                                             bias=nsk[:, QJ * q + u:QJ * q + u + 1])
                i.then_inc(signs_ready, 1)

            for q in range(NQ):
                t0 = QJ * q
                signs(0, 0, 0, q)
                if q == 0:
                    act.wait_ge(wX0_ready, 1)
                else:
                    act.wait_ge(wX_ready, q)
                nc.scalar.activation(operands[:, t0:t0 + QJ, 0:V], wX[:, q % 2, :, :], ACT.Copy,
                                     scale=1.0 / LOW).then_inc(hiX_ready, 1)
                act.wait_ge(wY_ready, q + 1)
                nc.scalar.activation(operands[:, t0:t0 + QJ, 2 * V:3 * V], wY[:, q % 2, :, :], ACT.Copy,
                                     scale=1.0 / LOW).then_inc(hiY_ready, 1)
                keep_adjT(1, 2 * q)
                keep_adjT(1, 2 * q + 1)
            act.wait_ge(sumwh_done, 1)
            nc.scalar.activation(sumWh[:], misc[:, P:P + V], ACT.Copy).then_inc(sumwh_ready, 1)

            def copy_accC(e):
                act.wait_ge(masks_used, NQ * (e + 1))
                if not isinstance(e, int) or e > 0:
                    act.wait_ge(x1_ready, e)
                nc.scalar.activation(RC[:], acc[:, 2:4, 0:2 * V], ACT.Copy).then_inc(accC_copied, 1)

            def elu_exp(n):
                act.wait_ge(emin_ready, 2 * n + 2)
                nc.scalar.activation(emin[:], emin[:], ACT.Exp).then_inc(eexp_ready, 1)

            def relu_T(n):
                act.wait_ge(eT_done, n + 1)
                nc.scalar.activation(hT[:, 0:IB], misc[:, 0:IB], ACT.Relu).then_inc(ehT_ready, 1)

            def split_G0(e, n):
                act.wait_ge(sg_done, n + 1)
                sg = misc[:].rearrange("p (s k f) -> p s k f", s=2, k=2)
                nc.scalar.activation(G0[:, ds(2 * e, 2), 0:F], sg[:, :, 1, :], ACT.Copy,
                                     scale=1.0 / LOW).then_inc(ghi_ready, 1)
                if not isinstance(n, int) or n > 0:
                    act.wait_ge(self_stored, 16 * n)
                nc.scalar.activation(selfst[:], sg[:, :, 0, :], ACT.Copy).then_inc(self_ready, 1)

            def act_block(b, par, half, next_block=True):
                e = b - 1
                signs(b, par, half, 0)
                copy_accC(e)
                for q in range(NQ):
                    if q >= 1:
                        signs(b, par, half, q)
                    if next_block:
                        keep_adjT(b + 1, 2 * q)
                        keep_adjT(b + 1, 2 * q + 1)
                    if q == 2:
                        elu_exp(e)
                    if q == 5:
                        relu_T(e)
                    if q == 6:
                        split_G0(e, e)

            act.wait_ge(wh_stored, 16)
            act_block(1, 1, 0)
            act_block(2, 0, 1)
            with act.Fori(1, (NB - 2) // 2, 1) as it:
                act_block(2 * it + 1, 1, it)
                act_block(2 * it + 2, 0, it + 1)
            act_block(NB - 1, 1, NB // 2 - 1, next_block=False)
            e = NB - 1
            copy_accC(e)
            elu_exp(e)
            relu_T(e)
            split_G0(e, e)

            act.wait_ge(wide_ready, 1)
            with act.If(nc.scalar.value_load(wide[0:1, 0:1], min_val=0, max_val=1)):
                with act.Fori(0, NB, 1) as e:
                    for s in range(2):
                        k = 2 * e + s
                        act.wait_ge(ab_done, k + 1)
                        nc.scalar.activation(abT, misc[:, 0:2 * P].rearrange("p (k i) -> p k i", k=2),
                                             ACT.Copy).then_inc(abT_ready, 1)
                        act.wait_ge(abT_ready, k + 1)
                        for jt in range(NT):
                            m = NT * k + jt
                            act.wait_ge(wcols_ready, 2)
                            if jt >= 2:
                                act.wait_ge(probs_ready, m - 1)
                            for h in range(2):
                                nc.scalar.activation(exps[:, jt % 2, h, :], abT[:, h, :], ACT.Exp,
                                                     bias=wcols[:, h, jt:jt + 1]).then_inc(wexps_ready, 1)
                    elu_exp(NB + e)
                    relu_T(NB + e)
                    split_G0(e, NB + e)

            def layer1_tile(t, k):
                act.wait_ge(hpT_done, t + 1)
                nc.scalar.activation(hT[:, P * (k % 2):P * (k % 2) + P], misc[:, 0:P], ACT.Relu).then_inc(h1T_ready, 1)
                act.wait_ge(sg1_done, t + 1)
                nc.scalar.activation(G1[:, ds(t, 1), 0:F].squeeze(1), tp[:, 0, F:2 * F], ACT.Copy,
                                     scale=1.0 / LOW).then_inc(g1hi_ready, 1)
                nc.scalar.activation(self1[:, ds(t, 1), :].squeeze(1), tp[:, 0, 0:F], ACT.Copy).then_inc(
                    self1_ready, 1)

            with act.Fori(0, NT // RT, 1) as r:
                for k in range(RT):
                    layer1_tile(RT * r + k, k)

        @block.vector
        def _(dve):
            V_ = nc.vector
            n = [0]

            def step(ins):
                ins.then_inc(dstep, 1)
                n[0] += 1
                return n[0]

            dve.wait_ge(pool_const, 5)
            nc.vector.tensor_copy(ident8[:], ident[:], saturate=False).then_inc(const_ready, 1)
            nc.vector.memset(rhs0[:, F:F + 1], 0.0).then_inc(rhs0_ready, 1)
            def center(c):
                dve.wait_ge(x_landed[c], 16)
                for t in range(8):
                    last = step(nc.vector.bn_stats(bn6[:, t, :], xin[:, 8 * c + t, :]))
                dve.wait_ge(dstep, last)
                for t in range(8):
                    last = step(nc.vector.bn_aggr(mv[:, t, :], bn6[:, t, :]))
                dve.wait_ge(dstep, last)
                nc.vector.tensor_scalar(rstdx[:, 8 * c:8 * c + 8], mv[:, :, 1], LN_EPS, None,
                                        ALU.add).then_inc(veps_ready, 1)
                for h in range(2):
                    t = 8 * c + 4 * h
                    nc.vector.tensor_tensor(xin[:, t:t + 4, :], xin[:, t:t + 4, :],
                                            mv[:, 4 * h:4 * h + 4, 0:1].broadcast_to([P, 4, F]),
                                            ALU.subtract).then_inc(ln_done, 1)
                dve.wait_ge(ln_done, 2 * c + 2)

            center(0)
            dve.wait_ge(weights_landed, 96)
            for c, k in ((1, 1), (2, 2), (3, 4)):
                nc.vector.tensor_tensor_reduce(out=junk[:], in0=wnat[:, k, :], in1=wnat[:, k, :], scale=1.0,
                                               scalar=TINY, op0=ALU.mult, op1=ALU.add,
                                               accum_out=stats[:, c:c + 1]).then_inc(stats_ready, 1)
                dve.wait_ge(stats_ready, c)
            dve.wait_ge(wt_copied, 1)
            nc.vector.tensor_tensor_reduce(out=junk[:], in0=WT[:], in1=WT[:], scale=1.0, scalar=TINY, op0=ALU.mult,
                                           op1=ALU.add, accum_out=stats[:, 0:1]).then_inc(stats_ready, 1)

            center(1)
            dve.wait_ge(norms_ready, 2)
            nW, nS0, nN0, nN1 = (norms[:, k:k + 1] for k in range(4))
            step(V_.tensor_scalar(BND, nW, HNORM, None, ALU.mult))
            step(V_.tensor_scalar(B0, nN0, HNORM, None, ALU.mult))
            step(V_.scalar_tensor_tensor(out=H, in0=nN0, scalar=float(N), in1=nS0, op0=ALU.mult, op1=ALU.add))
            dve.wait_ge(dstep, n[0])
            dve.wait_ge(dstep, step(V_.tensor_scalar(B1, H, nN1, HNORM * HNORM, ALU.mult, ALU.mult)))
            step(V_.reciprocal(INVB, BND))
            step(V_.reciprocal(S0, B0))
            step(V_.reciprocal(S1, B1))
            step(V_.tensor_scalar(I0, B0, 1.0 / TOP, None, ALU.mult))
            step(V_.tensor_scalar(I1, B1, 1.0 / TOP, None, ALU.mult))
            step(V_.tensor_scalar(K0, B0, 1.0 / TOP / LOW, None, ALU.mult))
            step(V_.tensor_scalar(K1, B1, 1.0 / TOP / LOW, None, ALU.mult))
            dve.wait_ge(dstep, n[0])
            step(V_.tensor_scalar(S, INVB, TOP * LOW, None, ALU.mult))
            step(V_.tensor_scalar(S0, S0, TOP * LOW, None, ALU.mult))
            V_.tensor_scalar(S1, S1, TOP * LOW, None, ALU.mult).then_inc(scales_ready, 1)
            center(2)
            center(3)

            dve.wait_ge(wh_copied, NT)
            sk = wh[:, :, F + 1]
            V_.reduce_max(ext[:, 0:1], sk, AX.X).then_inc(ext_ready, 1)
            last = step(V_.tensor_scalar(nsk[:], sk, -1.0, None, ALU.mult))
            dve.wait_ge(dstep, last)
            V_.reduce_max(ext[:, 1:2], nsk[:], AX.X).then_inc(ext_ready, 1)
            V_.tensor_copy(wh[:, :, F], BND.broadcast_to([P, NT])).then_inc(bound_col, 1)
            dve.wait_ge(red_ready, 1)
            V_.tensor_scalar(negc[:, 0:1], red[:, 0:1], -1.0, None, ALU.mult).then_inc(negc_ready, 1)
            V_.tensor_scalar(negc[:, 1:2], red[:, 0:1], -SLOPE, None, ALU.mult).then_inc(negc_ready, 1)
            dve.wait_ge(dstep, step(V_.tensor_scalar(z[:], wh[:, :, F + 2], red[:, 0:1], None, ALU.add)))
            V_.tensor_scalar(zu[:], z[:], 1.0 - SLOPE, 0.0, ALU.mult, ALU.min).then_inc(negc_ready, 1)
            V_.tensor_scalar(zv[:], z[:], SLOPE - 1.0, 0.0, ALU.mult, ALU.min).then_inc(negc_ready, 1)
            dve.wait_ge(dstep, step(V_.tensor_scalar(spread, red[:, 0:1], red[:, 1:2], None, ALU.add)))
            V_.tensor_scalar(wide[:], spread, SPREAD, None, ALU.is_gt).then_inc(wide_ready, 1)
            dve.wait_ge(exps_ready, 2)
            V_.tensor_scalar(Xs[:], Xs[:], S, None, ALU.mult).then_inc(xs_ready, 1)
            V_.tensor_scalar(Ys[:], Ys[:], S, None, ALU.mult).then_inc(xs_ready, 1)
            dve.wait_ge(xs_ready, 1)
            dve.wait_ge(bound_col, 1)

            V_.tensor_tensor(wX[:, 0, :, :], wh[:, 0:QJ, 0:V], Xs[:, 0:QJ].unsqueeze(2).broadcast_to([P, QJ, V]),
                             ALU.mult).then_inc(wX0_ready, 1)

            def low_parts(c):
                t0 = QJ * c
                dve.wait_ge(hiX_ready, c + 1)
                V_.scalar_tensor_tensor(out=operands[:, t0:t0 + QJ, V:2 * V], in0=operands[:, t0:t0 + QJ, 0:V],
                                        scalar=-LOW, in1=wX[:, c % 2, :, :], op0=ALU.mult,
                                        op1=ALU.add).then_inc(loX_ready, 1)
                dve.wait_ge(hiY_ready, c + 1)
                V_.scalar_tensor_tensor(out=operands[:, t0:t0 + QJ, 3 * V:4 * V],
                                        in0=operands[:, t0:t0 + QJ, 2 * V:3 * V], scalar=-LOW,
                                        in1=wY[:, c % 2, :, :], op0=ALU.mult, op1=ALU.add).then_inc(loY_ready, 1)

            def mask_quad(b, par, half, q, e=None):
                r = q % 2
                count = NQ * b + q
                if q == 0:
                    dve.wait_ge(sq_landed[par], 16 * half + 16)
                dve.wait_ge(adjT_ready, FILLS * b + 2 * q + 2)
                if isinstance(b, int):
                    adj8 = adjT[:, b, QJ * q:QJ * q + QJ, :]
                else:
                    adj8 = adjT[:, ds(b, 1), QJ * q:QJ * q + QJ, :].squeeze(1)
                for u in range(DJ):
                    V_.tensor_scalar(keep[:, r, u, :], SQ[:, par, :], nsk[:, QJ * q + u:QJ * q + u + 1], ONE8,
                                     ALU.is_gt, ALU.mult).then_inc(compared, 1)
                    if e is not None:
                        epilogue_step(e, q, u)
                if not isinstance(count, int) or count >= 2:
                    dve.wait_ge(masks_used, count - 1)
                dve.wait_ge(signs_ready, count + 1)
                dve.wait_ge(compared, DJ * (count + 1))
                V_.tensor_tensor(maskB[:, r, :, :].bitcast(u32), keep[:, r, :, :].bitcast(u32), adj8.bitcast(u32),
                                 ALU.bitwise_and).then_inc(maskB_ready, 1)
                if e is not None:
                    epilogue_step(e, q, 2)
                dve.wait_ge(maskB_ready, count + 1)
                V_.tensor_tensor(maskC[:, r, :, :].bitcast(u32), maskB[:, r, :, :].bitcast(u32), adj8.bitcast(u32),
                                 ALU.bitwise_xor).then_inc(maskC_ready, 1)
                if e is not None:
                    epilogue_step(e, q, 3)
                if e is not None and q == 0:
                    copy_accB(e)
                if e is not None and q == 4:
                    rows_x1(e)
                if e is not None and q == 6:
                    low_part_G0(e, e)

            def epilogue_step(e, q, u):
                at = EPI * e
                if (q, u) == (1, 0):
                    combine(e, at)
                if (q, u) == (1, 1):
                    scale_B(e, at)
                if (q, u) == (1, 2):
                    add_C(e, at)
                if (q, u) == (1, 3):
                    flag_empty(at)
                if (q, u) == (2, 0):
                    fill_empty(at)
                if (q, u) == (2, 1):
                    recip(at)
                if (q, u) == (2, 2):
                    row_factor(at)
                if (q, u) == (2, 3):
                    split_sign(at)
                if (q, u) == (3, 0):
                    add_x(e, at)
                if (q, u) == (3, 2):
                    make_x1(e, at)
                if (q, u) == (3, 3):
                    stats_x1(e, at)
                if (q, u) == (4, 0):
                    aggregate_x1(at)
                if (q, u) == (4, 1):
                    add_eps(at)

            def copy_accB(e):
                dve.wait_ge(masks_used, NQ * (e + 1))
                V_.tensor_copy(RB[:], acc[:, 0:2, 0:2 * V]).then_inc(accB_copied, 1)

            def tile_col(src, e, s):
                return src[:, ds(2 * e + s, 1)]

            def combine(e, at):
                dve.wait_ge(accB_copied, e + 1)
                V_.scalar_tensor_tensor(out=eM, in0=RB[:, :, V:2 * V], scalar=1.0 / LOW, in1=RB[:, :, 0:V],
                                        op0=ALU.mult, op1=ALU.add).then_inc(epi, 1)
                dve.wait_ge(accC_copied, e + 1)
                V_.scalar_tensor_tensor(out=eC, in0=RC[:, :, V:2 * V], scalar=1.0 / LOW, in1=RC[:, :, 0:V],
                                        op0=ALU.mult, op1=ALU.add).then_inc(combined, 1)

            def scale_B(e, at):
                dve.wait_ge(epi, at + 1)
                for s in range(2):
                    V_.tensor_scalar(eM[:, s, :], eM[:, s, :], tile_col(U, e, s), None, ALU.mult).then_inc(epi, 1)

            def add_C(e, at):
                dve.wait_ge(epi, at + 3)
                dve.wait_ge(combined, e + 1)
                for s in range(2):
                    V_.scalar_tensor_tensor(out=eM[:, s, :], in0=eC[:, s, :], scalar=tile_col(Vv, e, s),
                                            in1=eM[:, s, :], op0=ALU.mult, op1=ALU.add).then_inc(epi, 1)

            def flag_empty(at):
                dve.wait_ge(epi, at + 5)
                V_.tensor_scalar(eflag[:], eM[:, :, F], 0.0, None, ALU.is_equal).then_inc(epi, 1)

            def fill_empty(at):
                dve.wait_ge(epi, at + 6)
                for s in range(2):
                    V_.scalar_tensor_tensor(out=eM[:, s, :], in0=sumWh[:], scalar=eflag[:, s:s + 1],
                                            in1=eM[:, s, :], op0=ALU.mult, op1=ALU.add).then_inc(epi, 1)

            def recip(at):
                dve.wait_ge(epi, at + 8)
                V_.reciprocal(erec[:], eM[:, :, F]).then_inc(epi, 1)

            def row_factor(at):
                dve.wait_ge(epi, at + 9)
                V_.tensor_scalar(escale[:], erec[:], BND, None, ALU.mult).then_inc(epi, 1)

            def split_sign(at):
                dve.wait_ge(epi, at + 10)
                for s in range(2):
                    V_.tensor_scalar(emin[:, s, :], eM[:, s, 0:F], escale[:, s:s + 1], 0.0, ALU.mult,
                                     ALU.min).then_inc(emin_ready, 1)
                for s in range(2):
                    V_.tensor_scalar(eM[:, s, 0:F], eM[:, s, 0:F], escale[:, s:s + 1], 0.0, ALU.mult,
                                     ALU.max).then_inc(epi, 1)

            def add_x(n, at):
                dve.wait_ge(epi, at + 12)
                dve.wait_ge(xt_landed, 16 * n + 16)
                V_.scalar_tensor_tensor(out=ey, in0=eM[:, :, 0:F], scalar=-1.0, in1=xt[:],
                                        op0=ALU.add, op1=ALU.add).then_inc(epi, 1)

            def make_x1(n, at):
                dve.wait_ge(epi, at + 13)
                dve.wait_ge(eexp_ready, n + 1)
                if not isinstance(n, int) or n > 0:
                    dve.wait_ge(x1_stored, 16 * n)
                V_.tensor_tensor(x1[:], ey, emin[:], ALU.add).then_inc(x1_ready, 1)

            def stats_x1(n, at):
                dve.wait_ge(x1_ready, n + 1)
                for s in range(2):
                    V_.bn_stats(bn6[:, s, :], x1[:, s, :]).then_inc(epi, 1)

            def aggregate_x1(at):
                dve.wait_ge(epi, at + 15)
                V_.memset(wait_slot[:], 0.0)
                for s in range(2):
                    V_.bn_aggr(mv[:, s, :], bn6[:, s, :]).then_inc(epi, 1)

            def add_eps(at):
                dve.wait_ge(epi, at + 17)
                V_.tensor_scalar(veps[:, 0:2], mv[:, 0:2, 1], LN_EPS, None, ALU.add).then_inc(veps_ready, 1)

            def rows_x1(n):
                dve.wait_ge(rstd_ready, n + 5)
                for s in range(2):
                    V_.tensor_scalar(emin[:, s, :], x1[:, s, :], mv[:, s, 0:1], rstd[:, s:s + 1], ALU.subtract,
                                     ALU.mult).then_inc(xn_ready, 1)

            def low_part_G0(e, n):
                dve.wait_ge(ghi_ready, n + 1)
                dve.wait_ge(self_ready, n + 1)
                sg = misc[:].rearrange("p (s k f) -> p s k f", s=2, k=2)
                V_.scalar_tensor_tensor(out=G0[:, ds(2 * e, 2), F:2 * F], in0=G0[:, ds(2 * e, 2), 0:F], scalar=-LOW,
                                        in1=sg[:, :, 1, :], op0=ALU.mult, op1=ALU.add).then_inc(g_ready, 1)

            def rest_of_epilogue(e, n, at):
                flag_empty(at)
                fill_empty(at)
                recip(at)
                row_factor(at)
                split_sign(at)
                add_x(n, at)
                make_x1(n, at)
                stats_x1(n, at)
                aggregate_x1(at)
                add_eps(at)
                rows_x1(n)
                low_part_G0(e, n)

            for q in range(NQ):
                mask_quad(0, 0, 0, q)
                low_parts(q)

            def dve_block(b, par, half):
                for q in range(NQ):
                    mask_quad(b, par, half, q, b - 1)

            dve.wait_ge(exps_ready, 4)
            dve.wait_ge(sumwh_ready, 1)
            dve_block(1, 1, 0)
            dve_block(2, 0, 1)
            with dve.Fori(1, (NB - 2) // 2, 1) as it:
                dve_block(2 * it + 1, 1, it)
                dve_block(2 * it + 2, 0, it + 1)
            dve_block(NB - 1, 1, NB // 2 - 1)
            e = NB - 1
            copy_accB(e)
            combine(e, EPI * e)
            scale_B(e, EPI * e)
            add_C(e, EPI * e)
            rest_of_epilogue(e, e, EPI * e)

            with dve.If(nc.vector.value_load(wide[0:1, 0:1], min_val=0, max_val=1)):
                V_.tensor_scalar(wcols[:, 0, :], nsk[:], -1.0, None, ALU.mult).then_inc(wcols_ready, 1)
                V_.tensor_scalar(wcols[:, 1, :], nsk[:], -SLOPE, None, ALU.mult).then_inc(wcols_ready, 1)
                dve.wait_ge(wrow_done, 1)
                V_.tensor_scalar(wrow, misc[0:NT, 0:P], red[0:NT, 1:2], 1.0, ALU.add, ALU.add).then_inc(
                    wrow_ready, 1)
                dve.wait_ge(wh_reloaded, 16)
                with dve.Fori(0, NB, 1) as e:
                    for s in range(2):
                        k = 2 * e + s
                        for c in range(CH):
                            m = CH * k + c
                            dve.wait_ge(wadj_landed, 32 * m + 32)
                            V_.scalar_tensor_tensor(out=wsk, in0=wadj, scalar=BIG, in1=wsk, op0=ALU.mult,
                                                    op1=ALU.min).then_inc(wcand_ready, 1)
                            dve.wait_ge(wcand_ready, m + 1)
                            V_.reduce_max(wmax[:, c:c + 1], wsk, AX.X).then_inc(wmax_ready, 1)
                        dve.wait_ge(wmax_ready, CH * k + CH)
                        V_.reduce_max(wm[:, 0:1], wmax[:, 0:CH], AX.X).then_inc(wstep, 1)
                        dve.wait_ge(wstep, 6 * k + 1)
                        V_.tensor_scalar(wm[:, 1:2], wm[:, 0:1], red[:, 1:2], 1.0, ALU.subtract,
                                         ALU.subtract).then_inc(wstep, 1)
                        dve.wait_ge(wstep, 6 * k + 2)
                        sq = wwh[:, ds(k, 1), F + 2]
                        V_.tensor_tensor(wm[:, 2:3], wm[:, 1:2], sq, ALU.add).then_inc(wstep, 1)
                        dve.wait_ge(wstep, 6 * k + 3)
                        V_.scalar_tensor_tensor(out=wm[:, 3:4], in0=wm[:, 2:3], scalar=SLOPE, in1=wm[:, 2:3],
                                                op0=ALU.mult, op1=ALU.max).then_inc(wstep, 1)
                        dve.wait_ge(wstep, 6 * k + 4)
                        V_.tensor_tensor(wab[:, 0:1], sq, wm[:, 3:4], ALU.subtract).then_inc(wstep, 1)
                        V_.scalar_tensor_tensor(out=wab[:, 1:2], in0=sq, scalar=SLOPE, in1=wm[:, 3:4],
                                                op0=ALU.mult, op1=ALU.subtract).then_inc(wstep, 1)
                        for jt in range(NT):
                            m = NT * k + jt
                            dve.wait_ge(wexps_ready, 2 * m + 2)
                            V_.tensor_tensor(exps[:, jt % 2, 0, :], exps[:, jt % 2, 0, :], exps[:, jt % 2, 1, :],
                                             ALU.max).then_inc(wlarger, 1)
                            dve.wait_ge(wlarger, m + 1)
                            if jt >= 2:
                                dve.wait_ge(probs_used, m - 1)
                            V_.scalar_tensor_tensor(
                                out=probs[:, jt % 2, :],
                                in0=adjT[:, ds(e, 1), jt, s * P:(s + 1) * P].squeeze(1).bitcast(u8), scalar=BIG,
                                in1=exps[:, jt % 2, 0, :], op0=ALU.mult, op1=ALU.min).then_inc(probs_ready, 1)
                        dve.wait_ge(probs_used, NT * k + NT)
                        V_.tensor_copy(eM[:, s, :], acc[:, 0, 0:V]).then_inc(wrows_ready, 1)
                    dve.wait_ge(wrows_ready, 2 * e + 2)
                    rest_of_epilogue(e, NB + e, EPI * NB + (EPI - 5) * e - 5)

            def layer1_rows(t, k, r):
                dve.wait_ge(l1_done, t + 1)
                dve.wait_ge(ring_landed[k], 16 * r + 16)
                V_.scalar_tensor_tensor(out=lring[:, k, :], in0=acc[:, k, F:2 * F], scalar=K0, in1=lring[:, k, :],
                                        op0=ALU.mult, op1=ALU.add).then_inc(l1_sum, 1)
                dve.wait_ge(l1_sum, t + 1)
                if not isinstance(t, int) or t >= 2:
                    dve.wait_ge(hpT_done, t - 1)
                V_.scalar_tensor_tensor(out=hpre[:, k % 2, :], in0=acc[:, k, 0:F], scalar=I0, in1=lring[:, k, :],
                                        op0=ALU.mult, op1=ALU.add).then_inc(l1_half, 1)

            def layer1_low(t):
                dve.wait_ge(g1hi_ready, t + 1)
                dve.wait_ge(self1_ready, t + 1)
                V_.scalar_tensor_tensor(out=G1[:, ds(t, 1), F:2 * F].squeeze(1), in0=G1[:, ds(t, 1), 0:F].squeeze(1),
                                        scalar=-LOW, in1=tp[:, 0, F:2 * F], op0=ALU.mult,
                                        op1=ALU.add).then_inc(g1_ready, 1)

            for k in range(RT):
                layer1_rows(k, k, 0)
                if k >= 1:
                    layer1_low(k - 1)
            with dve.Fori(1, NT // RT, 1) as r:
                for k in range(RT):
                    layer1_rows(RT * r + k, k, r)
                    layer1_low(RT * r + k - 1)
            layer1_low(NT - 1)

            def layer2_rows(t, k, r):
                dve.wait_ge(l2_done, t + 1)
                dve.wait_ge(self1_ready, t + 1)
                V_.scalar_tensor_tensor(out=hpre[:, k % 2, :], in0=acc[:, k, F:2 * F], scalar=K1,
                                        in1=self1[:, ds(t, 1), :].squeeze(1), op0=ALU.mult,
                                        op1=ALU.add).then_inc(l2_half, 1)
                dve.wait_ge(l2_half, t + 1)
                V_.scalar_tensor_tensor(out=hpre[:, k % 2, :], in0=acc[:, k, 0:F], scalar=I1,
                                        in1=hpre[:, k % 2, :], op0=ALU.mult, op1=ALU.add).then_inc(l2_read, 1)
                dve.wait_ge(l2_read, t + 1)
                dve.wait_ge(ring_landed[k], 16 * r + 16 * (NT // RT) + 16)
                if not isinstance(r, int):
                    dve.wait_ge(out_stored[k], 16 * r)
                V_.scalar_tensor_tensor(out=oring[:, k, :], in0=hpre[:, k % 2, :], scalar=0.0,
                                        in1=lring[:, k, :], op0=ALU.max, op1=ALU.add).then_inc(out_ready, 1)

            for k in range(RT):
                layer2_rows(k, k, 0)
            with dve.Fori(1, NT // RT, 1) as r:
                for k in range(RT):
                    layer2_rows(RT * r + k, k, r)

        @block.tensor
        def _(pe):
            PE = nc.tensor
            pe.wait_ge(pool_const, 5)
            pe.wait_ge(weights_landed, 96)
            for k, src in enumerate((0, 1, 2, 3)):
                PE.transpose(tp[:, 0, k * F:(k + 1) * F], wnat[:, src, :], ident[:])
            PE.transpose(acc[:, 3, 0:F], wnat[:, 4, :], ident[:]).then_inc(weightsT, 1)
            pe.wait_ge(wt_copied, 1)
            PE.matmul(misc[:, 0:2], WT[:], acols[:], start=True, stop=True).then_inc(wa_done, 1)
            pe.wait_ge(rhs0_ready, 3)
            pe.wait_ge(const_ready, 1)

            def transpose_adj(b, q):
                for h in range(2):
                    m = 2 * q + h
                    n = FILLS * b + m
                    if n == 0:
                        pe.wait_ge(wsn_ready, 4)
                    if n >= 2:
                        pe.wait_ge(adjT_ready, n - 1)
                    if m % 4 == 0:
                        pe.wait_ge(adj_landed[m // 4], 16 * b + 16)
                    for t in range(2):
                        for s in range(2):
                            jt = 2 * m + t
                            c, at = jt // 8, (jt % 8) * P
                            last = PE.matmul(tp[:, m % 2, t * IB + s * P:t * IB + (s + 1) * P],
                                             stage[:, c, s, at:at + P], ident8[:], start=True, stop=True)
                    last.then_inc(tp_filled, 1)

            for g in range(NT // 4):
                pe.wait_ge(ln_done, g + 1)
                if g >= 1:
                    pe.wait_ge(hT_ready, g)
                for k in range(4):
                    last = PE.transpose(misc[:, k * P:(k + 1) * P], xin[:, 4 * g + k, :], ident[:])
                last.then_inc(xT_done, 1)
                transpose_adj(0, g)
                pe.wait_ge(hT_ready, g + 1)
                if g >= 2:
                    pe.wait_ge(wh_copied, 4 * (g - 1))
                for k in range(4):
                    last = PE.matmul(acc[:, 2 * (g % 2) + k // 2, (k % 2) * 256:(k % 2) * 256 + WHC],
                                     hT[:, k * P:(k + 1) * P], rhs0[:], start=True, stop=True)
                last.then_inc(wh_done, 1)
            pe.wait_ge(wh_copied, NT)
            PE.matmul(misc[0:NT, 0:P], wh[:, :, F + 2], ident[:], start=True, stop=True).then_inc(sqT_done, 1)

            def sum_Wh(q):
                if q == 0:
                    pe.wait_ge(bound_col, 1)
                    pe.wait_ge(sqrow_ready, 1)
                for t in range(QJ * q, QJ * q + QJ):
                    last = PE.matmul(misc[:, P:P + V], ones, wh[:, t, 0:V], start=(t == 0), stop=(t == NT - 1))
                if q == NQ - 1:
                    last.then_inc(sumwh_done, 1)

            def masked_products(b, q):
                pe.wait_ge(maskB_ready, NQ * b + q + 1)
                pe.wait_ge(maskC_ready, NQ * b + q + 1)
                if b == 0:
                    pe.wait_ge(loX_ready, q + 1)
                    pe.wait_ge(loY_ready, q + 1)
                if q == 0 and b >= 1:
                    pe.wait_ge(accB_copied, b)
                    pe.wait_ge(accC_copied, b)
                for u in range(QJ):
                    jt = QJ * q + u
                    for s in range(2):
                        for k, mask in enumerate((maskB, maskC)):
                            last = PE.matmul(acc[:, 2 * k + s, 0:2 * V], mask[:, q % 2, u, s * P:(s + 1) * P],
                                             operands[:, jt, 2 * k * V:2 * (k + 1) * V], start=(jt == 0),
                                             stop=(jt == NT - 1))
                last.then_inc(masks_used, 1)

            def transpose_xn(n):
                pe.wait_ge(xn_ready, 2 * n + 2)
                if not isinstance(n, int) or n >= 1:
                    pe.wait_ge(g_ready, n)
                    pe.wait_ge(self_ready, n)
                for s in range(2):
                    last = PE.transpose(misc[:, s * P:(s + 1) * P], emin[:, s, :], ident[:])
                last.then_inc(eT_done, 1)

            def self_and_G0(n):
                pe.wait_ge(ehT_ready, n + 1)
                for s in range(2):
                    last = PE.matmul(misc[:, s * IB:(s + 1) * IB], hT[:, s * P:(s + 1) * P], wsn0[:], start=True,
                                     stop=True)
                last.then_inc(sg_done, 1)

            for b in range(NB):
                if b + 1 < NB:
                    transpose_adj(b + 1, 0)
                for q in range(NQ):
                    if b + 1 < NB and q + 1 < NQ:
                        transpose_adj(b + 1, q + 1)
                    masked_products(b, q)
                    if b == 0:
                        sum_Wh(q)
                    if b == 1 and q == 0:
                        pe.wait_ge(sumwh_ready, 1)
                    if b >= 1 and q == 4:
                        transpose_xn(b - 1)
                    if b >= 1 and q == 5:
                        self_and_G0(b - 1)
            transpose_xn(NB - 1)
            self_and_G0(NB - 1)

            pe.wait_ge(wide_ready, 1)
            with pe.If(nc.tensor.value_load(wide[0:1, 0:1], min_val=0, max_val=1)):
                pe.wait_ge(wcols_ready, 1)
                pe.wait_ge(g_ready, NB)
                pe.wait_ge(self_ready, NB)
                PE.matmul(misc[0:NT, 0:P], wcols[:, 0, :], ident[:], start=True, stop=True).then_inc(wrow_done, 1)
                pe.wait_ge(wrow_ready, 1)
                pe.wait_ge(wh_reloaded, 16)
                pe.wait_ge(accB_copied, NB)
                with pe.Fori(0, NB, 1) as e:
                    for s in range(2):
                        k = 2 * e + s
                        pe.wait_ge(wstep, 6 * k + 6)
                        for h in range(2):
                            last = PE.matmul(misc[:, h * P:(h + 1) * P], wab[:, h:h + 1].broadcast_to([P, P]),
                                             ident[:], start=True, stop=True)
                        last.then_inc(ab_done, 1)
                        for jt in range(NT):
                            pe.wait_ge(probs_ready, NT * k + jt + 1)
                            PE.matmul(acc[:, 0, 0:V], probs[:, jt % 2, :], wwh[:, jt, 0:V], start=(jt == 0),
                                      stop=(jt == NT - 1)).then_inc(probs_used, 1)
                        pe.wait_ge(wrows_ready, k + 1)
                    transpose_xn(NB + e)
                    self_and_G0(NB + e)
                    pe.wait_ge(g_ready, NB + e + 1)
                    pe.wait_ge(self_ready, NB + e + 1)

            def neighbour_sum(t, jt, G):
                b, s = t // 2, t % 2
                return PE.matmul(acc[:, t % RT, 0:2 * F], adjT[:, b, jt, s * P:(s + 1) * P], G[:, jt, :],
                                 start=(jt == 0), stop=(jt == NT - 1))

            def transpose_h1(t):
                pe.wait_ge(l1_half, t + 1)
                if t >= 1:
                    pe.wait_ge(h1T_ready, t)
                PE.transpose(misc[:, 0:P], hpre[:, t % 2, :], ident[:]).then_inc(hpT_done, 1)

            def self_and_G1(t):
                pe.wait_ge(h1T_ready, t + 1)
                if t >= 1:
                    pe.wait_ge(g1_ready, t)
                    pe.wait_ge(self1_ready, t)
                PE.matmul(tp[:, 0, 0:2 * F], hT[:, (t % 2) * P:(t % 2) * P + P], wsn1[:], start=True,
                          stop=True).then_inc(sg1_done, 1)

            pe.wait_ge(accB_copied, NB)
            pe.wait_ge(accC_copied, NB)
            for t in range(NT):
                if t >= RT:
                    pe.wait_ge(l1_half, t - RT + 1)
                for jt in range(NT):
                    if t == 0:
                        pe.wait_ge(g_ready, jt // 2 + 1)
                    last = neighbour_sum(t, jt, G0)
                    if t >= 1 and jt == 12:
                        transpose_h1(t - 1)
                    if t >= 1 and jt == 24:
                        self_and_G1(t - 1)
                last.then_inc(l1_done, 1)
            transpose_h1(NT - 1)
            self_and_G1(NT - 1)
            for t in range(NT):
                if t < RT:
                    pe.wait_ge(l1_half, NT - RT + t + 1)
                else:
                    pe.wait_ge(l2_read, t - RT + 1)
                for jt in range(NT):
                    if t == 0:
                        pe.wait_ge(g1_ready, jt + 1)
                    last = neighbour_sum(t, jt, G1)
                last.then_inc(l2_done, 1)


_INS = ['x', 'adj', 'L0_gnn_W', 'L0_gnn_a', 'L1_gnn_w_self_0', 'L1_gnn_w_neigh_0', 'L1_gnn_w_self_1',
        'L1_gnn_w_neigh_1']
_OUTS = [((4096, 128), 'float32')]


def kernel(**inputs):
    import numpy as _np
    import concourse.bacc as _bacc
    from concourse import mybir as _mybir
    from concourse.bass_utils import run_bass_kernel_spmd as _run

    nc = _bacc.Bacc("TRN2", target_bir_lowering=False, num_devices=1)
    arrays, args = {}, []
    for name in _INS:
        a = _np.ascontiguousarray(inputs[name])
        arrays[f"in_{name}_dram"] = a
        args.append(nc.dram_tensor(f"in_{name}_dram", a.shape, _mybir.dt.from_np(a.dtype), kind="ExternalInput").ap())
    for i, (shape, dtype) in enumerate(_OUTS):
        dt = _mybir.dt.from_np(_np.dtype(dtype))
        args.append(nc.dram_tensor(f"out_{i}_dram", shape, dt, kind="ExternalOutput").ap())
    gat_sage_kernel(nc, *args)
    r = _run(nc, [arrays], core_ids=[0])
    got = tuple(r.results[0][f"out_{i}_dram"] for i in range(len(_OUTS)))
    return got[0]
```

```python
import concourse.bass as bass
from concourse import mybir
from contextlib import ExitStack


def gat_sage_kernel(nc, x, adj, W, a, ws0, wn0, ws1, wn1, out):
    f32 = mybir.dt.float32
    f16 = mybir.dt.float16
    f8 = mybir.dt.float8e4
    u8 = mybir.dt.uint8
    u16 = mybir.dt.uint16
    i8 = mybir.dt.int8
    u32 = mybir.dt.uint32
    i32 = mybir.dt.int32
    ALU = mybir.AluOpType
    ACT = mybir.ActivationFunctionType
    AX = mybir.AxisListType
    ds = bass.ds

    N, F = x.shape
    P = 128
    NT = N // P
    IB = 2 * P
    NB = N // IB
    QJ = 4
    NQ = NT // QJ
    DJ = 1
    CH = 4
    CW = N // CH
    CQ = NQ // CH
    HP = P // 2
    V = F + 1
    LN_EPS = 1e-5
    SLOPE = 0.2
    HNORM = 11.4
    TINY = 1e-30
    SPREAD = 10.0
    BIG = 1e30
    TOP = 2.0 ** 14
    LOW = 2.0 ** 11
    ONE8 = 56.0
    EPI = 17

    ctx = ExitStack()
    with ctx:
        def sb(name, shape, dt):
            return ctx.enter_context(nc.sbuf_tensor(name, shape, dt))

        def pb(name, shape, dt):
            return ctx.enter_context(nc.psum_tensor(name, shape, dt))

        def sem(name):
            return ctx.enter_context(nc.semaphore(name))

        x1_dram = nc.dram_tensor("x1_scratch", (N, F), f32).ap()
        self0_dram = nc.dram_tensor("self0_scratch", (N, F), f32).ap()
        sq_dram = nc.dram_tensor("sq_scratch", (N,), f32).ap()
        wh_dram = nc.dram_tensor("wh_scratch", (P, NT * (F + 3)), f32).ap()
        skpos_dram = nc.dram_tensor("skpos_scratch", (N,), f32).ap()
        x_t = x.rearrange("(t p) f -> p t f", p=P)
        x1_t = x1_dram.rearrange("(t p) f -> p t f", p=P)
        self0_t = self0_dram.rearrange("(t p) f -> p t f", p=P)
        out_t = out.rearrange("(t p) f -> p t f", p=P)
        adj_c = adj.rearrange("(b s p) (c j) -> b c p s j", s=2, p=P, c=CH)
        skpos_c = skpos_dram.rearrange("(c j) -> c j", c=CH)
        sq_b = sq_dram.rearrange("(b i) -> b i", b=NB)

        adjT = sb("adjT", [P, NB, NT, IB], f8)
        late = adjT[:, NB // 2:, :, :].rearrange("p b t i -> p (b t i)").bitcast(f32)
        xin = late[:, 0:NT * F].rearrange("p (t f) -> p t f", f=F)
        WHC = F + 3
        o = NT * F
        wh = late[:, o:o + NT * WHC].rearrange("p (t f) -> p t f", f=WHC)
        o += NT * WHC
        wX = late[:, o:o + 2 * QJ * V].rearrange("p (k t f) -> p k t f", k=2, f=V)
        o += 2 * QJ * V
        wY = late[:, o:o + 2 * QJ * V].rearrange("p (k t f) -> p k t f", k=2, f=V)

        late_wh = late[:, NT * F:NT * F + NT * WHC]
        setup_end = [o + 2 * QJ * V]

        def setup_only(width):
            setup_end[0] += width
            return late[:, setup_end[0] - width:setup_end[0]]

        operands = sb("operands", [P, NT, 4 * V], f16)
        ops_flat = operands[:].rearrange("p t f -> p (t f)")
        G1 = ops_flat[:, 0:NT * 2 * F].rearrange("p (t f) -> p t f", f=2 * F)
        self1 = ops_flat[:, NT * 2 * F:2 * NT * 2 * F].bitcast(f32).rearrange("p (t f) -> p t f", f=F)
        G0 = sb("G0", [P, NT, 2 * F], f16)
        stage = sb("stage", [P, CH, 2, CW], f8)
        keep = sb("keep", [P, 2, QJ, IB], i8)
        maskB = sb("maskB", [P, 2, QJ, IB], f8)
        maskC = sb("maskC", [P, 2, QJ, IB], f8)
        SQ = sb("SQ", [P, 2, IB], f32)
        ident = sb("ident", [P, P], f32)
        pairs = sb("pairs", [P, HP], f16)
        ones = setup_only(P)
        wnat = setup_only(5 * F).rearrange("p (k f) -> p k f", k=5)
        WT = setup_only(F)
        acols = setup_only(2)
        rhs0 = setup_only(WHC)
        wsn0 = sb("wsn0", [P, 2 * F], f32)
        wsn1 = sb("wsn1", [P, 2 * F], f32)
        junk = sb("junk", [P, F], f32)
        stats = sb("stats", [P, 4], f32)
        norms = sb("norms", [P, 4], f32)
        scales = sb("scales", [P, 16], f32)
        BND, INVB, S, B0, S0, I0, K0, H, B1, S1, I1, K1, spread = (scales[:, i:i + 1] for i in range(13))
        bn6 = sb("bn6", [P, 8, 6], f32)
        mv = sb("mv", [P, 8, 2], f32)
        veps = sb("veps", [P, 8], f32)
        rstdx = sb("rstdx", [P, NT], f32)
        rstd = sb("rstd", [P, 2], f32)
        minus_half = sb("minus_half", [P, 8], f32)
        half = sb("half", [P, 4], f32)
        wait_slot = sb("wait_slot", [P, 1], f32)
        wide = sb("wide", [P, 1], i32)
        hT = sb("hT", [P, 4 * P], f32)
        ext = sb("ext", [P, 2], f32)
        red = sb("red", [P, 2], f32)
        negc = sb("negc", [P, 2], f32)
        z = setup_only(NT)
        zu = setup_only(NT)
        zv = setup_only(NT)
        U = sb("U", [P, NT], f32)
        Vv = sb("Vv", [P, NT], f32)
        Xs = sb("Xs", [P, NT], f32)
        Ys = sb("Ys", [P, NT], f32)
        nsk = sb("nsk", [P, NT], f32)
        sqrow = setup_only(P)[0:NT, :]
        sumWh = sb("sumWh", [P, V], f32)
        RB = sb("RB", [P, 2, 2 * V], f32)
        RC = sb("RC", [P, 2, 2 * V], f32)
        eM, eC, ey = RB[:, :, 0:V], RC[:, :, 0:V], RB[:, :, V:V + F]
        eflag = sb("eflag", [P, 2], f32)
        erec = sb("erec", [P, 2], f32)
        escale = sb("escale", [P, 2], f32)
        emin = sb("emin", [P, 2, F], f32)
        xt = sb("xt", [P, 2, F], f32)
        x1 = sb("x1", [P, 2, F], f32)
        selfst = sb("selfst", [P, 2, F], f32)
        RT = 4
        halves = stage[:].rearrange("p c s j -> p (c s j)").bitcast(f32)
        wadj, wsk = halves[:, 0:CW].bitcast(i32), halves[:, CW:2 * CW]
        o = NT * WHC
        opf = ops_flat.bitcast(f32)
        wwh_flat = opf[:, 0:o]
        wwh = wwh_flat.rearrange("p (t f) -> p t f", f=WHC)
        exps = opf[:, o:o + 4 * P].rearrange("p (k h i) -> p k h i", k=2, h=2)
        o += 4 * P
        probs = opf[:, o:o + 2 * P].rearrange("p (k i) -> p k i", k=2)
        o += 2 * P
        abT = opf[:, o:o + 2 * P].rearrange("p (k i) -> p k i", k=2)
        o += 2 * P
        wrow = opf[0:NT, o:o + P]
        o += P
        wcols = opf[:, o:o + 2 * NT].rearrange("p (k t) -> p k t", k=2)
        o += 2 * NT
        wmax, wm, wab = opf[:, o:o + CH], opf[:, o + CH:o + CH + 4], opf[:, o + CH + 4:o + CH + 6]
        rings = stage[:].rearrange("p c s j -> p (c s j)").bitcast(f32).rearrange("p (k f) -> p k f", f=F)
        lring, oring, hpre = rings[:, 0:RT, :], rings[:, RT:2 * RT, :], rings[:, 2 * RT:2 * RT + 2, :]

        acc = pb("acc", [P, 5, 512], f32)
        tp = pb("tp", [P, 2, 512], f32)
        misc = pb("misc", [P, 512], f32)

        weights_landed = sem("weights_landed")
        x_landed = [sem(f"x_landed{c}") for c in range(4)]
        adj_landed = [sem(f"adj_landed{c}") for c in range(CH)]
        sq_landed = [sem(f"sq_landed{k}") for k in range(2)]
        xt_landed = sem("xt_landed")
        x1_stored = sem("x1_stored")
        self_stored = sem("self_stored")
        sq_stored = sem("sq_stored")
        ring_landed = [sem(f"ring_landed{k}") for k in range(RT)]
        out_stored = [sem(f"out_stored{k}") for k in range(RT)]
        pool_const = sem("pool_const")
        const_ready = sem("const_ready")
        weightsT = sem("weightsT")
        wt_copied = sem("wt_copied")
        wa_done = sem("wa_done")
        rhs0_ready = sem("rhs0_ready")
        stats_ready = sem("stats_ready")
        norms_ready = sem("norms_ready")
        scales_ready = sem("scales_ready")
        dstep = sem("dstep")
        wsn_ready = sem("wsn_ready")
        veps_ready = sem("veps_ready")
        rstd_ready = sem("rstd_ready")
        ln_done = sem("ln_done")
        xT_done = sem("xT_done")
        hT_ready = sem("hT_ready")
        wh_done = sem("wh_done")
        wh_copied = sem("wh_copied")
        bound_col = sem("bound_col")
        ext_ready = sem("ext_ready")
        red_ready = sem("red_ready")
        negc_ready = sem("negc_ready")
        exps_ready = sem("exps_ready")
        xs_ready = sem("xs_ready")
        sqT_done = sem("sqT_done")
        sqrow_ready = sem("sqrow_ready")
        sumwh_done = sem("sumwh_done")
        sumwh_ready = sem("sumwh_ready")
        wX0_ready = sem("wX0_ready")
        wX_ready = sem("wX_ready")
        wY_ready = sem("wY_ready")
        hiX_ready = sem("hiX_ready")
        hiY_ready = sem("hiY_ready")
        loX_ready = sem("loX_ready")
        loY_ready = sem("loY_ready")
        wh_stored = sem("wh_stored")
        tp_filled = sem("tp_filled")
        wide_ready = sem("wide_ready")
        wh_reloaded = sem("wh_reloaded")
        wcols_ready = sem("wcols_ready")
        wrow_done = sem("wrow_done")
        wrow_ready = sem("wrow_ready")
        wrow_stored = sem("wrow_stored")
        wadj_landed = sem("wadj_landed")
        wcand_ready = sem("wcand_ready")
        wmax_ready = sem("wmax_ready")
        wstep = sem("wstep")
        ab_done = sem("ab_done")
        abT_ready = sem("abT_ready")
        wexps_ready = sem("wexps_ready")
        wlarger = sem("wlarger")
        probs_ready = sem("probs_ready")
        probs_used = sem("probs_used")
        wrows_ready = sem("wrows_ready")
        adjT_ready = sem("adjT_ready")
        signs_ready = sem("signs_ready")
        compared = sem("compared")
        maskB_ready = sem("maskB_ready")
        maskC_ready = sem("maskC_ready")
        masks_used = sem("masks_used")
        accB0_copied = sem("accB0_copied")
        accB1_copied = sem("accB1_copied")
        accC_copied = sem("accC_copied")
        epi = sem("epi")
        combined = sem("combined")
        emin_ready = sem("emin_ready")
        eexp_ready = sem("eexp_ready")
        x1_ready = sem("x1_ready")
        xn_ready = sem("xn_ready")
        eT_done = sem("eT_done")
        ehT_ready = sem("ehT_ready")
        sg_done = sem("sg_done")
        ghi_ready = sem("ghi_ready")
        self_ready = sem("self_ready")
        g_ready = sem("g_ready")
        l1_done = sem("l1_done")
        l1_read = sem("l1_read")
        l1_half = sem("l1_half")
        l1_sum = sem("l1_sum")
        hpre_ready = sem("hpre_ready")
        hpT_done = sem("hpT_done")
        h1T_ready = sem("h1T_ready")
        sg1_done = sem("sg1_done")
        g1hi_ready = sem("g1hi_ready")
        self1_ready = sem("self1_ready")
        g1_ready = sem("g1_ready")
        l2_done = sem("l2_done")
        l2_read = sem("l2_read")
        l2_half = sem("l2_half")
        l2_sum = sem("l2_sum")
        out_ready = sem("out_ready")

        B0_BANKS = (0, 4)

        block = ctx.enter_context(nc.Block())

        @block.sync
        def _(sp):
            for c in range(4):
                sp.dma_start(xin[:, 8 * c:8 * c + 8, :], x_t[:, 8 * c:8 * c + 8, :]).then_inc(x_landed[c], 16)
            sp.wait_ge(sqrow_ready, 1)
            sp.dma_start(sq_dram.rearrange("(t p) -> t p", p=P), sqrow[:]).then_inc(sq_stored, 16)
            sp.wait_ge(sq_stored, 16)
            sp.dma_start(SQ[:, 0, :], sq_b[0:1, :].broadcast_to([P, IB])).then_inc(sq_landed[0], 16)
            sp.dma_start(SQ[:, 1, :], sq_b[1:2, :].broadcast_to([P, IB])).then_inc(sq_landed[1], 16)
            sp.dma_start(xt[:], x_t[:, 0:2, :]).then_inc(xt_landed, 16)
            sp.wait_ge(bound_col, 1)
            sp.dma_start(wh_dram, late_wh).then_inc(wh_stored, 16)

            def store_block(e, n):
                sp.wait_ge(x1_ready, n + 1)
                sp.dma_start(x1_t[:, ds(2 * e, 2), :], x1[:]).then_inc(x1_stored, 16)
                sp.wait_ge(self_ready, n + 1)
                sp.dma_start(self0_t[:, ds(2 * e, 2), :], selfst[:]).then_inc(self_stored, 16)

            def serve_block(b, par, last=False):
                sp.wait_ge(maskB_ready, NQ * b)
                if not last:
                    sp.dma_start(SQ[:, 1 - par, :], sq_b[ds(b + 1, 1), :].broadcast_to([P, IB])).then_inc(
                        sq_landed[1 - par], 16)
                sp.wait_ge(x1_ready, b)
                sp.dma_start(xt[:], x_t[:, ds(2 * b, 2), :]).then_inc(xt_landed, 16)
                store_block(b - 1, b - 1)

            serve_block(1, 1)
            with sp.Fori(0, (NB - 4) // 2, 1) as it:
                serve_block(2 * it + 2, 0)
                serve_block(2 * it + 3, 1)
            serve_block(NB - 2, 0)
            serve_block(NB - 1, 1, last=True)
            store_block(NB - 1, NB - 1)
            sp.wait_ge(x1_stored, 16 * NB)
            sp.wait_ge(self_stored, 16 * NB)
            sp.wait_ge(wide_ready, 1)
            with sp.If(nc.sync.value_load(wide[0:1, 0:1], min_val=0, max_val=1)):
                sp.wait_ge(masks_used, NQ * NB)
                sp.wait_ge(wh_stored, 16)
                sp.dma_start(wwh_flat, wh_dram).then_inc(wh_reloaded, 16)
                sp.wait_ge(wrow_ready, 1)
                sp.dma_start(skpos_dram.rearrange("(t p) -> t p", p=P), wrow).then_inc(wrow_stored, 16)
                sp.wait_ge(wrow_stored, 16)
                with sp.Fori(0, NB, 1) as e:
                    for s in range(2):
                        for c in range(CH):
                            if c >= 1:
                                sp.wait_ge(wmax_ready, CH * (2 * e + s) + c)
                            elif s >= 1:
                                sp.wait_ge(wmax_ready, CH * (2 * e + s))
                            else:
                                sp.wait_ge(x1_ready, NB + e)
                            sp.dma_start(wadj, adj_c[ds(e, 1), c, :, s, :].squeeze(0)).then_inc(wadj_landed, 16)
                            sp.dma_start(wsk, skpos_c[c:c + 1, :].broadcast_to([P, CW])).then_inc(wadj_landed, 16)
                    sp.dma_start(xt[:], x_t[:, ds(2 * e, 2), :]).then_inc(xt_landed, 16)
                    store_block(e, NB + e)
                sp.wait_ge(x1_stored, 32 * NB)
                sp.wait_ge(self_stored, 32 * NB)
            for k in range(RT):
                sp.dma_start(lring[:, k, :], self0_t[:, k, :]).then_inc(ring_landed[k], 16)
            with sp.Fori(1, NT // RT, 1) as r:
                for k in range(RT):
                    sp.wait_ge(l1_half, RT * r - RT + k + 1)
                    sp.dma_start(lring[:, k, :], self0_t[:, ds(RT * r + k, 1), :]).then_inc(ring_landed[k], 16)
            for k in range(RT):
                sp.wait_ge(l1_half, NT - RT + k + 1)
                sp.dma_start(lring[:, k, :], x1_t[:, k, :]).then_inc(ring_landed[k], 16)
            with sp.Fori(1, NT // RT, 1) as r:
                for k in range(RT):
                    sp.wait_ge(out_ready, RT * r - RT + k + 1)
                    sp.dma_start(lring[:, k, :], x1_t[:, ds(RT * r + k, 1), :]).then_inc(ring_landed[k], 16)
                    sp.dma_start(out_t[:, ds(RT * r - RT + k, 1), :], oring[:, k, :]).then_inc(out_stored[k], 16)
            for k in range(RT):
                sp.wait_ge(out_ready, NT - RT + k + 1)
                sp.dma_start(out_t[:, NT - RT + k, :], oring[:, k, :]).then_inc(out_stored[k], 16)
            for k in range(RT):
                sp.wait_ge(out_stored[k], 16 * NT // RT)

        @block.gpsimd
        def _(pool):
            nc.gpsimd.memset(ident[:], 0.0).then_inc(pool_const, 1)
            nc.gpsimd.memset(ones, 1.0).then_inc(pool_const, 1)
            nc.gpsimd.memset(minus_half[:], -0.5).then_inc(pool_const, 1)
            nc.gpsimd.memset(half[:], 0.5).then_inc(pool_const, 1)
            pool.wait_ge(pool_const, 4)
            nc.gpsimd.affine_select(out=ident[:], in_=ident[:], compare_op=ALU.not_equal, fill=1.0, base=0,
                                    pattern=[[-1, P]], channel_multiplier=1).then_inc(pool_const, 1)

            def load_adj(b, c):
                pool.dma_start(stage[:, c, :, :], adj_c[b, c, :, :, :]).then_inc(adj_landed[c], 16)

            pool.wait_ge(x_landed[1], 16)
            for c in range(CH):
                load_adj(0, c)
            RMAX = bass.bass_isa.ReduceOp.max

            def x_row_scales(c):
                pool.wait_ge(veps_ready, c + 1)
                nc.gpsimd.tensor_tensor(rstdx[:, 8 * c:8 * c + 8], rstdx[:, 8 * c:8 * c + 8], minus_half[:],
                                        ALU.pow).then_inc(rstd_ready, 1)

            def row_scales(n):
                pool.wait_ge(veps_ready, n + 5)
                nc.gpsimd.tensor_tensor(rstd[:], veps[:, 0:2], minus_half[:, 0:2], ALU.pow).then_inc(rstd_ready, 1)

            x_row_scales(0)
            pool.wait_ge(stats_ready, 4)
            nc.gpsimd.partition_all_reduce(norms[:], stats[:], P, RMAX).then_inc(norms_ready, 1)
            pool.wait_ge(norms_ready, 1)
            nc.gpsimd.tensor_tensor(norms[:], norms[:], half[:], ALU.pow).then_inc(norms_ready, 1)
            for c in range(1, 4):
                x_row_scales(c)
            for c in range(2):
                pool.wait_ge(tp_filled, CQ * (c + 1))
                load_adj(1, c)
            pool.wait_ge(ext_ready, 2)
            nc.gpsimd.partition_all_reduce(red[:], ext[:], P, RMAX).then_inc(red_ready, 1)
            for c in range(2, CH):
                pool.wait_ge(tp_filled, CQ * (c + 1))
                load_adj(1, c)
            pool.wait_ge(xs_ready, 2)
            pool.wait_ge(bound_col, 1)
            for c in range(NQ):
                t0 = QJ * c
                if c >= 1:
                    if c >= 2:
                        pool.wait_ge(loX_ready, c - 1)
                    nc.gpsimd.tensor_tensor(wX[:, c % 2, :, :], wh[:, t0:t0 + QJ, 0:V],
                                            Xs[:, t0:t0 + QJ].unsqueeze(2).broadcast_to([P, QJ, V]),
                                            ALU.mult).then_inc(wX_ready, 1)
                if c >= 2:
                    pool.wait_ge(loY_ready, c - 1)
                nc.gpsimd.tensor_tensor(wY[:, c % 2, :, :], wh[:, t0:t0 + QJ, 0:V],
                                        Ys[:, t0:t0 + QJ].unsqueeze(2).broadcast_to([P, QJ, V]),
                                        ALU.mult).then_inc(wY_ready, 1)

            def refill(b, c):
                pool.wait_ge(tp_filled, NQ * (b - 1) + CQ * (c + 1))
                load_adj(b, c)

            for c in range(CH):
                refill(2, c)
            for b in range(3, NB):
                refill(b, 0)
                refill(b, 1)
                refill(b, 2)
                row_scales(b - 3)
                refill(b, 3)
            for n in range(NB - 3, NB):
                row_scales(n)

            pool.wait_ge(wide_ready, 1)
            with pool.If(nc.gpsimd.value_load(wide[0:1, 0:1], min_val=0, max_val=1)):
                with pool.Fori(0, NB, 1) as e:
                    row_scales(NB + e)

        @block.scalar
        def _(act):
            for k, w in enumerate((W, ws0, wn0, ws1, wn1)):
                act.dma_start(wnat[:, k, :], w).then_inc(weights_landed, 16)
            with nc.allow_non_contiguous_dma(reason="256 numbers"):
                act.dma_start(acols, a.rearrange("(k f) -> f k", k=2)).then_inc(weights_landed, 16)
            act.wait_ge(weightsT, 1)
            nc.scalar.activation(WT[:], tp[:, 0, 0:F], ACT.Copy).then_inc(wt_copied, 1)
            act.wait_ge(weights_landed, 96)
            nc.scalar.activation(rhs0[:, 0:F], wnat[:, 0, :], ACT.Copy).then_inc(rhs0_ready, 1)
            act.wait_ge(wa_done, 1)
            act.wait_ge(rhs0_ready, 2)
            nc.scalar.activation(rhs0[:, F + 1:F + 3], misc[:, 0:2], ACT.Copy).then_inc(rhs0_ready, 1)
            nc.scalar.activation(wsn0[:, 0:F], tp[:, 0, F:2 * F], ACT.Copy).then_inc(wsn_ready, 1)
            nc.scalar.activation(wsn1[:, 0:F], tp[:, 0, 3 * F:4 * F], ACT.Copy).then_inc(wsn_ready, 1)
            act.wait_ge(scales_ready, 1)
            nc.scalar.activation(wsn0[:, F:2 * F], tp[:, 0, 2 * F:3 * F], ACT.Copy, scale=S0).then_inc(wsn_ready, 1)
            nc.scalar.activation(wsn1[:, F:2 * F], acc[:, 3, 0:F], ACT.Copy, scale=S1).then_inc(wsn_ready, 1)

            def keep_adjT(b, q):
                act.wait_ge(tp_filled, NQ * b + q + 1)
                if isinstance(b, int):
                    to = adjT[:, b, QJ * q:QJ * q + QJ, :]
                else:
                    to = adjT[:, ds(b, 1), QJ * q:QJ * q + QJ, :].squeeze(1)
                nc.scalar.activation(to.bitcast(u16), tp[:, q % 2, :].rearrange("p (t i) -> p t i", t=QJ),
                                     ACT.Copy, scale=ONE8).then_inc(adjT_ready, 1)

            for g in range(NT // 4):
                act.wait_ge(xT_done, g + 1)
                if g >= 1:
                    act.wait_ge(wh_done, g)
                nc.scalar.activation(hT[:], misc[:], ACT.Relu).then_inc(hT_ready, 1)
                keep_adjT(0, g)
                act.wait_ge(wh_done, g + 1)
                act.wait_ge(rstd_ready, g // 2 + 1)
                for k in range(4):
                    t = 4 * g + k
                    nc.scalar.activation(wh[:, t, :], acc[:, 2 * (g % 2) + k // 2, (k % 2) * 256:(k % 2) * 256 + WHC],
                                         ACT.Copy, scale=rstdx[:, t:t + 1]).then_inc(wh_copied, 1)
            act.wait_ge(sqT_done, 1)
            nc.scalar.activation(sqrow[:], misc[0:NT, 0:P], ACT.Copy).then_inc(sqrow_ready, 1)
            act.wait_ge(negc_ready, 2)
            act.wait_ge(wh_copied, NT)
            nc.scalar.activation(Xs[:], wh[:, :, F + 1], ACT.Exp, bias=negc[:, 0:1]).then_inc(exps_ready, 1)
            nc.scalar.activation(Ys[:], wh[:, :, F + 1], ACT.Exp, bias=negc[:, 1:2], scale=SLOPE).then_inc(
                exps_ready, 1)
            act.wait_ge(negc_ready, 4)
            nc.scalar.activation(U[:], zu[:], ACT.Exp).then_inc(exps_ready, 1)
            nc.scalar.activation(Vv[:], zv[:], ACT.Exp).then_inc(exps_ready, 1)
            def signs(b, par, half, q):
                count = NQ * b + q
                if q == 0:
                    act.wait_ge(sq_landed[par], 16 * half + 16)
                if not isinstance(count, int) or count >= 2:
                    act.wait_ge(maskB_ready, count - 1)
                for u in range(DJ, QJ):
                    i = nc.scalar.activation(keep[:, q % 2, u, :], SQ[:, par, :], ACT.Sign, scale=-1.0,
                                             bias=nsk[:, QJ * q + u:QJ * q + u + 1])
                i.then_inc(signs_ready, 1)

            signs(0, 0, 0, 0)
            keep_adjT(1, 0)
            for q in range(NQ):
                t0 = QJ * q
                if q == 0:
                    act.wait_ge(wX0_ready, 1)
                else:
                    act.wait_ge(wX_ready, q)
                nc.scalar.activation(operands[:, t0:t0 + QJ, 0:V], wX[:, q % 2, :, :], ACT.Copy,
                                     scale=1.0 / LOW).then_inc(hiX_ready, 1)
                act.wait_ge(wY_ready, q + 1)
                nc.scalar.activation(operands[:, t0:t0 + QJ, 2 * V:3 * V], wY[:, q % 2, :, :], ACT.Copy,
                                     scale=1.0 / LOW).then_inc(hiY_ready, 1)
                if q + 1 < NQ:
                    signs(0, 0, 0, q + 1)
                    keep_adjT(1, q + 1)
                else:
                    signs(1, 1, 0, 0)
                    keep_adjT(2, 0)
            act.wait_ge(sumwh_done, 1)
            nc.scalar.activation(sumWh[:], misc[:, P:P + V], ACT.Copy).then_inc(sumwh_ready, 1)

            def copy_accC(e):
                act.wait_ge(masks_used, NQ * (e + 1))
                if not isinstance(e, int) or e > 0:
                    act.wait_ge(x1_ready, e)
                nc.scalar.activation(RC[:], acc[:, 2:4, 0:2 * V], ACT.Copy).then_inc(accC_copied, 1)

            def elu_exp(n):
                act.wait_ge(emin_ready, 2 * n + 2)
                nc.scalar.activation(emin[:], emin[:], ACT.Exp).then_inc(eexp_ready, 1)

            def relu_T(n):
                act.wait_ge(eT_done, n + 1)
                nc.scalar.activation(hT[:, 0:IB], misc[:, 0:IB], ACT.Relu).then_inc(ehT_ready, 1)

            def split_G0(e, n):
                act.wait_ge(sg_done, n + 1)
                sg = misc[:].rearrange("p (s k f) -> p s k f", s=2, k=2)
                nc.scalar.activation(G0[:, ds(2 * e, 2), 0:F], sg[:, :, 1, :], ACT.Copy,
                                     scale=1.0 / LOW).then_inc(ghi_ready, 1)
                if not isinstance(n, int) or n > 0:
                    act.wait_ge(self_stored, 16 * n)
                nc.scalar.activation(selfst[:], sg[:, :, 0, :], ACT.Copy).then_inc(self_ready, 1)

            def act_block(b, par, half, to_transpose=2, tail=True):
                for q in range(NQ):
                    if q + 1 < NQ:
                        signs(b, par, half, q + 1)
                    elif to_transpose >= 1:
                        signs(b + 1, 1 - par, half + par, 0)
                    if q == 0:
                        copy_accC(b - 1)
                    if q == 1 and tail:
                        relu_T(b - 2)
                    if q == 3 and tail:
                        split_G0(b - 2, b - 2)
                    if q + 1 < NQ and to_transpose >= 1:
                        keep_adjT(b + 1, q + 1)
                    elif q + 1 == NQ and to_transpose == 2:
                        keep_adjT(b + 2, 0)
                    if q == 4:
                        elu_exp(b - 1)

            act.wait_ge(wh_stored, 16)
            act_block(1, 1, 0, tail=False)
            act_block(2, 0, 1)
            with act.Fori(1, (NB - 4) // 2, 1) as it:
                act_block(2 * it + 1, 1, it)
                act_block(2 * it + 2, 0, it + 1)
            act_block(NB - 3, 1, NB // 2 - 2)
            act_block(NB - 2, 0, NB // 2 - 1, to_transpose=1)
            act_block(NB - 1, 1, NB // 2 - 1, to_transpose=0)
            e = NB - 1
            copy_accC(e)
            relu_T(e - 1)
            split_G0(e - 1, e - 1)
            elu_exp(e)
            relu_T(e)
            split_G0(e, e)

            act.wait_ge(wide_ready, 1)
            with act.If(nc.scalar.value_load(wide[0:1, 0:1], min_val=0, max_val=1)):
                with act.Fori(0, NB, 1) as e:
                    for s in range(2):
                        k = 2 * e + s
                        act.wait_ge(ab_done, k + 1)
                        nc.scalar.activation(abT, misc[:, 0:2 * P].rearrange("p (k i) -> p k i", k=2),
                                             ACT.Copy).then_inc(abT_ready, 1)
                        for jt in range(NT):
                            m = NT * k + jt
                            act.wait_ge(wlarger, 3 * m + 3)
                            nc.scalar.activation(exps[:, jt % 2, 0, :], exps[:, jt % 2, 1, :],
                                                 ACT.Exp).then_inc(wexps_ready, 1)
                    elu_exp(NB + e)
                    relu_T(NB + e)
                    split_G0(e, NB + e)

            def layer1_tile(t, k):
                act.wait_ge(hpT_done, t + 1)
                nc.scalar.activation(hT[:, P * (k % 2):P * (k % 2) + P], misc[:, 0:P], ACT.Relu).then_inc(h1T_ready, 1)
                act.wait_ge(sg1_done, t + 1)
                nc.scalar.activation(G1[:, ds(t, 1), 0:F].squeeze(1), tp[:, 0, F:2 * F], ACT.Copy,
                                     scale=1.0 / LOW).then_inc(g1hi_ready, 1)
                nc.scalar.activation(self1[:, ds(t, 1), :].squeeze(1), tp[:, 0, 0:F], ACT.Copy).then_inc(
                    self1_ready, 1)

            with act.Fori(0, NT // RT, 1) as r:
                for k in range(RT):
                    layer1_tile(RT * r + k, k)

        @block.vector
        def _(dve):
            V_ = nc.vector
            n = [0]

            def step(ins):
                ins.then_inc(dstep, 1)
                n[0] += 1
                return n[0]

            dve.wait_ge(pool_const, 5)
            ident_pairs = ident[:].rearrange("p (m k) -> p m k", k=2)
            nc.vector.scalar_tensor_tensor(out=pairs[:], in0=ident_pairs[:, :, 1], scalar=256.0, in1=ident_pairs[:, :, 0],
                                           op0=ALU.mult, op1=ALU.add).then_inc(const_ready, 1)
            nc.vector.memset(rhs0[:, F:F + 1], 0.0).then_inc(rhs0_ready, 1)
            def center(c):
                dve.wait_ge(x_landed[c], 16)
                for t in range(8):
                    last = step(nc.vector.bn_stats(bn6[:, t, :], xin[:, 8 * c + t, :]))
                dve.wait_ge(dstep, last)
                for t in range(8):
                    last = step(nc.vector.bn_aggr(mv[:, t, :], bn6[:, t, :]))
                dve.wait_ge(dstep, last)
                nc.vector.tensor_scalar(rstdx[:, 8 * c:8 * c + 8], mv[:, :, 1], LN_EPS, None,
                                        ALU.add).then_inc(veps_ready, 1)
                for h in range(2):
                    t = 8 * c + 4 * h
                    nc.vector.tensor_tensor(xin[:, t:t + 4, :], xin[:, t:t + 4, :],
                                            mv[:, 4 * h:4 * h + 4, 0:1].broadcast_to([P, 4, F]),
                                            ALU.subtract).then_inc(ln_done, 1)
                dve.wait_ge(ln_done, 2 * c + 2)

            center(0)
            dve.wait_ge(weights_landed, 96)
            for c, k in ((1, 1), (2, 2), (3, 4)):
                nc.vector.tensor_tensor_reduce(out=junk[:], in0=wnat[:, k, :], in1=wnat[:, k, :], scale=1.0,
                                               scalar=TINY, op0=ALU.mult, op1=ALU.add,
                                               accum_out=stats[:, c:c + 1]).then_inc(stats_ready, 1)
                dve.wait_ge(stats_ready, c)
            dve.wait_ge(wt_copied, 1)
            nc.vector.tensor_tensor_reduce(out=junk[:], in0=WT[:], in1=WT[:], scale=1.0, scalar=TINY, op0=ALU.mult,
                                           op1=ALU.add, accum_out=stats[:, 0:1]).then_inc(stats_ready, 1)

            center(1)
            dve.wait_ge(norms_ready, 2)
            nW, nS0, nN0, nN1 = (norms[:, k:k + 1] for k in range(4))
            step(V_.tensor_scalar(BND, nW, HNORM, None, ALU.mult))
            step(V_.tensor_scalar(B0, nN0, HNORM, None, ALU.mult))
            step(V_.scalar_tensor_tensor(out=H, in0=nN0, scalar=float(N), in1=nS0, op0=ALU.mult, op1=ALU.add))
            dve.wait_ge(dstep, n[0])
            dve.wait_ge(dstep, step(V_.tensor_scalar(B1, H, nN1, HNORM * HNORM, ALU.mult, ALU.mult)))
            step(V_.reciprocal(INVB, BND))
            step(V_.reciprocal(S0, B0))
            step(V_.reciprocal(S1, B1))
            step(V_.tensor_scalar(I0, B0, 1.0 / TOP, None, ALU.mult))
            step(V_.tensor_scalar(I1, B1, 1.0 / TOP, None, ALU.mult))
            step(V_.tensor_scalar(K0, B0, 1.0 / TOP / LOW, None, ALU.mult))
            step(V_.tensor_scalar(K1, B1, 1.0 / TOP / LOW, None, ALU.mult))
            dve.wait_ge(dstep, n[0])
            step(V_.tensor_scalar(S, INVB, TOP * LOW, None, ALU.mult))
            step(V_.tensor_scalar(S0, S0, TOP * LOW, None, ALU.mult))
            V_.tensor_scalar(S1, S1, TOP * LOW, None, ALU.mult).then_inc(scales_ready, 1)
            center(2)
            center(3)

            dve.wait_ge(wh_copied, NT)
            sk = wh[:, :, F + 1]
            V_.reduce_max(ext[:, 0:1], sk, AX.X).then_inc(ext_ready, 1)
            last = step(V_.tensor_scalar(nsk[:], sk, -1.0, None, ALU.mult))
            dve.wait_ge(dstep, last)
            V_.reduce_max(ext[:, 1:2], nsk[:], AX.X).then_inc(ext_ready, 1)
            V_.tensor_copy(wh[:, :, F], BND.broadcast_to([P, NT])).then_inc(bound_col, 1)
            dve.wait_ge(red_ready, 1)
            V_.tensor_scalar(negc[:, 0:1], red[:, 0:1], -1.0, None, ALU.mult).then_inc(negc_ready, 1)
            V_.tensor_scalar(negc[:, 1:2], red[:, 0:1], -SLOPE, None, ALU.mult).then_inc(negc_ready, 1)
            dve.wait_ge(dstep, step(V_.tensor_scalar(z[:], wh[:, :, F + 2], red[:, 0:1], None, ALU.add)))
            V_.tensor_scalar(zu[:], z[:], 1.0 - SLOPE, 0.0, ALU.mult, ALU.min).then_inc(negc_ready, 1)
            V_.tensor_scalar(zv[:], z[:], SLOPE - 1.0, 0.0, ALU.mult, ALU.min).then_inc(negc_ready, 1)
            dve.wait_ge(dstep, step(V_.tensor_scalar(spread, red[:, 0:1], red[:, 1:2], None, ALU.add)))
            V_.tensor_scalar(wide[:], spread, SPREAD, None, ALU.is_gt).then_inc(wide_ready, 1)
            dve.wait_ge(exps_ready, 2)
            V_.tensor_scalar(Xs[:], Xs[:], S, None, ALU.mult).then_inc(xs_ready, 1)
            V_.tensor_scalar(Ys[:], Ys[:], S, None, ALU.mult).then_inc(xs_ready, 1)
            dve.wait_ge(xs_ready, 1)
            dve.wait_ge(bound_col, 1)

            V_.tensor_tensor(wX[:, 0, :, :], wh[:, 0:QJ, 0:V], Xs[:, 0:QJ].unsqueeze(2).broadcast_to([P, QJ, V]),
                             ALU.mult).then_inc(wX0_ready, 1)

            def low_parts(c):
                t0 = QJ * c
                dve.wait_ge(hiX_ready, c + 1)
                V_.scalar_tensor_tensor(out=operands[:, t0:t0 + QJ, V:2 * V], in0=operands[:, t0:t0 + QJ, 0:V],
                                        scalar=-LOW, in1=wX[:, c % 2, :, :], op0=ALU.mult,
                                        op1=ALU.add).then_inc(loX_ready, 1)
                dve.wait_ge(hiY_ready, c + 1)
                V_.scalar_tensor_tensor(out=operands[:, t0:t0 + QJ, 3 * V:4 * V],
                                        in0=operands[:, t0:t0 + QJ, 2 * V:3 * V], scalar=-LOW,
                                        in1=wY[:, c % 2, :, :], op0=ALU.mult, op1=ALU.add).then_inc(loY_ready, 1)

            def compare(b, par, half, q):
                if q == 0:
                    dve.wait_ge(sq_landed[par], 16 * half + 16)
                for u in range(DJ):
                    V_.tensor_scalar(keep[:, q % 2, u, :], SQ[:, par, :], nsk[:, QJ * q + u:QJ * q + u + 1], ONE8,
                                     ALU.is_gt, ALU.mult).then_inc(compared, 1)

            def mask_quad(b, par, half, q, e=None, last=False):
                r = q % 2
                count = NQ * b + q
                if q + 1 < NQ:
                    compare(b, par, half, q + 1)
                elif not last:
                    compare(b + 1, 1 - par, half + par, 0)
                if e is not None:
                    epilogue_step(e, q, 0)
                dve.wait_ge(adjT_ready, count + 1)
                if isinstance(b, int):
                    adj8 = adjT[:, b, QJ * q:QJ * q + QJ, :]
                else:
                    adj8 = adjT[:, ds(b, 1), QJ * q:QJ * q + QJ, :].squeeze(1)
                if not isinstance(count, int) or count >= 2:
                    dve.wait_ge(masks_used, count - 1)
                dve.wait_ge(signs_ready, count + 1)
                dve.wait_ge(compared, DJ * (count + 1))
                V_.tensor_tensor(maskB[:, r, :, :].bitcast(u32), keep[:, r, :, :].bitcast(u32), adj8.bitcast(u32),
                                 ALU.bitwise_and).then_inc(maskB_ready, 1)
                if e is not None:
                    epilogue_step(e, q, 1)
                dve.wait_ge(maskB_ready, count + 1)
                V_.tensor_tensor(maskC[:, r, :, :].bitcast(u32), maskB[:, r, :, :].bitcast(u32), adj8.bitcast(u32),
                                 ALU.bitwise_xor).then_inc(maskC_ready, 1)
                if e is not None and q == 0:
                    copy_accB(e, 1 - par)
                if e is not None:
                    epilogue_step(e, q, 2)

            def epilogue_step(e, q, u):
                at = EPI * e
                if (q, u) == (1, 0):
                    combine(e, at)
                if (q, u) == (1, 1):
                    scale_B(e, at)
                if (q, u) == (1, 2):
                    add_C(e, at)
                if (q, u) == (2, 0):
                    flag_empty(at)
                if (q, u) == (2, 1):
                    fill_empty(at)
                if (q, u) == (2, 2):
                    recip(at)
                if (q, u) == (3, 0):
                    row_factor(at)
                if (q, u) == (3, 1):
                    split_sign(e, at)
                if (q, u) == (3, 2):
                    add_x(e, at)
                if (q, u) == (5, 0):
                    make_x1(e, at)
                if (q, u) == (5, 1):
                    stats_x1(e, at)
                if (q, u) == (5, 2):
                    aggregate_x1(at)
                if (q, u) == (6, 0):
                    add_eps(at)
                if (q, u) == (7, 0):
                    rows_x1(e)

            def copy_accB(e, par):
                dve.wait_ge(masks_used, NQ * (e + 1))
                V_.tensor_copy(RB[:, 1, :], acc[:, 1, 0:2 * V]).then_inc(accB1_copied, 1)
                V_.tensor_copy(RB[:, 0, :], acc[:, B0_BANKS[par], 0:2 * V]).then_inc(accB0_copied, 1)

            def tile_col(src, e, s):
                return src[:, ds(2 * e + s, 1)]

            def combine(e, at):
                dve.wait_ge(accB1_copied, e + 1)
                dve.wait_ge(accB0_copied, e + 1)
                V_.scalar_tensor_tensor(out=eM, in0=RB[:, :, V:2 * V], scalar=1.0 / LOW, in1=RB[:, :, 0:V],
                                        op0=ALU.mult, op1=ALU.add).then_inc(epi, 1)
                dve.wait_ge(accC_copied, e + 1)
                V_.scalar_tensor_tensor(out=eC, in0=RC[:, :, V:2 * V], scalar=1.0 / LOW, in1=RC[:, :, 0:V],
                                        op0=ALU.mult, op1=ALU.add).then_inc(combined, 1)

            def scale_B(e, at):
                dve.wait_ge(epi, at + 1)
                for s in range(2):
                    V_.tensor_scalar(eM[:, s, :], eM[:, s, :], tile_col(U, e, s), None, ALU.mult).then_inc(epi, 1)

            def add_C(e, at):
                dve.wait_ge(epi, at + 3)
                dve.wait_ge(combined, e + 1)
                for s in range(2):
                    V_.scalar_tensor_tensor(out=eM[:, s, :], in0=eC[:, s, :], scalar=tile_col(Vv, e, s),
                                            in1=eM[:, s, :], op0=ALU.mult, op1=ALU.add).then_inc(epi, 1)

            def flag_empty(at):
                dve.wait_ge(epi, at + 5)
                V_.tensor_scalar(eflag[:], eM[:, :, F], TINY, None, ALU.is_le).then_inc(epi, 1)

            def fill_empty(at):
                dve.wait_ge(epi, at + 6)
                for s in range(2):
                    V_.scalar_tensor_tensor(out=eM[:, s, :], in0=sumWh[:], scalar=eflag[:, s:s + 1],
                                            in1=eM[:, s, :], op0=ALU.mult, op1=ALU.add).then_inc(epi, 1)

            def recip(at):
                dve.wait_ge(epi, at + 8)
                V_.reciprocal(erec[:], eM[:, :, F]).then_inc(epi, 1)

            def row_factor(at):
                dve.wait_ge(epi, at + 9)
                V_.tensor_scalar(escale[:], erec[:], BND, None, ALU.mult).then_inc(epi, 1)

            def split_sign(n, at):
                dve.wait_ge(epi, at + 10)
                if not isinstance(n, int) or n > 0:
                    dve.wait_ge(eT_done, n)
                for s in range(2):
                    V_.tensor_scalar(emin[:, s, :], eM[:, s, 0:F], escale[:, s:s + 1], 0.0, ALU.mult,
                                     ALU.min).then_inc(emin_ready, 1)
                for s in range(2):
                    V_.tensor_scalar(eM[:, s, 0:F], eM[:, s, 0:F], escale[:, s:s + 1], 0.0, ALU.mult,
                                     ALU.max).then_inc(epi, 1)

            def add_x(n, at):
                dve.wait_ge(epi, at + 12)
                dve.wait_ge(xt_landed, 16 * n + 16)
                V_.scalar_tensor_tensor(out=ey, in0=eM[:, :, 0:F], scalar=-1.0, in1=xt[:],
                                        op0=ALU.add, op1=ALU.add).then_inc(epi, 1)

            def make_x1(n, at):
                dve.wait_ge(epi, at + 13)
                dve.wait_ge(eexp_ready, n + 1)
                if not isinstance(n, int) or n > 0:
                    dve.wait_ge(x1_stored, 16 * n)
                V_.tensor_tensor(x1[:], ey, emin[:], ALU.add).then_inc(x1_ready, 1)

            def stats_x1(n, at):
                dve.wait_ge(x1_ready, n + 1)
                for s in range(2):
                    V_.bn_stats(bn6[:, s, :], x1[:, s, :]).then_inc(epi, 1)

            def aggregate_x1(at):
                dve.wait_ge(epi, at + 15)
                V_.memset(wait_slot[:], 0.0)
                for s in range(2):
                    V_.bn_aggr(mv[:, s, :], bn6[:, s, :]).then_inc(epi, 1)

            def add_eps(at):
                dve.wait_ge(epi, at + 17)
                V_.tensor_scalar(veps[:, 0:2], mv[:, 0:2, 1], LN_EPS, None, ALU.add).then_inc(veps_ready, 1)

            def rows_x1(n):
                dve.wait_ge(rstd_ready, n + 5)
                for s in range(2):
                    V_.tensor_scalar(emin[:, s, :], x1[:, s, :], mv[:, s, 0:1], rstd[:, s:s + 1], ALU.subtract,
                                     ALU.mult).then_inc(xn_ready, 1)

            def low_part_G0(e, n):
                dve.wait_ge(ghi_ready, n + 1)
                dve.wait_ge(self_ready, n + 1)
                sg = misc[:].rearrange("p (s k f) -> p s k f", s=2, k=2)
                V_.scalar_tensor_tensor(out=G0[:, ds(2 * e, 2), F:2 * F], in0=G0[:, ds(2 * e, 2), 0:F], scalar=-LOW,
                                        in1=sg[:, :, 1, :], op0=ALU.mult, op1=ALU.add).then_inc(g_ready, 1)

            def rest_of_epilogue(e, n, at):
                flag_empty(at)
                fill_empty(at)
                recip(at)
                row_factor(at)
                split_sign(n, at)
                add_x(n, at)
                make_x1(n, at)
                stats_x1(n, at)
                aggregate_x1(at)
                add_eps(at)
                rows_x1(n)
                low_part_G0(e, n)

            compare(0, 0, 0, 0)
            for q in range(NQ):
                mask_quad(0, 0, 0, q)
                low_parts(q)

            def dve_block(b, par, half, tail=True, last=False):
                for q in range(NQ):
                    mask_quad(b, par, half, q, b - 1, last)
                    if q == 3 and tail:
                        low_part_G0(b - 2, b - 2)

            dve.wait_ge(exps_ready, 4)
            dve.wait_ge(sumwh_ready, 1)
            dve_block(1, 1, 0, tail=False)
            dve_block(2, 0, 1)
            with dve.Fori(1, (NB - 2) // 2, 1) as it:
                dve_block(2 * it + 1, 1, it)
                dve_block(2 * it + 2, 0, it + 1)
            dve_block(NB - 1, 1, NB // 2 - 1, last=True)
            e = NB - 1
            copy_accB(e, 1)
            combine(e, EPI * e)
            scale_B(e, EPI * e)
            add_C(e, EPI * e)
            low_part_G0(e - 1, e - 1)
            rest_of_epilogue(e, e, EPI * e)

            with dve.If(nc.vector.value_load(wide[0:1, 0:1], min_val=0, max_val=1)):
                V_.tensor_scalar(wcols[:, 0, :], nsk[:], -1.0, None, ALU.mult).then_inc(wcols_ready, 1)
                V_.tensor_scalar(wcols[:, 1, :], nsk[:], -SLOPE, None, ALU.mult).then_inc(wcols_ready, 1)
                dve.wait_ge(wrow_done, 1)
                V_.tensor_scalar(wrow, misc[0:NT, 0:P], red[0:NT, 1:2], 1.0, ALU.add, ALU.add).then_inc(
                    wrow_ready, 1)
                dve.wait_ge(wh_reloaded, 16)
                with dve.Fori(0, NB, 1) as e:
                    for s in range(2):
                        k = 2 * e + s
                        for c in range(CH):
                            m = CH * k + c
                            dve.wait_ge(wadj_landed, 32 * m + 32)
                            V_.scalar_tensor_tensor(out=wsk, in0=wadj, scalar=BIG, in1=wsk, op0=ALU.mult,
                                                    op1=ALU.min).then_inc(wcand_ready, 1)
                            dve.wait_ge(wcand_ready, m + 1)
                            V_.reduce_max(wmax[:, c:c + 1], wsk, AX.X).then_inc(wmax_ready, 1)
                        dve.wait_ge(wmax_ready, CH * k + CH)
                        V_.reduce_max(wm[:, 0:1], wmax[:, 0:CH], AX.X).then_inc(wstep, 1)
                        dve.wait_ge(wstep, 6 * k + 1)
                        V_.tensor_scalar(wm[:, 1:2], wm[:, 0:1], red[:, 1:2], 1.0, ALU.subtract,
                                         ALU.subtract).then_inc(wstep, 1)
                        dve.wait_ge(wstep, 6 * k + 2)
                        sq = wwh[:, ds(k, 1), F + 2]
                        V_.tensor_tensor(wm[:, 2:3], wm[:, 1:2], sq, ALU.add).then_inc(wstep, 1)
                        dve.wait_ge(wstep, 6 * k + 3)
                        V_.scalar_tensor_tensor(out=wm[:, 3:4], in0=wm[:, 2:3], scalar=SLOPE, in1=wm[:, 2:3],
                                                op0=ALU.mult, op1=ALU.max).then_inc(wstep, 1)
                        dve.wait_ge(wstep, 6 * k + 4)
                        V_.tensor_tensor(wab[:, 0:1], sq, wm[:, 3:4], ALU.subtract).then_inc(wstep, 1)
                        V_.scalar_tensor_tensor(out=wab[:, 1:2], in0=sq, scalar=SLOPE, in1=wm[:, 3:4],
                                                op0=ALU.mult, op1=ALU.subtract).then_inc(wstep, 1)
                        dve.wait_ge(wcols_ready, 2)
                        dve.wait_ge(abT_ready, k + 1)
                        for jt in range(NT):
                            m = NT * k + jt
                            if jt >= 2:
                                dve.wait_ge(probs_ready, m - 1)
                            V_.tensor_scalar(exps[:, jt % 2, 0, :], abT[:, 0, :], wcols[:, 0, jt:jt + 1], None,
                                             ALU.add).then_inc(wlarger, 1)
                            dve.wait_ge(wlarger, 3 * m + 1)
                            V_.scalar_tensor_tensor(out=exps[:, jt % 2, 1, :], in0=abT[:, 1, :],
                                                    scalar=wcols[:, 1, jt:jt + 1], in1=exps[:, jt % 2, 0, :],
                                                    op0=ALU.add, op1=ALU.max).then_inc(wlarger, 1)
                            dve.wait_ge(wlarger, 3 * m + 2)
                            V_.tensor_scalar(exps[:, jt % 2, 1, :], exps[:, jt % 2, 1, :], 1.0, None,
                                             ALU.min).then_inc(wlarger, 1)
                            dve.wait_ge(wexps_ready, m + 1)
                            if jt >= 2:
                                dve.wait_ge(probs_used, m - 1)
                            V_.scalar_tensor_tensor(
                                out=probs[:, jt % 2, :],
                                in0=adjT[:, ds(e, 1), jt, s * P:(s + 1) * P].squeeze(1).bitcast(u8), scalar=BIG,
                                in1=exps[:, jt % 2, 0, :], op0=ALU.mult, op1=ALU.min).then_inc(probs_ready, 1)
                        dve.wait_ge(probs_used, NT * k + NT)
                        V_.tensor_copy(eM[:, s, :], acc[:, 0, 0:V]).then_inc(wrows_ready, 1)
                    dve.wait_ge(wrows_ready, 2 * e + 2)
                    rest_of_epilogue(e, NB + e, EPI * NB + (EPI - 5) * e - 5)

            def layer1_rows(t, k, r):
                dve.wait_ge(l1_done, t + 1)
                dve.wait_ge(ring_landed[k], 16 * r + 16)
                V_.scalar_tensor_tensor(out=lring[:, k, :], in0=acc[:, k, F:2 * F], scalar=K0, in1=lring[:, k, :],
                                        op0=ALU.mult, op1=ALU.add).then_inc(l1_sum, 1)
                dve.wait_ge(l1_sum, t + 1)
                if not isinstance(t, int) or t >= 2:
                    dve.wait_ge(hpT_done, t - 1)
                V_.scalar_tensor_tensor(out=hpre[:, k % 2, :], in0=acc[:, k, 0:F], scalar=I0, in1=lring[:, k, :],
                                        op0=ALU.mult, op1=ALU.add).then_inc(l1_half, 1)

            def layer1_low(t):
                dve.wait_ge(g1hi_ready, t + 1)
                dve.wait_ge(self1_ready, t + 1)
                V_.scalar_tensor_tensor(out=G1[:, ds(t, 1), F:2 * F].squeeze(1), in0=G1[:, ds(t, 1), 0:F].squeeze(1),
                                        scalar=-LOW, in1=tp[:, 0, F:2 * F], op0=ALU.mult,
                                        op1=ALU.add).then_inc(g1_ready, 1)

            for k in range(RT):
                layer1_rows(k, k, 0)
                if k >= 1:
                    layer1_low(k - 1)
            with dve.Fori(1, NT // RT, 1) as r:
                for k in range(RT):
                    layer1_rows(RT * r + k, k, r)
                    layer1_low(RT * r + k - 1)
            layer1_low(NT - 1)

            def layer2_rows(t, k, r):
                dve.wait_ge(l2_done, t + 1)
                dve.wait_ge(self1_ready, t + 1)
                V_.scalar_tensor_tensor(out=hpre[:, k % 2, :], in0=acc[:, k, F:2 * F], scalar=K1,
                                        in1=self1[:, ds(t, 1), :].squeeze(1), op0=ALU.mult,
                                        op1=ALU.add).then_inc(l2_half, 1)
                dve.wait_ge(l2_half, t + 1)
                V_.scalar_tensor_tensor(out=hpre[:, k % 2, :], in0=acc[:, k, 0:F], scalar=I1,
                                        in1=hpre[:, k % 2, :], op0=ALU.mult, op1=ALU.add).then_inc(l2_read, 1)
                dve.wait_ge(l2_read, t + 1)
                dve.wait_ge(ring_landed[k], 16 * r + 16 * (NT // RT) + 16)
                if not isinstance(r, int):
                    dve.wait_ge(out_stored[k], 16 * r)
                V_.scalar_tensor_tensor(out=oring[:, k, :], in0=hpre[:, k % 2, :], scalar=0.0,
                                        in1=lring[:, k, :], op0=ALU.max, op1=ALU.add).then_inc(out_ready, 1)

            for k in range(RT):
                layer2_rows(k, k, 0)
            with dve.Fori(1, NT // RT, 1) as r:
                for k in range(RT):
                    layer2_rows(RT * r + k, k, r)

        @block.tensor
        def _(pe):
            PE = nc.tensor
            pe.wait_ge(pool_const, 5)
            pe.wait_ge(weights_landed, 96)
            for k, src in enumerate((0, 1, 2, 3)):
                PE.transpose(tp[:, 0, k * F:(k + 1) * F], wnat[:, src, :], ident[:])
            PE.transpose(acc[:, 3, 0:F], wnat[:, 4, :], ident[:]).then_inc(weightsT, 1)
            pe.wait_ge(wt_copied, 1)
            PE.matmul(misc[:, 0:2], WT[:], acols[:], start=True, stop=True).then_inc(wa_done, 1)
            pe.wait_ge(rhs0_ready, 3)
            pe.wait_ge(const_ready, 1)

            def transpose_adj(b, q):
                n = NQ * b + q
                if n == 0:
                    pe.wait_ge(wsn_ready, 4)
                if n >= 2:
                    pe.wait_ge(adjT_ready, n - 1)
                if q % CQ == 0:
                    pe.wait_ge(adj_landed[q // CQ], 16 * b + 16)
                for u in range(QJ):
                    for s in range(2):
                        jt = QJ * q + u
                        c, at = jt * P // CW, jt * P % CW
                        last = PE.matmul(tp[:, q % 2, (2 * u + s) * HP:(2 * u + s + 1) * HP],
                                         stage[:, c, s, at:at + P], pairs[:], start=True, stop=True)
                last.then_inc(tp_filled, 1)

            for g in range(NT // 4):
                pe.wait_ge(ln_done, g + 1)
                if g >= 1:
                    pe.wait_ge(hT_ready, g)
                for k in range(4):
                    last = PE.transpose(misc[:, k * P:(k + 1) * P], xin[:, 4 * g + k, :], ident[:])
                last.then_inc(xT_done, 1)
                transpose_adj(0, g)
                pe.wait_ge(hT_ready, g + 1)
                if g >= 2:
                    pe.wait_ge(wh_copied, 4 * (g - 1))
                for k in range(4):
                    last = PE.matmul(acc[:, 2 * (g % 2) + k // 2, (k % 2) * 256:(k % 2) * 256 + WHC],
                                     hT[:, k * P:(k + 1) * P], rhs0[:], start=True, stop=True)
                last.then_inc(wh_done, 1)
            pe.wait_ge(wh_copied, NT)
            PE.matmul(misc[0:NT, 0:P], wh[:, :, F + 2], ident[:], start=True, stop=True).then_inc(sqT_done, 1)

            def sum_Wh(q):
                if q == 0:
                    pe.wait_ge(bound_col, 1)
                    pe.wait_ge(sqrow_ready, 1)
                for t in range(QJ * q, QJ * q + QJ):
                    last = PE.matmul(misc[:, P:P + V], ones, wh[:, t, 0:V], start=(t == 0), stop=(t == NT - 1))
                if q == NQ - 1:
                    last.then_inc(sumwh_done, 1)

            def masked_products(b, q):
                for k, mask in enumerate((maskB, maskC)):
                    if k == 0:
                        pe.wait_ge(maskB_ready, NQ * b + q + 1)
                    else:
                        pe.wait_ge(maskC_ready, NQ * b + q + 1)
                    if b == 0:
                        pe.wait_ge((loX_ready, loY_ready)[k], q + 1)
                    for s in range(2):
                        bank = B0_BANKS[b % 2] if 2 * k + s == 0 else 2 * k + s
                        if q == 0 and b >= 1 and k == 1:
                            pe.wait_ge(accC_copied, b)
                        if q == 0 and b >= 1 and k == 0 and s == 1:
                            pe.wait_ge(accB1_copied, b)
                        if q == 0 and b >= 2 and k == 0 and s == 0:
                            pe.wait_ge(accB0_copied, b - 1)
                        for u in range(QJ):
                            jt = QJ * q + u
                            last = PE.matmul(acc[:, bank, 0:2 * V], mask[:, q % 2, u, s * P:(s + 1) * P],
                                             operands[:, jt, 2 * k * V:2 * (k + 1) * V], start=(jt == 0),
                                             stop=(jt == NT - 1))
                last.then_inc(masks_used, 1)

            def transpose_xn(n):
                pe.wait_ge(xn_ready, 2 * n + 2)
                if not isinstance(n, int) or n >= 1:
                    pe.wait_ge(g_ready, n)
                    pe.wait_ge(self_ready, n)
                for s in range(2):
                    last = PE.transpose(misc[:, s * P:(s + 1) * P], emin[:, s, :], ident[:])
                last.then_inc(eT_done, 1)

            def self_and_G0(n):
                pe.wait_ge(ehT_ready, n + 1)
                for s in range(2):
                    last = PE.matmul(misc[:, s * IB:(s + 1) * IB], hT[:, s * P:(s + 1) * P], wsn0[:], start=True,
                                     stop=True)
                last.then_inc(sg_done, 1)

            transpose_adj(1, 0)
            for b in range(NB):
                for q in range(NQ):
                    ahead = NQ * (b + 1) + q + 1
                    if ahead < NQ * NB:
                        transpose_adj(ahead // NQ, ahead % NQ)
                    masked_products(b, q)
                    if b == 0:
                        sum_Wh(q)
                    if b == 1 and q == NQ - 1:
                        pe.wait_ge(sumwh_ready, 1)
                    if b >= 1 and q == NQ - 1:
                        transpose_xn(b - 1)
                    if b >= 2 and q == 1:
                        self_and_G0(b - 2)

            def neighbour_sum(t, jt, G):
                b, s = t // 2, t % 2
                return PE.matmul(acc[:, t % RT, 0:2 * F], adjT[:, b, jt, s * P:(s + 1) * P], G[:, jt, :],
                                 start=(jt == 0), stop=(jt == NT - 1))

            EARLY = NT - 4
            self_and_G0(NB - 2)
            pe.wait_ge(g_ready, NB - 2)
            pe.wait_ge(accB0_copied, NB)
            pe.wait_ge(accB1_copied, NB)
            pe.wait_ge(accC_copied, NB)
            for t in range(RT):
                for jt in range(EARLY):
                    neighbour_sum(t, jt, G0)
                if t == 1:
                    transpose_xn(NB - 1)
                if t == 2:
                    self_and_G0(NB - 1)

            pe.wait_ge(wide_ready, 1)
            with pe.If(nc.tensor.value_load(wide[0:1, 0:1], min_val=0, max_val=1)):
                pe.wait_ge(wcols_ready, 1)
                pe.wait_ge(g_ready, NB)
                pe.wait_ge(self_ready, NB)
                PE.matmul(misc[0:NT, 0:P], wcols[:, 0, :], ident[:], start=True, stop=True).then_inc(wrow_done, 1)
                pe.wait_ge(wrow_ready, 1)
                pe.wait_ge(wh_reloaded, 16)
                with pe.Fori(0, NB, 1) as e:
                    for s in range(2):
                        k = 2 * e + s
                        pe.wait_ge(wstep, 6 * k + 6)
                        for h in range(2):
                            last = PE.matmul(misc[:, h * P:(h + 1) * P], wab[:, h:h + 1].broadcast_to([P, P]),
                                             ident[:], start=True, stop=True)
                        last.then_inc(ab_done, 1)
                        for jt in range(NT):
                            pe.wait_ge(probs_ready, NT * k + jt + 1)
                            PE.matmul(acc[:, 0, 0:V], probs[:, jt % 2, :], wwh[:, jt, 0:V], start=(jt == 0),
                                      stop=(jt == NT - 1)).then_inc(probs_used, 1)
                        pe.wait_ge(wrows_ready, k + 1)
                    transpose_xn(NB + e)
                    self_and_G0(NB + e)
                    pe.wait_ge(g_ready, NB + e + 1)
                    pe.wait_ge(self_ready, NB + e + 1)
                for t in range(RT):
                    for jt in range(EARLY):
                        neighbour_sum(t, jt, G0)

            def transpose_h1(t):
                pe.wait_ge(l1_half, t + 1)
                if t >= 1:
                    pe.wait_ge(h1T_ready, t)
                PE.transpose(misc[:, 0:P], hpre[:, t % 2, :], ident[:]).then_inc(hpT_done, 1)

            def self_and_G1(t):
                pe.wait_ge(h1T_ready, t + 1)
                if t >= 1:
                    pe.wait_ge(g1_ready, t)
                    pe.wait_ge(self1_ready, t)
                PE.matmul(tp[:, 0, 0:2 * F], hT[:, (t % 2) * P:(t % 2) * P + P], wsn1[:], start=True,
                          stop=True).then_inc(sg1_done, 1)

            for t in range(NT):
                if t >= RT:
                    pe.wait_ge(l1_half, t - RT + 1)
                for jt in range(EARLY if t < RT else 0, NT):
                    if t == 0:
                        pe.wait_ge(g_ready, jt // 2 + 1)
                    last = neighbour_sum(t, jt, G0)
                    if t >= RT and jt == 12:
                        transpose_h1(t - 1)
                    if t >= RT and jt == 24:
                        self_and_G1(t - 1)
                last.then_inc(l1_done, 1)
                if 1 <= t < RT:
                    transpose_h1(t - 1)
                    self_and_G1(t - 1)
            for t in range(2):
                pe.wait_ge(l1_half, NT - RT + t + 1)
                for jt in range(EARLY):
                    if t == 0:
                        pe.wait_ge(g1_ready, jt + 1)
                    neighbour_sum(t, jt, G1)
                if t == 0:
                    transpose_h1(NT - 1)
                else:
                    self_and_G1(NT - 1)
            for t in range(NT):
                if 2 <= t < RT:
                    pe.wait_ge(l1_half, NT - RT + t + 1)
                elif t >= RT:
                    pe.wait_ge(l2_read, t - RT + 1)
                for jt in range(EARLY if t < 2 else 0, NT):
                    if t == 0:
                        pe.wait_ge(g1_ready, jt + 1)
                    last = neighbour_sum(t, jt, G1)
                last.then_inc(l2_done, 1)


_INS = ['x', 'adj', 'L0_gnn_W', 'L0_gnn_a', 'L1_gnn_w_self_0', 'L1_gnn_w_neigh_0', 'L1_gnn_w_self_1',
        'L1_gnn_w_neigh_1']
_OUTS = [((4096, 128), 'float32')]


def kernel(**inputs):
    import numpy as _np
    import concourse.bacc as _bacc
    from concourse import mybir as _mybir
    from concourse.bass_utils import run_bass_kernel_spmd as _run

    nc = _bacc.Bacc("TRN2", target_bir_lowering=False, num_devices=1)
    arrays, args = {}, []
    for name in _INS:
        a = _np.ascontiguousarray(inputs[name])
        arrays[f"in_{name}_dram"] = a
        args.append(nc.dram_tensor(f"in_{name}_dram", a.shape, _mybir.dt.from_np(a.dtype), kind="ExternalInput").ap())
    for i, (shape, dtype) in enumerate(_OUTS):
        dt = _mybir.dt.from_np(_np.dtype(dtype))
        args.append(nc.dram_tensor(f"out_{i}_dram", shape, dt, kind="ExternalOutput").ap())
    gat_sage_kernel(nc, *args)
    r = _run(nc, [arrays], core_ids=[0])
    got = tuple(r.results[0][f"out_{i}_dram"] for i in range(len(_OUTS)))
    return got[0]
```

```python
import concourse.bass as bass
from concourse import mybir
from contextlib import ExitStack


def gat_sage_kernel(nc, x, adj, W, a, ws0, wn0, ws1, wn1, out):
    f32 = mybir.dt.float32
    f16 = mybir.dt.float16
    f8 = mybir.dt.float8e4
    u8 = mybir.dt.uint8
    u16 = mybir.dt.uint16
    i8 = mybir.dt.int8
    u32 = mybir.dt.uint32
    i32 = mybir.dt.int32
    ALU = mybir.AluOpType
    ACT = mybir.ActivationFunctionType
    AX = mybir.AxisListType
    ds = bass.ds

    N, F = x.shape
    P = 128
    NT = N // P
    IB = 2 * P
    NB = N // IB
    QJ = 4
    NQ = NT // QJ
    DJ0 = 2
    DJ = 1
    CH = 4
    CW = N // CH
    CQ = NQ // CH
    HP = P // 2
    V = F + 1
    LN_EPS = 1e-5
    SLOPE = 0.2
    HNORM = 11.4
    TINY = 1e-30
    SPREAD = 10.0
    BIG = 1e30
    TOP = 2.0 ** 14
    LOW = 2.0 ** 11
    ONE8 = 56.0
    RW = 4
    GT = 4
    NG = NT // GT
    POOL_G = 5
    EPI = 17

    ctx = ExitStack()
    with ctx:
        def sb(name, shape, dt):
            return ctx.enter_context(nc.sbuf_tensor(name, shape, dt))

        def pb(name, shape, dt):
            return ctx.enter_context(nc.psum_tensor(name, shape, dt))

        def sem(name):
            return ctx.enter_context(nc.semaphore(name))

        x1_dram = nc.dram_tensor("x1_scratch", (N, F), f32).ap()
        self0_dram = nc.dram_tensor("self0_scratch", (N, F), f32).ap()
        sq_dram = nc.dram_tensor("sq_scratch", (N,), f32).ap()
        wh_dram = nc.dram_tensor("wh_scratch", (P, NT * (F + 3)), f32).ap()
        skpos_dram = nc.dram_tensor("skpos_scratch", (N,), f32).ap()
        x_t = x.rearrange("(t p) f -> p t f", p=P)
        x1_t = x1_dram.rearrange("(t p) f -> p t f", p=P)
        self0_t = self0_dram.rearrange("(t p) f -> p t f", p=P)
        out_t = out.rearrange("(t p) f -> p t f", p=P)
        adj_c = adj.rearrange("(b s p) (c j) -> b c p s j", s=2, p=P, c=CH)
        skpos_c = skpos_dram.rearrange("(c j) -> c j", c=CH)
        sq_b = sq_dram.rearrange("(b i) -> b i", b=NB)

        adjT = sb("adjT", [P, NB, NT, IB], f8)
        late = adjT[:, NB // 2:, :, :].rearrange("p b t i -> p (b t i)").bitcast(f32)
        xin = late[:, 0:NT * F].rearrange("p (t f) -> p t f", f=F)
        WHC = F + 3
        o = NT * F
        wh = late[:, o:o + NT * WHC].rearrange("p (t f) -> p t f", f=WHC)
        o += NT * WHC
        wX = late[:, o:o + RW * QJ * V].rearrange("p (k t f) -> p k t f", k=RW, f=V)
        o += RW * QJ * V
        wY = late[:, o:o + RW * QJ * V].rearrange("p (k t f) -> p k t f", k=RW, f=V)

        late_wh = late[:, NT * F:NT * F + NT * WHC]
        setup_end = [o + RW * QJ * V]

        def setup_only(width):
            setup_end[0] += width
            return late[:, setup_end[0] - width:setup_end[0]]

        operands = sb("operands", [P, NT, 4 * V], f16)
        ops_flat = operands[:].rearrange("p t f -> p (t f)")
        G1 = ops_flat[:, 0:NT * 2 * F].rearrange("p (t f) -> p t f", f=2 * F)
        self1 = ops_flat[:, NT * 2 * F:2 * NT * 2 * F].bitcast(f32).rearrange("p (t f) -> p t f", f=F)
        G0 = sb("G0", [P, NT, 2 * F], f16)
        stage = sb("stage", [P, CH, 2, CW], f8)
        keep = sb("keep", [P, 2, QJ, IB], i8)
        maskB = sb("maskB", [P, 2, QJ, IB], f8)
        maskC = sb("maskC", [P, 2, QJ, IB], f8)
        SQ = sb("SQ", [P, 2, IB], f32)
        ident = sb("ident", [P, P], f32)
        pairs = sb("pairs", [P, HP], f16)
        ones = setup_only(P)
        wnat = setup_only(5 * F).rearrange("p (k f) -> p k f", k=5)
        WT = setup_only(F)
        acols = setup_only(2)
        rhs0 = setup_only(WHC)
        wsn0 = sb("wsn0", [P, 2 * F], f32)
        wsn1 = sb("wsn1", [P, 2 * F], f32)
        squares = sb("squares", [P, F], f32)
        stats = sb("stats", [P, 4], f32)
        norms = sb("norms", [P, 4], f32)
        scales = sb("scales", [P, 16], f32)
        BND, INVB, S, B0, S0, I0, K0, H, B1, S1, I1, K1, spread = (scales[:, i:i + 1] for i in range(13))
        bn6 = sb("bn6", [P, 8, 6], f32)
        mv = sb("mv", [P, 8, 2], f32)
        veps = sb("veps", [P, 8], f32)
        rstdx = sb("rstdx", [P, NT], f32)
        rstd = sb("rstd", [P, 2], f32)
        minus_half = sb("minus_half", [P, 8], f32)
        half = sb("half", [P, 4], f32)
        wait_slot = sb("wait_slot", [P, 1], f32)
        wide = sb("wide", [P, 1], i32)
        hT = sb("hT", [P, GT * P], f32)
        hT_ring = (hT[:], setup_only(GT * P))
        mvx = setup_only(2 * NT).rearrange("p (t k) -> p t k", k=2)
        ext = sb("ext", [P, 2], f32)
        red = sb("red", [P, 2], f32)
        negc = sb("negc", [P, 2], f32)
        z = setup_only(NT)
        zu = setup_only(NT)
        zv = setup_only(NT)
        Urow = sb("Urow", [P, NT], f32)
        Vrow = sb("Vrow", [P, NT], f32)
        Xs = sb("Xs", [P, NT], f32)
        Ys = sb("Ys", [P, NT], f32)
        nsk = sb("nsk", [P, NT], f32)
        sqrow = setup_only(P)[0:NT, :]
        sumWh = sb("sumWh", [P, V], f32)
        RB = sb("RB", [P, 2, 2 * V], f32)
        RC = sb("RC", [P, 2, 2 * V], f32)
        eM, eC, ey = RB[:, :, 0:V], RC[:, :, 0:V], RB[:, :, V:V + F]
        eflag = sb("eflag", [P, 2], f32)
        erec = sb("erec", [P, 2], f32)
        escale = sb("escale", [P, 2], f32)
        emin = sb("emin", [P, 2, F], f32)
        xt = sb("xt", [P, 2, F], f32)
        x1 = sb("x1", [P, 2, F], f32)
        selfst = sb("selfst", [P, 2, F], f32)
        RT = 4
        halves = stage[:].rearrange("p c s j -> p (c s j)").bitcast(f32)
        wadj, wsk = halves[:, 0:CW].bitcast(i32), halves[:, CW:2 * CW]
        o = NT * WHC
        opf = ops_flat.bitcast(f32)
        wwh_flat = opf[:, 0:o]
        wwh = wwh_flat.rearrange("p (t f) -> p t f", f=WHC)
        exps = opf[:, o:o + 4 * P].rearrange("p (k h i) -> p k h i", k=2, h=2)
        o += 4 * P
        probs = opf[:, o:o + 2 * P].rearrange("p (k i) -> p k i", k=2)
        o += 2 * P
        abT = opf[:, o:o + 2 * P].rearrange("p (k i) -> p k i", k=2)
        o += 2 * P
        wrow = opf[0:NT, o:o + P]
        o += P
        wcols = opf[:, o:o + 2 * NT].rearrange("p (k t) -> p k t", k=2)
        o += 2 * NT
        wmax, wm, wab = opf[:, o:o + CH], opf[:, o + CH:o + CH + 4], opf[:, o + CH + 4:o + CH + 6]
        rings = stage[:].rearrange("p c s j -> p (c s j)").bitcast(f32).rearrange("p (k f) -> p k f", f=F)
        lring, oring, hpre = rings[:, 0:RT, :], rings[:, RT:2 * RT, :], rings[:, 2 * RT:2 * RT + 2, :]

        acc = pb("acc", [P, 5, 512], f32)
        tp = pb("tp", [P, 2, 512], f32)
        misc = pb("misc", [P, 512], f32)

        W_landed = sem("W_landed")
        weights_landed = sem("weights_landed")
        x_landed = [sem(f"x_landed{c}") for c in range(4)]
        adj_landed = [sem(f"adj_landed{c}") for c in range(CH)]
        sq_landed = [sem(f"sq_landed{k}") for k in range(2)]
        xt_landed = sem("xt_landed")
        x1_stored = sem("x1_stored")
        self_stored = sem("self_stored")
        sq_stored = sem("sq_stored")
        ring_landed = [sem(f"ring_landed{k}") for k in range(RT)]
        out_stored = [sem(f"out_stored{k}") for k in range(RT)]
        pool_const = sem("pool_const")
        const_ready = sem("const_ready")
        weightsT = sem("weightsT")
        wt_copied = sem("wt_copied")
        wa_done = sem("wa_done")
        rhs0_ready = sem("rhs0_ready")
        stats_ready = sem("stats_ready")
        norms_ready = sem("norms_ready")
        scales_ready = sem("scales_ready")
        setup_steps = sem("setup_steps")
        wsn_ready = sem("wsn_ready")
        veps_ready = sem("veps_ready")
        rstd_ready = sem("rstd_ready")
        ln_done = sem("ln_done")
        wsn_copied = sem("wsn_copied")
        wsnT_done = sem("wsnT_done")
        wh_scaled_pool = sem("wh_scaled_pool")
        wh_scaled_dve = sem("wh_scaled_dve")
        first_sq_done = sem("first_sq_done")
        first_sq_ready = sem("first_sq_ready")
        xT_done = sem("xT_done")
        hT_ready = sem("hT_ready")
        wh_done = sem("wh_done")
        wh_copied = sem("wh_copied")
        bound_col = sem("bound_col")
        ext_ready = sem("ext_ready")
        nsk_ready = sem("nsk_ready")
        red_ready = sem("red_ready")
        negc_ready = sem("negc_ready")
        exps_ready = sem("exps_ready")
        xs_ready = sem("xs_ready")
        sqT_done = sem("sqT_done")
        sqrow_ready = sem("sqrow_ready")
        sumwh_done = sem("sumwh_done")
        sumwh_ready = sem("sumwh_ready")
        wX0_ready = sem("wX0_ready")
        wX_ready = sem("wX_ready")
        wY_ready = sem("wY_ready")
        hiX_ready = sem("hiX_ready")
        hiY_ready = sem("hiY_ready")
        loX_ready = sem("loX_ready")
        loY_ready = sem("loY_ready")
        wh_stored = sem("wh_stored")
        adj_transposed = sem("adj_transposed")
        wide_ready = sem("wide_ready")
        wh_reloaded = sem("wh_reloaded")
        wcols_ready = sem("wcols_ready")
        wrow_done = sem("wrow_done")
        wrow_ready = sem("wrow_ready")
        wrow_stored = sem("wrow_stored")
        wadj_landed = sem("wadj_landed")
        wcand_ready = sem("wcand_ready")
        wmax_ready = sem("wmax_ready")
        wstep = sem("wstep")
        ab_done = sem("ab_done")
        abT_ready = sem("abT_ready")
        wexps_ready = sem("wexps_ready")
        wsum_steps = sem("wsum_steps")
        probs_ready = sem("probs_ready")
        probs_used = sem("probs_used")
        wrows_ready = sem("wrows_ready")
        adjT_ready = sem("adjT_ready")
        signs_ready = sem("signs_ready")
        compared = sem("compared")
        maskB_ready = sem("maskB_ready")
        maskC_ready = sem("maskC_ready")
        masks_used = sem("masks_used")
        accB0_copied = sem("accB0_copied")
        accB1_copied = sem("accB1_copied")
        accC_copied = sem("accC_copied")
        epilogue_steps = sem("epilogue_steps")
        combined = sem("combined")
        emin_ready = sem("emin_ready")
        emin_exp_ready = sem("emin_exp_ready")
        x1_ready = sem("x1_ready")
        xn_ready = sem("xn_ready")
        xnT_done = sem("xnT_done")
        xnT_ready = sem("xnT_ready")
        self_G0_done = sem("self_G0_done")
        ghi_ready = sem("ghi_ready")
        self_ready = sem("self_ready")
        g_ready = sem("g_ready")
        l1_done = sem("l1_done")
        l1_half = sem("l1_half")
        l1_sum = sem("l1_sum")
        hpT_done = sem("hpT_done")
        h1T_ready = sem("h1T_ready")
        self_G1_done = sem("self_G1_done")
        g1hi_ready = sem("g1hi_ready")
        self1_ready = sem("self1_ready")
        g1_ready = sem("g1_ready")
        l2_done = sem("l2_done")
        l2_sum = sem("l2_sum")
        l2_half = sem("l2_half")
        out_ready = sem("out_ready")

        B0_BANKS = (0, 4)

        block = ctx.enter_context(nc.Block())

        @block.sync
        def _(sp):
            for c in range(4):
                sp.dma_start(xin[:, 8 * c:8 * c + 8, :], x_t[:, 8 * c:8 * c + 8, :]).then_inc(x_landed[c], 16)
            for k, w in enumerate((ws0, wn0, ws1, wn1)):
                sp.dma_start(wnat[:, 1 + k, :], w).then_inc(weights_landed, 16)
            sp.wait_ge(sqrow_ready, 1)
            sp.dma_start(sq_dram.rearrange("(t p) -> t p", p=P), sqrow[:]).then_inc(sq_stored, 16)
            sp.wait_ge(sq_stored, 16)
            sp.dma_start(xt[:], x_t[:, 0:2, :]).then_inc(xt_landed, 16)
            sp.wait_ge(bound_col, 1)
            sp.dma_start(wh_dram, late_wh).then_inc(wh_stored, 16)

            def store_block(e, n):
                sp.wait_ge(x1_ready, n + 1)
                sp.dma_start(x1_t[:, ds(2 * e, 2), :], x1[:]).then_inc(x1_stored, 16)
                sp.wait_ge(self_ready, n + 1)
                sp.dma_start(self0_t[:, ds(2 * e, 2), :], selfst[:]).then_inc(self_stored, 16)

            def serve_block(b, par, last=False):
                sp.wait_ge(maskB_ready, NQ * b)
                if not last:
                    sp.dma_start(SQ[:, 1 - par, :], sq_b[ds(b + 1, 1), :].broadcast_to([P, IB])).then_inc(
                        sq_landed[1 - par], 16)
                sp.wait_ge(x1_ready, b)
                sp.dma_start(xt[:], x_t[:, ds(2 * b, 2), :]).then_inc(xt_landed, 16)
                store_block(b - 1, b - 1)

            serve_block(1, 1)
            with sp.Fori(0, (NB - 4) // 2, 1) as it:
                serve_block(2 * it + 2, 0)
                serve_block(2 * it + 3, 1)
            serve_block(NB - 2, 0)
            serve_block(NB - 1, 1, last=True)


            def first_self_tiles():
                for k in range(RT):
                    sp.dma_start(lring[:, k, :], self0_t[:, k, :]).then_inc(ring_landed[k], 16)

            sp.wait_ge(wide_ready, 1)
            is_wide = nc.sync.value_load(wide[0:1, 0:1], min_val=0, max_val=1)
            with sp.If(is_wide < 1):
                sp.wait_ge(adj_transposed, NQ * NB)
                sp.wait_ge(x1_stored, 16 * (NB - 1))
                sp.wait_ge(self_stored, 16 * RT // 2)
                first_self_tiles()
            store_block(NB - 1, NB - 1)
            sp.wait_ge(x1_stored, 16 * NB)
            sp.wait_ge(self_stored, 16 * NB)
            with sp.If(is_wide > 0):
                sp.wait_ge(masks_used, NQ * NB)
                sp.wait_ge(wh_stored, 16)
                sp.dma_start(wwh_flat, wh_dram).then_inc(wh_reloaded, 16)
                sp.wait_ge(wrow_ready, 1)
                sp.dma_start(skpos_dram.rearrange("(t p) -> t p", p=P), wrow).then_inc(wrow_stored, 16)
                sp.wait_ge(wrow_stored, 16)
                with sp.Fori(0, NB, 1) as e:
                    for s in range(2):
                        for c in range(CH):
                            if c >= 1:
                                sp.wait_ge(wmax_ready, CH * (2 * e + s) + c)
                            elif s >= 1:
                                sp.wait_ge(wmax_ready, CH * (2 * e + s))
                            else:
                                sp.wait_ge(x1_ready, NB + e)
                            sp.dma_start(wadj, adj_c[ds(e, 1), c, :, s, :].squeeze(0)).then_inc(wadj_landed, 16)
                            sp.dma_start(wsk, skpos_c[c:c + 1, :].broadcast_to([P, CW])).then_inc(wadj_landed, 16)
                    sp.dma_start(xt[:], x_t[:, ds(2 * e, 2), :]).then_inc(xt_landed, 16)
                    store_block(e, NB + e)
                sp.wait_ge(x1_stored, 32 * NB)
                sp.wait_ge(self_stored, 32 * NB)
                first_self_tiles()
            with sp.Fori(1, NT // RT, 1) as r:
                for k in range(RT):
                    sp.wait_ge(l1_half, RT * r - RT + k + 1)
                    sp.dma_start(lring[:, k, :], self0_t[:, ds(RT * r + k, 1), :]).then_inc(ring_landed[k], 16)
            for k in range(RT):
                sp.wait_ge(l1_half, NT - RT + k + 1)
                sp.dma_start(lring[:, k, :], x1_t[:, k, :]).then_inc(ring_landed[k], 16)
            with sp.Fori(1, NT // RT, 1) as r:
                for k in range(RT):
                    sp.wait_ge(out_ready, RT * r - RT + k + 1)
                    sp.dma_start(lring[:, k, :], x1_t[:, ds(RT * r + k, 1), :]).then_inc(ring_landed[k], 16)
                    sp.dma_start(out_t[:, ds(RT * r - RT + k, 1), :], oring[:, k, :]).then_inc(out_stored[k], 16)
            for k in range(RT):
                sp.wait_ge(out_ready, NT - RT + k + 1)
                sp.dma_start(out_t[:, NT - RT + k, :], oring[:, k, :]).then_inc(out_stored[k], 16)
            for k in range(RT):
                sp.wait_ge(out_stored[k], 16 * NT // RT)

        @block.gpsimd
        def _(pool):
            nc.gpsimd.memset(ident[:], 0.0).then_inc(pool_const, 1)
            nc.gpsimd.memset(ones, 1.0).then_inc(pool_const, 1)
            nc.gpsimd.memset(minus_half[:], -0.5).then_inc(pool_const, 1)
            nc.gpsimd.memset(half[:], 0.5).then_inc(pool_const, 1)
            pool.wait_ge(pool_const, 4)
            nc.gpsimd.affine_select(out=ident[:], in_=ident[:], compare_op=ALU.not_equal, fill=1.0, base=0,
                                    pattern=[[-1, P]], channel_multiplier=1).then_inc(pool_const, 1)

            def load_adj(b, c):
                pool.dma_start(stage[:, c, :, :], adj_c[b, c, :, :, :]).then_inc(adj_landed[c], 16)

            pool.wait_ge(x_landed[1], 16)
            for c in range(CH):
                load_adj(0, c)
            RMAX = bass.bass_isa.ReduceOp.max

            def x_row_scales(c):
                pool.wait_ge(veps_ready, c + 1)
                nc.gpsimd.tensor_tensor(rstdx[:, 8 * c:8 * c + 8], rstdx[:, 8 * c:8 * c + 8], minus_half[:],
                                        ALU.pow).then_inc(rstd_ready, 1)

            def row_scales(n):
                pool.wait_ge(veps_ready, n + 5)
                nc.gpsimd.tensor_tensor(rstd[:], veps[:, 0:2], minus_half[:, 0:2], ALU.pow).then_inc(rstd_ready, 1)

            def scale_Wh(g):
                pool.wait_ge(wh_copied, g + 1)
                pool.wait_ge(rstd_ready, g // 2 + 1)
                nc.gpsimd.tensor_tensor(wh[:, GT * g:GT * g + GT, :], wh[:, GT * g:GT * g + GT, :],
                                        rstdx[:, GT * g:GT * g + GT].unsqueeze(2).broadcast_to([P, GT, WHC]),
                                        ALU.mult).then_inc(wh_scaled_pool, 1)

            x_row_scales(0)
            x_row_scales(1)
            scale_Wh(0)
            x_row_scales(2)
            scale_Wh(1)
            x_row_scales(3)
            scale_Wh(2)
            pool.wait_ge(stats_ready, 4)
            nc.gpsimd.partition_all_reduce(norms[:], stats[:], P, RMAX).then_inc(norms_ready, 1)
            pool.wait_ge(norms_ready, 1)
            nc.gpsimd.tensor_tensor(norms[:], norms[:], half[:], ALU.pow).then_inc(norms_ready, 1)
            for g in range(3, POOL_G):
                scale_Wh(g)
            for c in range(2):
                pool.wait_ge(adj_transposed, CQ * (c + 1))
                load_adj(1, c)
            pool.wait_ge(ext_ready, 2)
            nc.gpsimd.partition_all_reduce(red[:], ext[:], P, RMAX).then_inc(red_ready, 1)
            for c in range(2, CH):
                pool.wait_ge(adj_transposed, CQ * (c + 1))
                load_adj(1, c)
            pool.wait_ge(xs_ready, 2)
            pool.wait_ge(bound_col, 1)
            for c in range(NQ):
                t0 = QJ * c
                if c >= 1:
                    if c >= RW:
                        pool.wait_ge(loX_ready, c - RW + 1)
                    nc.gpsimd.tensor_tensor(wX[:, c % RW, :, :], wh[:, t0:t0 + QJ, 0:V],
                                            Xs[:, t0:t0 + QJ].unsqueeze(2).broadcast_to([P, QJ, V]),
                                            ALU.mult).then_inc(wX_ready, 1)
                if c >= RW:
                    pool.wait_ge(loY_ready, c - RW + 1)
                nc.gpsimd.tensor_tensor(wY[:, c % RW, :, :], wh[:, t0:t0 + QJ, 0:V],
                                        Ys[:, t0:t0 + QJ].unsqueeze(2).broadcast_to([P, QJ, V]),
                                        ALU.mult).then_inc(wY_ready, 1)

            def refill(b, c):
                pool.wait_ge(adj_transposed, NQ * (b - 1) + CQ * (c + 1))
                load_adj(b, c)

            for c in range(CH):
                refill(2, c)
            for b in range(3, NB):
                refill(b, 0)
                refill(b, 1)
                refill(b, 2)
                row_scales(b - 3)
                refill(b, 3)
            for n in range(NB - 3, NB):
                row_scales(n)

            pool.wait_ge(wide_ready, 1)
            with pool.If(nc.gpsimd.value_load(wide[0:1, 0:1], min_val=0, max_val=1)):
                with pool.Fori(0, NB, 1) as e:
                    row_scales(NB + e)

        @block.scalar
        def _(act):
            act.dma_start(wnat[:, 0, :], W).then_inc(W_landed, 16)
            with nc.allow_non_contiguous_dma(reason="256 numbers"):
                act.dma_start(acols, a.rearrange("(k f) -> f k", k=2)).then_inc(W_landed, 16)
            act.wait_ge(W_landed, 32)
            nc.scalar.activation(rhs0[:, 0:F], wnat[:, 0, :], ACT.Copy).then_inc(rhs0_ready, 1)
            act.wait_ge(weightsT, 1)
            nc.scalar.activation(WT[:], tp[:, 1, 0:F], ACT.Copy).then_inc(wt_copied, 1)
            act.wait_ge(wa_done, 1)
            act.wait_ge(rhs0_ready, 2)
            nc.scalar.activation(rhs0[:, F + 1:F + 3], tp[:, 1, F:F + 2], ACT.Copy).then_inc(rhs0_ready, 1)

            def keep_adjT(b, q):
                act.wait_ge(adj_transposed, NQ * b + q + 1)
                if isinstance(b, int):
                    to = adjT[:, b, QJ * q:QJ * q + QJ, :]
                else:
                    to = adjT[:, ds(b, 1), QJ * q:QJ * q + QJ, :].squeeze(1)
                nc.scalar.activation(to.bitcast(u16), tp[:, q % 2, :].rearrange("p (t i) -> p t i", t=QJ),
                                     ACT.Copy, scale=ONE8).then_inc(adjT_ready, 1)

            def copy_Wh(g):
                act.wait_ge(wh_done, g + 1)
                pair = 2 * (g % 2)
                nc.scalar.activation(wh[:, GT * g:GT * g + GT, :],
                                     acc[:, pair:pair + 2, :].rearrange("p k (t f) -> p (k t) f", t=2)[:, :, 0:WHC],
                                     ACT.Copy).then_inc(wh_copied, 1)

            for g in range(NG):
                act.wait_ge(xT_done, g + 1)
                if g >= 2:
                    act.wait_ge(wh_done, g - 1)
                nc.scalar.activation(hT_ring[g % 2], misc[:], ACT.Relu).then_inc(hT_ready, 1)
                if g == 1:
                    act.wait_ge(wsnT_done, 1)
                    nc.scalar.activation(wsn0[:], acc[:, 4, 0:2 * F], ACT.Copy).then_inc(wsn_copied, 1)
                    nc.scalar.activation(wsn1[:], acc[:, 4, 2 * F:4 * F], ACT.Copy).then_inc(wsn_copied, 1)
                if g >= 1:
                    copy_Wh(g - 1)
                    keep_adjT(0, g - 1)
            copy_Wh(NG - 1)
            keep_adjT(0, NG - 1)
            act.wait_ge(first_sq_done, 1)
            nc.scalar.activation(SQ[:].rearrange("p b i -> p (b i)"), acc[:, 4, :],
                                 ACT.Copy).then_inc(first_sq_ready, 1)
            act.wait_ge(sqT_done, 1)
            nc.scalar.activation(sqrow[:], misc[0:NT, 0:P], ACT.Copy).then_inc(sqrow_ready, 1)

            def signs(b, par, half, q):
                count = NQ * b + q
                if q == 0 and isinstance(b, int) and b < 2:
                    act.wait_ge(first_sq_ready, 1)
                elif q == 0:
                    act.wait_ge(sq_landed[par], 16 * half)
                if not isinstance(count, int) or count >= 2:
                    act.wait_ge(maskB_ready, count - 1)
                for u in range(DJ0 if isinstance(b, int) and b == 0 else DJ, QJ):
                    i = nc.scalar.activation(keep[:, q % 2, u, :], SQ[:, par, :], ACT.Sign, scale=-1.0,
                                             bias=nsk[:, QJ * q + u:QJ * q + u + 1])
                i.then_inc(signs_ready, 1)

            act.wait_ge(nsk_ready, 1)
            signs(0, 0, 0, 0)
            act.wait_ge(negc_ready, 2)
            act.wait_ge(wh_scaled_pool, POOL_G)
            act.wait_ge(wh_scaled_dve, NG - POOL_G)
            nc.scalar.activation(Xs[:], wh[:, :, F + 1], ACT.Exp, bias=negc[:, 0:1]).then_inc(exps_ready, 1)
            nc.scalar.activation(Ys[:], wh[:, :, F + 1], ACT.Exp, bias=negc[:, 1:2], scale=SLOPE).then_inc(
                exps_ready, 1)
            act.wait_ge(negc_ready, 4)
            nc.scalar.activation(Urow[:], zu[:], ACT.Exp).then_inc(exps_ready, 1)
            nc.scalar.activation(Vrow[:], zv[:], ACT.Exp).then_inc(exps_ready, 1)
            keep_adjT(1, 0)
            for q in range(NQ):
                t0 = QJ * q
                if q == 0:
                    act.wait_ge(wX0_ready, 1)
                else:
                    act.wait_ge(wX_ready, q)
                nc.scalar.activation(operands[:, t0:t0 + QJ, 0:V], wX[:, q % RW, :, :], ACT.Copy,
                                     scale=1.0 / LOW).then_inc(hiX_ready, 1)
                act.wait_ge(wY_ready, q + 1)
                nc.scalar.activation(operands[:, t0:t0 + QJ, 2 * V:3 * V], wY[:, q % RW, :, :], ACT.Copy,
                                     scale=1.0 / LOW).then_inc(hiY_ready, 1)
                if q + 1 < NQ:
                    signs(0, 0, 0, q + 1)
                    keep_adjT(1, q + 1)
                else:
                    signs(1, 1, 0, 0)
                    keep_adjT(2, 0)
            act.wait_ge(sumwh_done, 1)
            nc.scalar.activation(sumWh[:], misc[:, P:P + V], ACT.Copy).then_inc(sumwh_ready, 1)

            def copy_accC(e):
                act.wait_ge(masks_used, NQ * (e + 1))
                if not isinstance(e, int) or e > 0:
                    act.wait_ge(x1_ready, e)
                nc.scalar.activation(RC[:], acc[:, 2:4, 0:2 * V], ACT.Copy).then_inc(accC_copied, 1)

            def elu_exp(n):
                act.wait_ge(emin_ready, 2 * n + 2)
                nc.scalar.activation(emin[:], emin[:], ACT.Exp).then_inc(emin_exp_ready, 1)

            def relu_T(n):
                act.wait_ge(xnT_done, n + 1)
                nc.scalar.activation(hT[:, 0:IB], misc[:, 0:IB], ACT.Relu).then_inc(xnT_ready, 1)

            def split_G0(e, n):
                act.wait_ge(self_G0_done, n + 1)
                sg = misc[:].rearrange("p (s k f) -> p s k f", s=2, k=2)
                nc.scalar.activation(G0[:, ds(2 * e, 2), 0:F], sg[:, :, 1, :], ACT.Copy,
                                     scale=1.0 / LOW).then_inc(ghi_ready, 1)
                if not isinstance(n, int) or n > 0:
                    act.wait_ge(self_stored, 16 * n)
                nc.scalar.activation(selfst[:], sg[:, :, 0, :], ACT.Copy).then_inc(self_ready, 1)

            def act_block(b, par, half, to_transpose=2, tail=True):
                for q in range(NQ):
                    if q + 1 < NQ:
                        signs(b, par, half, q + 1)
                    elif to_transpose >= 1:
                        signs(b + 1, 1 - par, half + par, 0)
                    if q == 0:
                        copy_accC(b - 1)
                    if q == 1 and tail:
                        relu_T(b - 2)
                    if q == 3 and tail:
                        split_G0(b - 2, b - 2)
                    if q + 1 < NQ and to_transpose >= 1:
                        keep_adjT(b + 1, q + 1)
                    elif q + 1 == NQ and to_transpose == 2:
                        keep_adjT(b + 2, 0)
                    if q == 4:
                        elu_exp(b - 1)

            act.wait_ge(wh_stored, 16)
            act_block(1, 1, 0, tail=False)
            act_block(2, 0, 1)
            with act.Fori(1, (NB - 4) // 2, 1) as it:
                act_block(2 * it + 1, 1, it)
                act_block(2 * it + 2, 0, it + 1)
            act_block(NB - 3, 1, NB // 2 - 2)
            act_block(NB - 2, 0, NB // 2 - 1, to_transpose=1)
            act_block(NB - 1, 1, NB // 2 - 1, to_transpose=0)
            e = NB - 1
            copy_accC(e)
            relu_T(e - 1)
            split_G0(e - 1, e - 1)
            elu_exp(e)
            relu_T(e)
            split_G0(e, e)

            act.wait_ge(wide_ready, 1)
            with act.If(nc.scalar.value_load(wide[0:1, 0:1], min_val=0, max_val=1)):
                with act.Fori(0, NB, 1) as e:
                    for s in range(2):
                        k = 2 * e + s
                        act.wait_ge(ab_done, k + 1)
                        nc.scalar.activation(abT, misc[:, 0:2 * P].rearrange("p (k i) -> p k i", k=2),
                                             ACT.Copy).then_inc(abT_ready, 1)
                        for jt in range(NT):
                            m = NT * k + jt
                            act.wait_ge(wsum_steps, 3 * m + 3)
                            nc.scalar.activation(exps[:, jt % 2, 0, :], exps[:, jt % 2, 1, :],
                                                 ACT.Exp).then_inc(wexps_ready, 1)
                    elu_exp(NB + e)
                    relu_T(NB + e)
                    split_G0(e, NB + e)

            def layer1_tile(t, k):
                act.wait_ge(hpT_done, t + 1)
                nc.scalar.activation(hT[:, P * (k % 2):P * (k % 2) + P], misc[:, 0:P], ACT.Relu).then_inc(h1T_ready, 1)
                act.wait_ge(self_G1_done, t + 1)
                nc.scalar.activation(G1[:, ds(t, 1), 0:F].squeeze(1), tp[:, 0, F:2 * F], ACT.Copy,
                                     scale=1.0 / LOW).then_inc(g1hi_ready, 1)
                nc.scalar.activation(self1[:, ds(t, 1), :].squeeze(1), tp[:, 0, 0:F], ACT.Copy).then_inc(
                    self1_ready, 1)

            with act.Fori(0, NT // RT, 1) as r:
                for k in range(RT):
                    layer1_tile(RT * r + k, k)

        @block.vector
        def _(dve):
            counted = [0]

            def step(ins):
                ins.then_inc(setup_steps, 1)
                counted[0] += 1
                return counted[0]

            dve.wait_ge(pool_const, 5)
            ident_pairs = ident[:].rearrange("p (m k) -> p m k", k=2)
            nc.vector.scalar_tensor_tensor(out=pairs[:], in0=ident_pairs[:, :, 1], scalar=256.0,
                                           in1=ident_pairs[:, :, 0], op0=ALU.mult, op1=ALU.add).then_inc(const_ready, 1)
            nc.vector.memset(rhs0[:, F:F + 1], 0.0).then_inc(rhs0_ready, 1)

            def center(c):
                dve.wait_ge(x_landed[c], 16)
                for t in range(8):
                    last = step(nc.vector.bn_stats(bn6[:, t, :], xin[:, 8 * c + t, :]))
                dve.wait_ge(setup_steps, last)
                for t in range(8):
                    last = step(nc.vector.bn_aggr(mvx[:, 8 * c + t, :], bn6[:, t, :]))
                dve.wait_ge(setup_steps, last)
                for h in range(2):
                    t = 8 * c + GT * h
                    nc.vector.tensor_tensor(xin[:, t:t + GT, :], xin[:, t:t + GT, :],
                                            mvx[:, t:t + GT, 0:1].broadcast_to([P, GT, F]),
                                            ALU.subtract).then_inc(ln_done, 1)
                nc.vector.tensor_scalar(rstdx[:, 8 * c:8 * c + 8], mvx[:, 8 * c:8 * c + 8, 1], LN_EPS, None,
                                        ALU.add).then_inc(veps_ready, 1)

            for c in range(4):
                center(c)
            dve.wait_ge(weights_landed, 64)
            for c, k in ((1, 1), (2, 2), (3, 4)):
                nc.vector.tensor_tensor_reduce(out=squares[:], in0=wnat[:, k, :], in1=wnat[:, k, :], scale=1.0,
                                               scalar=TINY, op0=ALU.mult, op1=ALU.add,
                                               accum_out=stats[:, c:c + 1]).then_inc(stats_ready, 1)
                dve.wait_ge(stats_ready, c)
            dve.wait_ge(wt_copied, 1)
            nc.vector.tensor_tensor_reduce(out=squares[:], in0=WT[:], in1=WT[:], scale=1.0, scalar=TINY, op0=ALU.mult,
                                           op1=ALU.add, accum_out=stats[:, 0:1]).then_inc(stats_ready, 1)

            dve.wait_ge(norms_ready, 2)
            nW, nS0, nN0, nN1 = (norms[:, k:k + 1] for k in range(4))
            step(nc.vector.tensor_scalar(BND, nW, HNORM, None, ALU.mult))
            step(nc.vector.tensor_scalar(B0, nN0, HNORM, None, ALU.mult))
            step(nc.vector.scalar_tensor_tensor(out=H, in0=nN0, scalar=float(N), in1=nS0, op0=ALU.mult, op1=ALU.add))
            dve.wait_ge(setup_steps, counted[0])
            dve.wait_ge(setup_steps, step(nc.vector.tensor_scalar(B1, H, nN1, HNORM * HNORM, ALU.mult, ALU.mult)))
            step(nc.vector.reciprocal(INVB, BND))
            step(nc.vector.reciprocal(S0, B0))
            step(nc.vector.reciprocal(S1, B1))
            step(nc.vector.tensor_scalar(I0, B0, 1.0 / TOP, None, ALU.mult))
            step(nc.vector.tensor_scalar(I1, B1, 1.0 / TOP, None, ALU.mult))
            step(nc.vector.tensor_scalar(K0, B0, 1.0 / TOP / LOW, None, ALU.mult))
            step(nc.vector.tensor_scalar(K1, B1, 1.0 / TOP / LOW, None, ALU.mult))
            dve.wait_ge(setup_steps, counted[0])
            step(nc.vector.tensor_scalar(S, INVB, TOP * LOW, None, ALU.mult))
            step(nc.vector.tensor_scalar(S0, S0, TOP * LOW, None, ALU.mult))
            nc.vector.tensor_scalar(S1, S1, TOP * LOW, None, ALU.mult).then_inc(scales_ready, 1)
            dve.wait_ge(scales_ready, 1)
            dve.wait_ge(setup_steps, counted[0])
            for g in range(POOL_G, NG):
                dve.wait_ge(wh_copied, g + 1)
                dve.wait_ge(rstd_ready, g // 2 + 1)
                nc.vector.tensor_tensor(wh[:, GT * g:GT * g + GT, :], wh[:, GT * g:GT * g + GT, :],
                                        rstdx[:, GT * g:GT * g + GT].unsqueeze(2).broadcast_to([P, GT, WHC]),
                                        ALU.mult).then_inc(wh_scaled_dve, 1)

            def compare(b, par, half, q):
                if q == 0 and isinstance(b, int) and b < 2:
                    dve.wait_ge(first_sq_ready, 1)
                elif q == 0:
                    dve.wait_ge(sq_landed[par], 16 * half)
                for u in range(DJ0 if isinstance(b, int) and b == 0 else DJ):
                    nc.vector.tensor_scalar(keep[:, q % 2, u, :], SQ[:, par, :], nsk[:, QJ * q + u:QJ * q + u + 1],
                                            ONE8, ALU.is_gt, ALU.mult).then_inc(compared, 1)

            dve.wait_ge(wh_scaled_pool, POOL_G)
            dve.wait_ge(wh_scaled_dve, NG - POOL_G)
            sk = wh[:, :, F + 1]
            nc.vector.reduce_max(ext[:, 0:1], sk, AX.X).then_inc(ext_ready, 1)
            nc.vector.tensor_scalar(nsk[:], sk, -1.0, None, ALU.mult).then_inc(nsk_ready, 1)
            dve.wait_ge(nsk_ready, 1)
            nc.vector.reduce_max(ext[:, 1:2], nsk[:], AX.X).then_inc(ext_ready, 1)
            nc.vector.tensor_copy(wh[:, :, F], BND.broadcast_to([P, NT])).then_inc(bound_col, 1)
            compare(0, 0, 0, 0)
            dve.wait_ge(red_ready, 1)
            nc.vector.tensor_scalar(negc[:, 0:1], red[:, 0:1], -1.0, None, ALU.mult).then_inc(negc_ready, 1)
            nc.vector.tensor_scalar(negc[:, 1:2], red[:, 0:1], -SLOPE, None, ALU.mult).then_inc(negc_ready, 1)
            dve.wait_ge(setup_steps, step(nc.vector.tensor_scalar(z[:], wh[:, :, F + 2], red[:, 0:1], None, ALU.add)))
            nc.vector.tensor_scalar(zu[:], z[:], 1.0 - SLOPE, 0.0, ALU.mult, ALU.min).then_inc(negc_ready, 1)
            nc.vector.tensor_scalar(zv[:], z[:], SLOPE - 1.0, 0.0, ALU.mult, ALU.min).then_inc(negc_ready, 1)
            dve.wait_ge(setup_steps, step(nc.vector.tensor_scalar(spread, red[:, 0:1], red[:, 1:2], None, ALU.add)))
            nc.vector.tensor_scalar(wide[:], spread, SPREAD, None, ALU.is_gt).then_inc(wide_ready, 1)
            dve.wait_ge(exps_ready, 2)
            nc.vector.tensor_scalar(Xs[:], Xs[:], S, None, ALU.mult).then_inc(xs_ready, 1)
            nc.vector.tensor_scalar(Ys[:], Ys[:], S, None, ALU.mult).then_inc(xs_ready, 1)
            dve.wait_ge(xs_ready, 1)
            dve.wait_ge(bound_col, 1)

            nc.vector.tensor_tensor(wX[:, 0, :, :], wh[:, 0:QJ, 0:V], Xs[:, 0:QJ].unsqueeze(2).broadcast_to([P, QJ, V]),
                                    ALU.mult).then_inc(wX0_ready, 1)

            def low_parts(c):
                t0 = QJ * c
                dve.wait_ge(hiX_ready, c + 1)
                nc.vector.scalar_tensor_tensor(out=operands[:, t0:t0 + QJ, V:2 * V], in0=operands[:, t0:t0 + QJ, 0:V],
                                               scalar=-LOW, in1=wX[:, c % RW, :, :], op0=ALU.mult,
                                               op1=ALU.add).then_inc(loX_ready, 1)
                dve.wait_ge(hiY_ready, c + 1)
                nc.vector.scalar_tensor_tensor(out=operands[:, t0:t0 + QJ, 3 * V:4 * V],
                                               in0=operands[:, t0:t0 + QJ, 2 * V:3 * V], scalar=-LOW,
                                               in1=wY[:, c % RW, :, :], op0=ALU.mult,
                                               op1=ALU.add).then_inc(loY_ready, 1)

            def mask_quad(b, par, half, q, e=None, last=False):
                r = q % 2
                count = NQ * b + q
                if q + 1 < NQ:
                    compare(b, par, half, q + 1)
                elif not last:
                    compare(b + 1, 1 - par, half + par, 0)
                if e is not None:
                    epilogue_step(e, q, 0)
                dve.wait_ge(adjT_ready, count + 1)
                if isinstance(b, int):
                    adj8 = adjT[:, b, QJ * q:QJ * q + QJ, :]
                else:
                    adj8 = adjT[:, ds(b, 1), QJ * q:QJ * q + QJ, :].squeeze(1)
                if not isinstance(count, int) or count >= 2:
                    dve.wait_ge(masks_used, count - 1)
                dve.wait_ge(signs_ready, count + 1)
                if isinstance(b, int) and b == 0:
                    dve.wait_ge(compared, DJ0 * (count + 1))
                else:
                    dve.wait_ge(compared, DJ * (count + 1) + NQ * (DJ0 - DJ))
                nc.vector.tensor_tensor(maskB[:, r, :, :].bitcast(u32),
                                        keep[:, r, :, :].bitcast(u32), adj8.bitcast(u32),
                                        ALU.bitwise_and).then_inc(maskB_ready, 1)
                if e is not None:
                    epilogue_step(e, q, 1)
                dve.wait_ge(maskB_ready, count + 1)
                nc.vector.tensor_tensor(maskC[:, r, :, :].bitcast(u32),
                                        maskB[:, r, :, :].bitcast(u32), adj8.bitcast(u32),
                                        ALU.bitwise_xor).then_inc(maskC_ready, 1)
                if e is not None and q == 0:
                    copy_accB(e, 1 - par)
                if e is not None:
                    epilogue_step(e, q, 2)

            def epilogue_step(e, q, u):
                at = EPI * e
                if (q, u) == (1, 0):
                    combine(e, at)
                if (q, u) == (1, 1):
                    scale_B(e, at)
                if (q, u) == (1, 2):
                    add_C(e, at)
                if (q, u) == (2, 0):
                    flag_empty(at)
                if (q, u) == (2, 1):
                    fill_empty(at)
                if (q, u) == (2, 2):
                    recip(at)
                if (q, u) == (3, 0):
                    row_factor(at)
                if (q, u) == (3, 1):
                    split_sign(e, at)
                if (q, u) == (3, 2):
                    add_x(e, at)
                if (q, u) == (5, 0):
                    make_x1(e, at)
                if (q, u) == (5, 1):
                    stats_x1(e, at)
                if (q, u) == (5, 2):
                    aggregate_x1(at)
                if (q, u) == (6, 0):
                    add_eps(at)
                if (q, u) == (7, 0):
                    rows_x1(e)

            def copy_accB(e, par):
                dve.wait_ge(masks_used, NQ * (e + 1))
                nc.vector.tensor_copy(RB[:, 1, :], acc[:, 1, 0:2 * V]).then_inc(accB1_copied, 1)
                nc.vector.tensor_copy(RB[:, 0, :], acc[:, B0_BANKS[par], 0:2 * V]).then_inc(accB0_copied, 1)

            def tile_col(src, e, s):
                return src[:, ds(2 * e + s, 1)]

            def combine(e, at):
                dve.wait_ge(accB1_copied, e + 1)
                dve.wait_ge(accB0_copied, e + 1)
                nc.vector.scalar_tensor_tensor(out=eM, in0=RB[:, :, V:2 * V], scalar=1.0 / LOW, in1=RB[:, :, 0:V],
                                               op0=ALU.mult, op1=ALU.add).then_inc(epilogue_steps, 1)
                dve.wait_ge(accC_copied, e + 1)
                nc.vector.scalar_tensor_tensor(out=eC, in0=RC[:, :, V:2 * V], scalar=1.0 / LOW, in1=RC[:, :, 0:V],
                                               op0=ALU.mult, op1=ALU.add).then_inc(combined, 1)

            def scale_B(e, at):
                dve.wait_ge(epilogue_steps, at + 1)
                for s in range(2):
                    nc.vector.tensor_scalar(eM[:, s, :], eM[:, s, :], tile_col(Urow, e, s), None,
                                            ALU.mult).then_inc(epilogue_steps, 1)

            def add_C(e, at):
                dve.wait_ge(epilogue_steps, at + 3)
                dve.wait_ge(combined, e + 1)
                for s in range(2):
                    nc.vector.scalar_tensor_tensor(out=eM[:, s, :], in0=eC[:, s, :], scalar=tile_col(Vrow, e, s),
                                                   in1=eM[:, s, :], op0=ALU.mult,
                                                   op1=ALU.add).then_inc(epilogue_steps, 1)

            def flag_empty(at):
                dve.wait_ge(epilogue_steps, at + 5)
                nc.vector.tensor_scalar(eflag[:], eM[:, :, F], TINY, None, ALU.is_le).then_inc(epilogue_steps, 1)

            def fill_empty(at):
                dve.wait_ge(epilogue_steps, at + 6)
                if isinstance(at, int) and at == 0:
                    dve.wait_ge(sumwh_ready, 1)
                for s in range(2):
                    nc.vector.scalar_tensor_tensor(out=eM[:, s, :], in0=sumWh[:], scalar=eflag[:, s:s + 1],
                                                   in1=eM[:, s, :], op0=ALU.mult,
                                                   op1=ALU.add).then_inc(epilogue_steps, 1)

            def recip(at):
                dve.wait_ge(epilogue_steps, at + 8)
                nc.vector.reciprocal(erec[:], eM[:, :, F]).then_inc(epilogue_steps, 1)

            def row_factor(at):
                dve.wait_ge(epilogue_steps, at + 9)
                nc.vector.tensor_scalar(escale[:], erec[:], BND, None, ALU.mult).then_inc(epilogue_steps, 1)

            def split_sign(n, at):
                dve.wait_ge(epilogue_steps, at + 10)
                if not isinstance(n, int) or n > 0:
                    dve.wait_ge(xnT_done, n)
                for s in range(2):
                    nc.vector.tensor_scalar(emin[:, s, :], eM[:, s, 0:F], escale[:, s:s + 1], 0.0, ALU.mult,
                                            ALU.min).then_inc(emin_ready, 1)
                for s in range(2):
                    nc.vector.tensor_scalar(eM[:, s, 0:F], eM[:, s, 0:F], escale[:, s:s + 1], 0.0, ALU.mult,
                                            ALU.max).then_inc(epilogue_steps, 1)

            def add_x(n, at):
                dve.wait_ge(epilogue_steps, at + 12)
                dve.wait_ge(xt_landed, 16 * n + 16)
                nc.vector.scalar_tensor_tensor(out=ey, in0=eM[:, :, 0:F], scalar=-1.0, in1=xt[:],
                                               op0=ALU.add, op1=ALU.add).then_inc(epilogue_steps, 1)

            def make_x1(n, at):
                dve.wait_ge(epilogue_steps, at + 13)
                dve.wait_ge(emin_exp_ready, n + 1)
                if not isinstance(n, int) or n > 0:
                    dve.wait_ge(x1_stored, 16 * n)
                nc.vector.tensor_tensor(x1[:], ey, emin[:], ALU.add).then_inc(x1_ready, 1)

            def stats_x1(n, at):
                dve.wait_ge(x1_ready, n + 1)
                for s in range(2):
                    nc.vector.bn_stats(bn6[:, s, :], x1[:, s, :]).then_inc(epilogue_steps, 1)

            def aggregate_x1(at):
                dve.wait_ge(epilogue_steps, at + 15)
                nc.vector.memset(wait_slot[:], 0.0)
                for s in range(2):
                    nc.vector.bn_aggr(mv[:, s, :], bn6[:, s, :]).then_inc(epilogue_steps, 1)

            def add_eps(at):
                dve.wait_ge(epilogue_steps, at + 17)
                nc.vector.tensor_scalar(veps[:, 0:2], mv[:, 0:2, 1], LN_EPS, None, ALU.add).then_inc(veps_ready, 1)

            def rows_x1(n):
                dve.wait_ge(rstd_ready, n + 5)
                for s in range(2):
                    nc.vector.tensor_scalar(emin[:, s, :], x1[:, s, :], mv[:, s, 0:1], rstd[:, s:s + 1], ALU.subtract,
                                            ALU.mult).then_inc(xn_ready, 1)

            def low_part_G0(e, n):
                dve.wait_ge(ghi_ready, n + 1)
                dve.wait_ge(self_ready, n + 1)
                sg = misc[:].rearrange("p (s k f) -> p s k f", s=2, k=2)
                nc.vector.scalar_tensor_tensor(out=G0[:, ds(2 * e, 2), F:2 * F], in0=G0[:, ds(2 * e, 2), 0:F],
                                               scalar=-LOW, in1=sg[:, :, 1, :], op0=ALU.mult,
                                               op1=ALU.add).then_inc(g_ready, 1)

            def rest_of_epilogue(e, n, at, before=None):
                flag_empty(at)
                fill_empty(at)
                recip(at)
                row_factor(at)
                split_sign(n, at)
                add_x(n, at)
                make_x1(n, at)
                stats_x1(n, at)
                aggregate_x1(at)
                add_eps(at)
                if before is not None:
                    low_part_G0(before, before)
                rows_x1(n)
                low_part_G0(e, n)

            for q in range(NQ):
                mask_quad(0, 0, 0, q)
                low_parts(q)
                if q == 0:
                    dve.wait_ge(wsn_copied, 2)
                    nc.vector.tensor_scalar(wsn0[:, F:2 * F], wsn0[:, F:2 * F], S0, None,
                                            ALU.mult).then_inc(wsn_ready, 1)
                    nc.vector.tensor_scalar(wsn1[:, F:2 * F], wsn1[:, F:2 * F], S1, None,
                                            ALU.mult).then_inc(wsn_ready, 1)

            def dve_block(b, par, half, tail=True, last=False):
                for q in range(NQ):
                    mask_quad(b, par, half, q, b - 1, last)
                    if q == 3 and tail:
                        low_part_G0(b - 2, b - 2)

            dve.wait_ge(exps_ready, 4)
            dve_block(1, 1, 0, tail=False)
            dve_block(2, 0, 1)
            with dve.Fori(1, (NB - 2) // 2, 1) as it:
                dve_block(2 * it + 1, 1, it)
                dve_block(2 * it + 2, 0, it + 1)
            dve_block(NB - 1, 1, NB // 2 - 1, last=True)
            e = NB - 1
            copy_accB(e, 1)
            combine(e, EPI * e)
            scale_B(e, EPI * e)
            add_C(e, EPI * e)
            rest_of_epilogue(e, e, EPI * e, before=e - 1)

            with dve.If(nc.vector.value_load(wide[0:1, 0:1], min_val=0, max_val=1)):
                nc.vector.tensor_scalar(wcols[:, 0, :], nsk[:], -1.0, None, ALU.mult).then_inc(wcols_ready, 1)
                nc.vector.tensor_scalar(wcols[:, 1, :], nsk[:], -SLOPE, None, ALU.mult).then_inc(wcols_ready, 1)
                dve.wait_ge(wrow_done, 1)
                nc.vector.tensor_scalar(wrow, misc[0:NT, 0:P], red[0:NT, 1:2], 1.0, ALU.add, ALU.add).then_inc(
                    wrow_ready, 1)
                dve.wait_ge(wh_reloaded, 16)
                with dve.Fori(0, NB, 1) as e:
                    for s in range(2):
                        k = 2 * e + s
                        for c in range(CH):
                            m = CH * k + c
                            dve.wait_ge(wadj_landed, 32 * m + 32)
                            nc.vector.scalar_tensor_tensor(out=wsk, in0=wadj, scalar=BIG, in1=wsk, op0=ALU.mult,
                                                           op1=ALU.min).then_inc(wcand_ready, 1)
                            dve.wait_ge(wcand_ready, m + 1)
                            nc.vector.reduce_max(wmax[:, c:c + 1], wsk, AX.X).then_inc(wmax_ready, 1)
                        dve.wait_ge(wmax_ready, CH * k + CH)
                        nc.vector.reduce_max(wm[:, 0:1], wmax[:, 0:CH], AX.X).then_inc(wstep, 1)
                        dve.wait_ge(wstep, 6 * k + 1)
                        nc.vector.tensor_scalar(wm[:, 1:2], wm[:, 0:1], red[:, 1:2], 1.0, ALU.subtract,
                                                ALU.subtract).then_inc(wstep, 1)
                        dve.wait_ge(wstep, 6 * k + 2)
                        sq = wwh[:, ds(k, 1), F + 2]
                        nc.vector.tensor_tensor(wm[:, 2:3], wm[:, 1:2], sq, ALU.add).then_inc(wstep, 1)
                        dve.wait_ge(wstep, 6 * k + 3)
                        nc.vector.scalar_tensor_tensor(out=wm[:, 3:4], in0=wm[:, 2:3], scalar=SLOPE, in1=wm[:, 2:3],
                                                       op0=ALU.mult, op1=ALU.max).then_inc(wstep, 1)
                        dve.wait_ge(wstep, 6 * k + 4)
                        nc.vector.tensor_tensor(wab[:, 0:1], sq, wm[:, 3:4], ALU.subtract).then_inc(wstep, 1)
                        nc.vector.scalar_tensor_tensor(out=wab[:, 1:2], in0=sq, scalar=SLOPE, in1=wm[:, 3:4],
                                                       op0=ALU.mult, op1=ALU.subtract).then_inc(wstep, 1)
                        dve.wait_ge(wcols_ready, 2)
                        dve.wait_ge(abT_ready, k + 1)
                        for jt in range(NT):
                            m = NT * k + jt
                            if jt >= 2:
                                dve.wait_ge(probs_ready, m - 1)
                            nc.vector.tensor_scalar(exps[:, jt % 2, 0, :], abT[:, 0, :], wcols[:, 0, jt:jt + 1], None,
                                                    ALU.add).then_inc(wsum_steps, 1)
                            dve.wait_ge(wsum_steps, 3 * m + 1)
                            nc.vector.scalar_tensor_tensor(out=exps[:, jt % 2, 1, :], in0=abT[:, 1, :],
                                                           scalar=wcols[:, 1, jt:jt + 1], in1=exps[:, jt % 2, 0, :],
                                                           op0=ALU.add, op1=ALU.max).then_inc(wsum_steps, 1)
                            dve.wait_ge(wsum_steps, 3 * m + 2)
                            nc.vector.tensor_scalar(exps[:, jt % 2, 1, :], exps[:, jt % 2, 1, :], 1.0, None,
                                                    ALU.min).then_inc(wsum_steps, 1)
                            dve.wait_ge(wexps_ready, m + 1)
                            if jt >= 2:
                                dve.wait_ge(probs_used, m - 1)
                            nc.vector.scalar_tensor_tensor(
                                out=probs[:, jt % 2, :],
                                in0=adjT[:, ds(e, 1), jt, s * P:(s + 1) * P].squeeze(1).bitcast(u8), scalar=BIG,
                                in1=exps[:, jt % 2, 0, :], op0=ALU.mult, op1=ALU.min).then_inc(probs_ready, 1)
                        dve.wait_ge(probs_used, NT * k + NT)
                        nc.vector.tensor_copy(eM[:, s, :], acc[:, 0, 0:V]).then_inc(wrows_ready, 1)
                    dve.wait_ge(wrows_ready, 2 * e + 2)
                    rest_of_epilogue(e, NB + e, EPI * NB + (EPI - 5) * e - 5)

            def layer1_rows(t, k, r):
                dve.wait_ge(l1_done, t + 1)
                dve.wait_ge(ring_landed[k], 16 * r + 16)
                nc.vector.scalar_tensor_tensor(out=lring[:, k, :], in0=acc[:, k, F:2 * F], scalar=K0,
                                               in1=lring[:, k, :], op0=ALU.mult, op1=ALU.add).then_inc(l1_sum, 1)
                dve.wait_ge(l1_sum, t + 1)
                if not isinstance(t, int) or t >= 2:
                    dve.wait_ge(hpT_done, t - 1)
                nc.vector.scalar_tensor_tensor(out=hpre[:, k % 2, :], in0=acc[:, k, 0:F], scalar=I0, in1=lring[:, k, :],
                                               op0=ALU.mult, op1=ALU.add).then_inc(l1_half, 1)

            def layer1_low(t):
                dve.wait_ge(g1hi_ready, t + 1)
                dve.wait_ge(self1_ready, t + 1)
                nc.vector.scalar_tensor_tensor(out=G1[:, ds(t, 1), F:2 * F].squeeze(1),
                                               in0=G1[:, ds(t, 1), 0:F].squeeze(1), scalar=-LOW, in1=tp[:, 0, F:2 * F],
                                               op0=ALU.mult,
                                               op1=ALU.add).then_inc(g1_ready, 1)

            for k in range(RT):
                layer1_rows(k, k, 0)
                if k >= 1:
                    layer1_low(k - 1)
            with dve.Fori(1, NT // RT, 1) as r:
                for k in range(RT):
                    layer1_rows(RT * r + k, k, r)
                    layer1_low(RT * r + k - 1)
            layer1_low(NT - 1)

            def layer2_rows(t, k, r):
                dve.wait_ge(l2_done, t + 1)
                dve.wait_ge(self1_ready, t + 1)
                nc.vector.scalar_tensor_tensor(out=hpre[:, k % 2, :], in0=acc[:, k, F:2 * F], scalar=K1,
                                               in1=self1[:, ds(t, 1), :].squeeze(1), op0=ALU.mult,
                                               op1=ALU.add).then_inc(l2_half, 1)
                dve.wait_ge(l2_half, t + 1)
                nc.vector.scalar_tensor_tensor(out=hpre[:, k % 2, :], in0=acc[:, k, 0:F], scalar=I1,
                                               in1=hpre[:, k % 2, :], op0=ALU.mult, op1=ALU.add).then_inc(l2_sum, 1)
                dve.wait_ge(l2_sum, t + 1)
                dve.wait_ge(ring_landed[k], 16 * r + 16 * (NT // RT) + 16)
                if not isinstance(r, int):
                    dve.wait_ge(out_stored[k], 16 * r)
                nc.vector.scalar_tensor_tensor(out=oring[:, k, :], in0=hpre[:, k % 2, :], scalar=0.0,
                                               in1=lring[:, k, :], op0=ALU.max, op1=ALU.add).then_inc(out_ready, 1)

            for k in range(RT):
                layer2_rows(k, k, 0)
            with dve.Fori(1, NT // RT, 1) as r:
                for k in range(RT):
                    layer2_rows(RT * r + k, k, r)

        @block.tensor
        def _(pe):
            pe.wait_ge(pool_const, 5)
            pe.wait_ge(W_landed, 32)
            nc.tensor.transpose(tp[:, 1, 0:F], wnat[:, 0, :], ident[:]).then_inc(weightsT, 1)
            pe.wait_ge(wt_copied, 1)
            nc.tensor.matmul(tp[:, 1, F:F + 2], WT[:], acols[:], start=True, stop=True).then_inc(wa_done, 1)
            pe.wait_ge(const_ready, 1)

            def transpose_adj(b, q):
                n = NQ * b + q
                if n >= 2:
                    pe.wait_ge(adjT_ready, n - 1)
                if q % CQ == 0:
                    pe.wait_ge(adj_landed[q // CQ], 16 * b + 16)
                for u in range(QJ):
                    for s in range(2):
                        jt = QJ * q + u
                        c, at = jt * P // CW, jt * P % CW
                        last = nc.tensor.matmul(tp[:, q % 2, (2 * u + s) * HP:(2 * u + s + 1) * HP],
                                                stage[:, c, s, at:at + P], pairs[:], start=True, stop=True)
                last.then_inc(adj_transposed, 1)

            def product_Wh(g):
                pe.wait_ge(rhs0_ready, 3)
                pe.wait_ge(hT_ready, g + 1)
                if g >= 2:
                    pe.wait_ge(wh_copied, g - 1)
                for k in range(GT):
                    last = nc.tensor.matmul(acc[:, 2 * (g % 2) + k // 2, (k % 2) * 256:(k % 2) * 256 + WHC],
                                            hT_ring[g % 2][:, k * P:(k + 1) * P], rhs0[:], start=True, stop=True)
                last.then_inc(wh_done, 1)

            for g in range(NG):
                pe.wait_ge(ln_done, g + 1)
                if g >= 1:
                    pe.wait_ge(hT_ready, g)
                for k in range(GT):
                    last = nc.tensor.transpose(misc[:, k * P:(k + 1) * P], xin[:, GT * g + k, :], ident[:])
                last.then_inc(xT_done, 1)
                if g >= 1:
                    product_Wh(g - 1)
                    transpose_adj(0, g - 1)
                if g == 0:
                    pe.wait_ge(weights_landed, 64)
                    for k in range(4):
                        last = nc.tensor.transpose(acc[:, 4, k * F:(k + 1) * F], wnat[:, 1 + k, :], ident[:])
                    last.then_inc(wsnT_done, 1)
                if g == 4:
                    pe.wait_ge(wsn_copied, 2)
                    pe.wait_ge(wh_scaled_pool, 1)
                    for k in range(4):
                        last = nc.tensor.matmul(acc[:, 4, k * P:(k + 1) * P],
                                                wh[:, k, F + 2:F + 3].broadcast_to([P, P]),
                                                ident[:], start=True, stop=True)
                    last.then_inc(first_sq_done, 1)
            product_Wh(NG - 1)
            transpose_adj(0, NG - 1)
            pe.wait_ge(wh_scaled_pool, POOL_G)
            pe.wait_ge(wh_scaled_dve, NG - POOL_G)
            nc.tensor.matmul(misc[0:NT, 0:P], wh[:, :, F + 2], ident[:], start=True, stop=True).then_inc(sqT_done, 1)

            def sum_Wh(tiles):
                for t in tiles:
                    last = nc.tensor.matmul(misc[:, P:P + V], ones, wh[:, t, 0:V], start=(t == 0), stop=(t == NT - 1))
                if NT - 1 in tiles:
                    last.then_inc(sumwh_done, 1)

            pe.wait_ge(bound_col, 1)
            pe.wait_ge(sqrow_ready, 1)
            SUM_FIRST = 20
            sum_Wh(range(5))
            transpose_adj(1, 0)
            sum_Wh(range(5, SUM_FIRST))

            def masked_products(b, q):
                for k, mask in enumerate((maskB, maskC)):
                    if k == 0:
                        pe.wait_ge(maskB_ready, NQ * b + q + 1)
                    else:
                        pe.wait_ge(maskC_ready, NQ * b + q + 1)
                    if b == 0:
                        pe.wait_ge((loX_ready, loY_ready)[k], q + 1)
                    for s in range(2):
                        bank = B0_BANKS[b % 2] if 2 * k + s == 0 else 2 * k + s
                        if q == 0 and b >= 1 and k == 1:
                            pe.wait_ge(accC_copied, b)
                        if q == 0 and b >= 1 and k == 0 and s == 1:
                            pe.wait_ge(accB1_copied, b)
                        if q == 0 and b >= 2 and k == 0 and s == 0:
                            pe.wait_ge(accB0_copied, b - 1)
                        for u in range(QJ):
                            jt = QJ * q + u
                            last = nc.tensor.matmul(acc[:, bank, 0:2 * V], mask[:, q % 2, u, s * P:(s + 1) * P],
                                                    operands[:, jt, 2 * k * V:2 * (k + 1) * V], start=(jt == 0),
                                                    stop=(jt == NT - 1))
                last.then_inc(masks_used, 1)

            def transpose_xn(n):
                pe.wait_ge(xn_ready, 2 * n + 2)
                if not isinstance(n, int) or n >= 1:
                    pe.wait_ge(g_ready, n)
                    pe.wait_ge(self_ready, n)
                for s in range(2):
                    last = nc.tensor.transpose(misc[:, s * P:(s + 1) * P], emin[:, s, :], ident[:])
                last.then_inc(xnT_done, 1)

            def self_and_G0(n):
                pe.wait_ge(xnT_ready, n + 1)
                pe.wait_ge(wsn_ready, 2)
                for s in range(2):
                    last = nc.tensor.matmul(misc[:, s * IB:(s + 1) * IB], hT[:, s * P:(s + 1) * P], wsn0[:], start=True,
                                            stop=True)
                last.then_inc(self_G0_done, 1)

            for b in range(NB):
                for q in range(NQ):
                    ahead = NQ * (b + 1) + q + 1
                    if ahead < NQ * NB:
                        transpose_adj(ahead // NQ, ahead % NQ)
                    masked_products(b, q)
                    if b == 0 and SUM_FIRST + 2 * q < NT:
                        sum_Wh(range(SUM_FIRST + 2 * q, SUM_FIRST + 2 * q + 2))
                    if b == 1 and q == NQ - 1:
                        pe.wait_ge(sumwh_ready, 1)
                    if b >= 1 and q == NQ - 1:
                        transpose_xn(b - 1)
                    if b >= 2 and q == 1:
                        self_and_G0(b - 2)

            def neighbour_sum(t, jt, G):
                b, s = t // 2, t % 2
                return nc.tensor.matmul(acc[:, t % RT, 0:2 * F], adjT[:, b, jt, s * P:(s + 1) * P], G[:, jt, :],
                                        start=(jt == 0), stop=(jt == NT - 1))

            EARLY = NT - 4
            XN_AT = 2 * NT + 20
            pe.wait_ge(g_ready, NB - 2)
            for t in range(RT):
                if t == 0:
                    pe.wait_ge(accB0_copied, NB - 1)
                elif t == 1:
                    pe.wait_ge(accB1_copied, NB)
                else:
                    pe.wait_ge(accC_copied, NB)
                for jt in range(EARLY):
                    neighbour_sum(t, jt, G0)
                    if (t, jt) == (0, 8):
                        self_and_G0(NB - 2)
                    if (t, jt) == (XN_AT // NT, XN_AT % NT):
                        transpose_xn(NB - 1)
                    if (t, jt) == (3, 8):
                        self_and_G0(NB - 1)

            pe.wait_ge(wide_ready, 1)
            with pe.If(nc.tensor.value_load(wide[0:1, 0:1], min_val=0, max_val=1)):
                pe.wait_ge(g_ready, NB)
                pe.wait_ge(self_ready, NB)
                for t in range(RT):
                    neighbour_sum(t, NT - 1, G0)
                pe.wait_ge(wcols_ready, 1)
                nc.tensor.matmul(misc[0:NT, 0:P], wcols[:, 0, :], ident[:], start=True,
                                 stop=True).then_inc(wrow_done, 1)
                pe.wait_ge(wrow_ready, 1)
                pe.wait_ge(wh_reloaded, 16)
                with pe.Fori(0, NB, 1) as e:
                    for s in range(2):
                        k = 2 * e + s
                        pe.wait_ge(wstep, 6 * k + 6)
                        for h in range(2):
                            last = nc.tensor.matmul(misc[:, h * P:(h + 1) * P], wab[:, h:h + 1].broadcast_to([P, P]),
                                                    ident[:], start=True, stop=True)
                        last.then_inc(ab_done, 1)
                        for jt in range(NT):
                            pe.wait_ge(probs_ready, NT * k + jt + 1)
                            nc.tensor.matmul(acc[:, 0, 0:V], probs[:, jt % 2, :], wwh[:, jt, 0:V], start=(jt == 0),
                                             stop=(jt == NT - 1)).then_inc(probs_used, 1)
                        pe.wait_ge(wrows_ready, k + 1)
                    transpose_xn(NB + e)
                    self_and_G0(NB + e)
                    pe.wait_ge(g_ready, NB + e + 1)
                    pe.wait_ge(self_ready, NB + e + 1)
                for t in range(RT):
                    for jt in range(EARLY):
                        neighbour_sum(t, jt, G0)

            def transpose_h1(t):
                pe.wait_ge(l1_half, t + 1)
                if t >= 1:
                    pe.wait_ge(h1T_ready, t)
                nc.tensor.transpose(misc[:, 0:P], hpre[:, t % 2, :], ident[:]).then_inc(hpT_done, 1)

            def self_and_G1(t):
                pe.wait_ge(h1T_ready, t + 1)
                if t >= 1:
                    pe.wait_ge(g1_ready, t)
                    pe.wait_ge(self1_ready, t)
                nc.tensor.matmul(tp[:, 0, 0:2 * F], hT[:, (t % 2) * P:(t % 2) * P + P], wsn1[:], start=True,
                                 stop=True).then_inc(self_G1_done, 1)

            catch_up = {RT: {4: 0, 18: 1}, RT + 1: {4: 2, 18: 3}, RT + 2: {4: 4, 18: 5}}
            for t in range(NT):
                if t >= RT:
                    pe.wait_ge(l1_half, t - RT + 1)
                ready = catch_up.get(t, {12: t - 1} if t >= RT else {})
                for jt in range(EARLY if t < RT else 0, NT):
                    if t == 0:
                        pe.wait_ge(g_ready, jt // 2 + 1)
                    last = neighbour_sum(t, jt, G0)
                    if jt in ready:
                        transpose_h1(ready[jt])
                    if jt - 9 in ready:
                        self_and_G1(ready[jt - 9])
                last.then_inc(l1_done, 1)
            for t in range(3):
                pe.wait_ge(l1_half, NT - RT + t + 1)
                for jt in range(EARLY):
                    if t == 0:
                        pe.wait_ge(g1_ready, jt + 1)
                    neighbour_sum(t, jt, G1)
                if t == 0:
                    transpose_h1(NT - 1)
                if t == 1:
                    self_and_G1(NT - 1)
            for t in range(NT):
                if 3 <= t < RT:
                    pe.wait_ge(l1_half, NT - RT + t + 1)
                elif t >= RT:
                    pe.wait_ge(l2_sum, t - RT + 1)
                for jt in range(EARLY if t < 3 else 0, NT):
                    if t == 0:
                        pe.wait_ge(g1_ready, jt + 1)
                    last = neighbour_sum(t, jt, G1)
                last.then_inc(l2_done, 1)


_INS = ['x', 'adj', 'L0_gnn_W', 'L0_gnn_a', 'L1_gnn_w_self_0', 'L1_gnn_w_neigh_0', 'L1_gnn_w_self_1',
        'L1_gnn_w_neigh_1']
_OUTS = [((4096, 128), 'float32')]


def kernel(**inputs):
    import numpy as _np
    import concourse.bacc as _bacc
    from concourse import mybir as _mybir
    from concourse.bass_utils import run_bass_kernel_spmd as _run

    nc = _bacc.Bacc("TRN2", target_bir_lowering=False, num_devices=1)
    arrays, args = {}, []
    for name in _INS:
        a = _np.ascontiguousarray(inputs[name])
        arrays[f"in_{name}_dram"] = a
        args.append(nc.dram_tensor(f"in_{name}_dram", a.shape, _mybir.dt.from_np(a.dtype), kind="ExternalInput").ap())
    for i, (shape, dtype) in enumerate(_OUTS):
        dt = _mybir.dt.from_np(_np.dtype(dtype))
        args.append(nc.dram_tensor(f"out_{i}_dram", shape, dt, kind="ExternalOutput").ap())
    gat_sage_kernel(nc, *args)
    r = _run(nc, [arrays], core_ids=[0])
    got = tuple(r.results[0][f"out_{i}_dram"] for i in range(len(_OUTS)))
    return got[0]
```
